# Optimizing a Trainium2 kernel written in Bass

```python
import numpy as np
import jax
import jax.numpy as jnp

def _softmax(x, axis=-1):
    return jax.nn.softmax(x, axis=axis)

def _gelu(x):
    return jax.nn.gelu(x, approximate=True)

def _silu(x):
    return jax.nn.silu(x)

def _sigmoid(x):
    return jax.nn.sigmoid(x)

def _layernorm(x, axis=-1, eps=1e-05):
    m = jnp.mean(x, axis=axis, keepdims=True)
    v = jnp.var(x, axis=axis, keepdims=True)
    return (x - m) / jnp.sqrt(v + eps)

def _scatter_add(tgt, idx, src, axis=0):
    return tgt.at[idx].add(src)

def _segment_sum(src, seg, n):
    return jax.ops.segment_sum(src, seg, n)
kernel_name = 'mk_seq_postln_d1_jaxref_r4_e8e2b7'

def setup_inputs(seed: int=0):
    np.random.seed(seed)
    _w = jnp.asarray

    def _L0_attn_setup():
        import jax, jax.numpy as jnp
        import numpy as np
        EMB = 256
        HEADS = 16
        HEADSIZE = EMB // HEADS
        EPS = 1e-05

        def _layernorm(x, g, b):
            m = jnp.mean(x, axis=-1, keepdims=True)
            v = jnp.mean((x - m) ** 2, axis=-1, keepdims=True)
            return (x - m) * jax.lax.rsqrt(v + EPS) * g + b
        key = jax.random.key(seed)
        ks = jax.random.split(key, 6)
        B, T = (4, 512)
        s = 1.0 / np.sqrt(EMB)
        return {'x': jax.random.normal(ks[0], (B, T, EMB), dtype=jnp.float32), 'Wk': jax.random.normal(ks[1], (EMB, EMB), dtype=jnp.float32) * s, 'Wq': jax.random.normal(ks[2], (EMB, EMB), dtype=jnp.float32) * s, 'Wv': jax.random.normal(ks[3], (EMB, EMB), dtype=jnp.float32) * s, 'Wo': jax.random.normal(ks[4], (EMB, EMB), dtype=jnp.float32) * s, 'bo': jnp.zeros((EMB,), dtype=jnp.float32), 'kln_g': jnp.ones((HEADSIZE,), dtype=jnp.float32), 'kln_b': jnp.zeros((HEADSIZE,), dtype=jnp.float32), 'qln_g': jnp.ones((HEADSIZE,), dtype=jnp.float32), 'qln_b': jnp.zeros((HEADSIZE,), dtype=jnp.float32)}
    _L0_attn_in = _L0_attn_setup()

    def _L0_ffn_setup():
        import jax, jax.numpy as jnp
        import numpy as np
        B, T, D, E, FF, K = (4, 256, 256, 8, 512, 2)
        SINKHORN_ITERS = 3

        def _sinkhorn(log_alpha, iters=SINKHORN_ITERS):
            for _ in range(iters):
                log_alpha = log_alpha - jax.nn.logsumexp(log_alpha, axis=-1, keepdims=True)
                log_alpha = log_alpha - jax.nn.logsumexp(log_alpha, axis=-2, keepdims=True)
            gates = jnp.exp(log_alpha)
            return gates / (jnp.sum(gates, axis=-1, keepdims=True) + 1e-08)
        key = jax.random.key(seed)
        ks = jax.random.split(key, 7)
        scale = 0.02
        return {'x': jax.random.normal(ks[0], (B, T, D), dtype=jnp.float32), 'router_w': jax.random.normal(ks[1], (E, D), dtype=jnp.float32) * scale, 'router_b': jnp.zeros((E,), dtype=jnp.float32), 'temperature': jnp.ones((1,), dtype=jnp.float32) * 0.5, 'wg': jax.random.normal(ks[2], (E, D, FF), dtype=jnp.float32) * scale, 'wp': jax.random.normal(ks[3], (E, D, FF), dtype=jnp.float32) * scale, 'wo': jax.random.normal(ks[4], (E, FF, D), dtype=jnp.float32) * scale}
    _L0_ffn_in = _L0_ffn_setup()
    _d = {'L0_attn_x': _L0_attn_in['x'], 'L0_attn_Wk': _L0_attn_in['Wk'], 'L0_attn_Wq': _L0_attn_in['Wq'], 'L0_attn_Wv': _L0_attn_in['Wv'], 'L0_attn_Wo': _L0_attn_in['Wo'], 'L0_attn_bo': _L0_attn_in['bo'], 'L0_attn_kln_g': _L0_attn_in['kln_g'], 'L0_attn_kln_b': _L0_attn_in['kln_b'], 'L0_attn_qln_g': _L0_attn_in['qln_g'], 'L0_attn_qln_b': _L0_attn_in['qln_b'], 'L0_ffn_router_w': _L0_ffn_in['router_w'], 'L0_ffn_router_b': _L0_ffn_in['router_b'], 'L0_ffn_temperature': _L0_ffn_in['temperature'], 'L0_ffn_wg': _L0_ffn_in['wg'], 'L0_ffn_wp': _L0_ffn_in['wp'], 'L0_ffn_wo': _L0_ffn_in['wo']}
    _x0 = _d['L0_attn_x']
    _d['L0_attn_x'] = jax.random.normal(jax.random.fold_in(jax.random.key(seed), 1), (8, 512, 256), dtype=_x0.dtype)
    del _x0
    return _d

def reference(L0_attn_x, L0_attn_Wk, L0_attn_Wq, L0_attn_Wv, L0_attn_Wo, L0_attn_bo, L0_attn_kln_g, L0_attn_kln_b, L0_attn_qln_g, L0_attn_qln_b, L0_ffn_router_w, L0_ffn_router_b, L0_ffn_temperature, L0_ffn_wg, L0_ffn_wp, L0_ffn_wo):

    def _L0_attn_ref(x, Wk, Wq, Wv, Wo, bo, kln_g, kln_b, qln_g, qln_b):
        import jax, jax.numpy as jnp
        import numpy as np
        EMB = 256
        HEADS = 16
        HEADSIZE = EMB // HEADS
        EPS = 1e-05

        def _layernorm(x, g, b):
            m = jnp.mean(x, axis=-1, keepdims=True)
            v = jnp.mean((x - m) ** 2, axis=-1, keepdims=True)
            return (x - m) * jax.lax.rsqrt(v + EPS) * g + b
        B, T, E = x.shape
        k = jnp.einsum('bte,fe->btf', x, Wk).reshape(B, T, HEADS, HEADSIZE)
        q = jnp.einsum('bte,fe->btf', x, Wq).reshape(B, T, HEADS, HEADSIZE)
        v = jnp.einsum('bte,fe->btf', x, Wv).reshape(B, T, HEADS, HEADSIZE)
        k = _layernorm(k, kln_g, kln_b)
        q = _layernorm(q, qln_g, qln_b)
        scale = E ** (-0.25)
        q = q * scale
        k = k * scale
        dot = jnp.einsum('bihd,bjhd->bhij', q, k)
        causal = jnp.triu(jnp.ones((T, T), dtype=bool), k=1)
        dot = jnp.where(causal, -jnp.inf, dot)
        att = jax.nn.softmax(dot, axis=-1)
        out = jnp.einsum('bhij,bjhd->bihd', att, v).reshape(B, T, E)
        return jnp.einsum('bte,fe->btf', out, Wo) + bo

    def _L0_ffn_ref(x, router_w, router_b, temperature, wg, wp, wo):
        import jax, jax.numpy as jnp
        import numpy as np
        B, T, D, E, FF, K = (4, 256, 256, 8, 512, 2)
        SINKHORN_ITERS = 3

        def _sinkhorn(log_alpha, iters=SINKHORN_ITERS):
            for _ in range(iters):
                log_alpha = log_alpha - jax.nn.logsumexp(log_alpha, axis=-1, keepdims=True)
                log_alpha = log_alpha - jax.nn.logsumexp(log_alpha, axis=-2, keepdims=True)
            gates = jnp.exp(log_alpha)
            return gates / (jnp.sum(gates, axis=-1, keepdims=True) + 1e-08)
        temp = jnp.maximum(temperature, 0.1)
        scores = (jnp.einsum('btd,ed->bte', x, router_w) + router_b) / temp
        gates = _sinkhorn(scores)
        topk_vals, topk_idx = jax.lax.top_k(gates, K)
        topk_gates = topk_vals / (jnp.sum(topk_vals, axis=-1, keepdims=True) + 1e-08)
        g = jax.nn.relu(jnp.einsum('btd,edf->btef', x, wg))
        p = jnp.einsum('btd,edf->btef', x, wp)
        all_out = jnp.einsum('btef,efd->bted', g * p, wo)
        gathered = jnp.take_along_axis(all_out, topk_idx[..., None], axis=2)
        expert_out = jnp.sum(gathered * topk_gates[..., None], axis=2)
        return x + expert_out
    x = L0_attn_x
    x = _layernorm(x + _L0_attn_ref(x, L0_attn_Wk, L0_attn_Wq, L0_attn_Wv, L0_attn_Wo, L0_attn_bo, L0_attn_kln_g, L0_attn_kln_b, L0_attn_qln_g, L0_attn_qln_b), axis=-1)
    x = _layernorm(x + _L0_ffn_ref(x, L0_ffn_router_w, L0_ffn_router_b, L0_ffn_temperature, L0_ffn_wg, L0_ffn_wp, L0_ffn_wo), axis=-1)
    return x

_drawn_inputs = setup_inputs


def setup_inputs(seed=0):
    import zlib

    import numpy as np

    out = dict(_drawn_inputs(seed))
    spreads = {'L0_attn_bo': (0.0, 0.1),
     'L0_attn_kln_g': (1.0, 0.6),
     'L0_attn_kln_b': (0.0, 0.8),
     'L0_attn_qln_g': (1.0, 0.6),
     'L0_attn_qln_b': (0.0, 0.8),
     'L0_ffn_router_b': (0.0, 0.8)}
    factors = {'L0_ffn_router_w': 5.449, 'L0_ffn_wg': 5.779, 'L0_ffn_wp': 4.774, 'L0_ffn_wo': 4.775}
    for name, (base, spread) in spreads.items():
        noise = np.random.default_rng([zlib.crc32(name.encode()), seed]).standard_normal(out[name].shape)
        drawn = base * np.exp(spread * noise) if base else spread * noise
        out[name] = jnp.asarray(drawn.astype(out[name].dtype))
    for name, factor in factors.items():
        out[name] = (out[name] * factor).astype(out[name].dtype)
    return out
```

```python
from contextlib import ExitStack

import concourse.bass as bass
from concourse import mybir

P = 128
NB, T, EMB = 8, 512, 256
H, D = 16, 16
E, FF, K = 8, 512, 2
TT = T // P
NT = NB * TT
EC = EMB // P
FC = FF // P
HH = H // 2
PAIRS = HH // 2
SW = 64
EPS = 1e-5
QK_SCALE = EMB ** -0.25
MASKED = -1e30
SLOT_TILES = NB * T * K // P + E
SLOTS = SLOT_TILES * P
XW = EMB + 1
ITERS = 3

ALU = mybir.AluOpType
ACT = mybir.ActivationFunctionType
AX = mybir.AxisListType.X
F32 = mybir.dt.float32
F32R = mybir.dt.float32r
BF16 = mybir.dt.bfloat16
I32 = mybir.dt.int32
U32 = mybir.dt.uint32

MAXB = 6
STEPS_HALF = TT + 2 * PAIRS + MAXB * PAIRS
STEPS_BATCH = EC + 2 * STEPS_HALF
OUT_HALF = PAIRS + 1
OUT_BATCH = 2 * OUT_HALF + 2 + EC + 1
PIECES = 6 * PAIRS


def at_least(engine, semaphore, value):
    if not isinstance(value, int) or value > 0:
        engine.wait_ge(semaphore, value)


class Chain:

    def __init__(self, engine, semaphore, count):
        self.engine, self.semaphore, self.count = engine, semaphore, count

    def __call__(self, instruction):
        self.count += 1
        instruction.then_inc(self.semaphore, 1)
        self.engine.wait_ge(self.semaphore, self.count)


def layer(nc, x, Wk, Wq, Wv, Wo, bo, kln_g, kln_b, qln_g, qln_b, router_w, router_b,
          temperature, wg, wp, wo, out):
    x_tiles = x.rearrange("b (t p) e -> b p t e", p=P)
    out_tiles = out.rearrange("b (t p) e -> (b t) p e", p=P)
    x1_dram = nc.dram_tensor("x1_dram", [NB, P, TT, EMB], F32, kind="Internal").ap()
    xs_dram = nc.dram_tensor("xs_dram", [SLOTS, XW], F32, kind="Internal").ap()
    ys_dram = nc.dram_tensor("ys_dram", [NB * T * K + SLOTS, EMB], F32, kind="Internal").ap()

    with ExitStack() as ctx:
        def sb(name, shape, dt=F32, where=ctx):
            return where.enter_context(nc.sbuf_tensor(name, shape, dt))

        def bank(name, shape=(P, 512), dt=F32, where=ctx):
            return where.enter_context(nc.psum_tensor(name, list(shape), dt))

        def sem(name):
            return ctx.enter_context(nc.semaphore(name))

        experts = sb("experts", [P, 2, E * EC * FF])
        wg_sb = experts[:, 0, :].rearrange("p (e n) -> p e n", e=E)
        wp_sb = experts[:, 1, :].rearrange("p (e n) -> p e n", e=E)
        flat = experts[:, :, :].rearrange("p a n -> p (a n)")
        w_rows = flat[:, 2 * E * EC * FF - 8 * EMB:].rearrange("p (i c e) -> p i c e", i=4, c=2)
        empty_slots = flat[:, 0:SLOT_TILES // 2 * XW].rearrange("p (t w) -> p t w", w=XW)
        ident = sb("ident", [P, P])
        ident_b = sb("ident_b", [P, P], BF16)
        ones = sb("ones", [P, P])
        ones_b = sb("ones_b", [P, P], BF16)
        before_b = sb("before_b", [P, P], BF16)
        mask_ij = sb("mask_ij", [P, P], BF16)
        mask_ji = sb("mask_ji", [P, P], BF16)
        eps_col = sb("eps_col", [P, 1])
        eps4_col = sb("eps4_col", [P, 1])
        logits = sb("logits", [P, TT, NB, E])
        rb_row = sb("rb_row", [P, E])
        temp_col = sb("temp_col", [P, 1])
        inv_temp = sb("inv_temp", [P, 1])

        att_mem = ExitStack()
        a = lambda name, shape, dt=F32: sb(name, shape, dt, att_mem)
        w_qkvT = a("w_qkvT", [P, EC, 2, 3, P])
        w_oT = a("w_oT", [P, EC, EMB])
        w_mean = a("w_mean", [P, 2, EC, H])
        rw_rows = a("rw_rows", [E, EMB])
        rwT = a("rwT", [P, EC, E])
        gains = a("gains", [P, 2, D])
        shifts = a("shifts", [P, 2, D])
        bo_row = a("bo_row", [P, EMB])
        x_in = a("x_in", [P, TT, EMB])
        xT = a("xT", [P, EC, T])
        x_res = a("x_res", [P, TT, EMB])
        raw = a("raw", [P, TT, 2 * P])
        normed = a("normed", [P, TT, 2 * P])
        squares = normed
        ssum = a("ssum", [P, TT, 2 * HH])
        nt = [a(f"nt{i}", [P, TT, 2 * HH]) for i in range(5)]
        rstd = a("rstd", [P, TT, 2 * HH])
        stack = [a(f"stack{i}", [P, TT, 2, HH, SW], F32R) for i in range(2)]
        kT = [a(f"kT{i}", [P, PAIRS, T], F32R) for i in range(2)]
        qT = [a(f"qT{i}", [P, PAIRS, T], F32R) for i in range(2)]
        v_aug = [a(f"v_aug{i}", [P, TT, HH, D + 1]) for i in range(2)]
        neg_max = a("neg_max", [P, TT, HH])
        probsT = [a(f"probsT{i}", [P, 6, 512]) for i in range(2)]
        recip = a("recip", [P, TT, 4])
        heads = a("heads", [P, TT, P])
        headsT = a("headsT", [P, 2, T])
        y = a("y", [P, TT, EMB])
        y_stats = a("y_stats", [P, TT, 6])
        y_mv = a("y_mv", [P, TT, 2])
        yn = [a(f"yn{i}", [P, TT]) for i in range(5)]
        y_rstd = a("y_rstd", [P, TT])
        x1 = a("x1", [P, TT, EMB])
        x1T = headsT
        att_mem.close()

        ffn_mem = ExitStack()
        f = lambda name, shape, dt=F32: sb(name, shape, dt, ffn_mem)
        x1_all = f("x1_all", [P, NT, XW])
        wo_sb = f("wo_sb", [P, E, FC * EMB])
        row_a = f("row_a", [P, NT])
        row_b = f("row_b", [P, NT])
        exps = f("exps", [P, NT, E])
        col_nmax = f("col_nmax", [NB * E, 1])
        col_exps = f("col_exps", [NB * E, T])
        col_sum = f("col_sum", [NB * E, 1])
        col_ln = f("col_ln", [NB * E, 1])
        col_lse = f("col_lse", [NB * E, 1])
        col_diag = f("col_diag", [NB * E, NB * E])
        gates = f("gates", [P, NT, E])
        best = f("best", [P, NT, 8])
        best_at = f("best_at", [P, NT, 8], U32)
        best_atf = f("best_atf", [P, NT, K])
        expert_iota = f("expert_iota", [P, E])
        chosen = [f(f"chosen{k}", [P, NT, E]) for k in range(K)]
        chosen_b = f("chosen_b", [P, NT, E], BF16)
        counts = f("counts", [P, NT, E])
        scan = [f(f"scan{i}", [P, NT, E]) for i in range(2)]
        n_tiles_i = f("n_tiles_i", [P, E], I32)
        n_tiles_j = f("n_tiles_j", [P, E], I32)
        n_tiles = f("n_tiles", [P, E])
        escan = [f(f"escan{i}", [P, E]) for i in range(2)]
        first_slot = f("first_slot", [P, E])
        slot_all = f("slot_all", [P, NT, E])
        slot_of = [f(f"slot_of{k}", [P, NT, E]) for k in range(K)]
        slot_f = f("slot_f", [P, K, NT])
        slot_u = f("slot_u", [P, K, NT], U32)
        top_sum = f("top_sum", [P, NT])
        top_gate = f("top_gate", [P, NT, K])
        result_row = f("result_row", [P, NT], U32)
        tile_iota = f("tile_iota", [1, SLOT_TILES])
        past = f("past", [1, SLOT_TILES, E])
        tile_ef = f("tile_ef", [1, SLOT_TILES])
        tile_e = f("tile_e", [1, SLOT_TILES], I32)
        xg = [f(f"xg{i}", [P, XW]) for i in range(4)]
        xgT = [f(f"xgT{i}", [P, EC, P]) for i in range(2)]
        gate_act = [f(f"gate_act{i}", [P, FF]) for i in range(2)]
        hid = [f(f"hid{i}", [P, FF]) for i in range(2)]
        hidT = [f(f"hidT{i}", [P, FC, P]) for i in range(2)]
        y_out = [f(f"y_out{i}", [P, EMB]) for i in range(2)]
        y_at = [f(f"y_at{i}", [P, 1], U32) for i in range(2)]
        y_two = [f(f"y_two{i}", [P, K, EMB]) for i in range(4)]
        acc = [f(f"acc{i}", [P, EMB]) for i in range(4)]
        z_stats = f("z_stats", [P, 4, 6])
        z_mv = f("z_mv", [P, 4, 2])
        zn = [f(f"zn{i}", [P, 4]) for i in range(5)]
        z_rstd = f("z_rstd", [P, 4])
        ffn_mem.close()

        psum_a = ExitStack()
        st_bank = [bank(f"st_bank{i}", where=psum_a) for i in range(4)]
        prep_bank = [bank(f"prep_bank{i}", where=psum_a) for i in range(2)]
        out_bank = bank("out_bank", where=psum_a)
        pv_bank = bank("pv_bank", where=psum_a)

        g_bank, p_bank, h_bank, y_bank = st_bank
        x_bank = prep_bank[0]

        consts_ready = sem("consts_ready")
        inputs_loaded = sem("inputs_loaded")
        w_turned = sem("w_turned")
        w_copied = sem("w_copied")
        w_mean_done = sem("w_mean_done")
        w_ready = sem("w_ready")
        slots_imaged = sem("slots_imaged")
        slots_emptied = sem("slots_emptied")
        experts_loaded = sem("experts_loaded")
        x_loaded = sem("x_loaded")
        res_loaded = sem("res_loaded")
        res_ready = sem("res_ready")
        prep_full = sem("prep_full")
        prep_taken = [sem(f"prep_taken{i}") for i in range(2)]
        raw_ready = sem("raw_ready")
        squares_ready = sem("squares_ready")
        ssum_ready = sem("ssum_ready")
        ln_ready = sem("ln_ready")
        seed_ready = sem("seed_ready")
        newton = sem("newton")
        normed_ready = sem("normed_ready")
        gained = sem("gained")
        shifted = sem("shifted")
        high_ready = sem("high_ready")
        low_ready = sem("low_ready")
        again_ready = sem("again_ready")
        max_cleared = sem("max_cleared")
        max_high = sem("max_high")
        max_ready = sem("max_ready")
        out_full = sem("out_full")
        out_taken = sem("out_taken")
        st_full = sem("st_full")
        st_taken = [sem(f"st_taken{i}") for i in range(4)]
        pv_done = sem("pv_done")
        recip_ready = sem("recip_ready")
        heads_ready = sem("heads_ready")
        y_stats_ready = sem("y_stats_ready")
        y_mv_ready = sem("y_mv_ready")
        y_ln_ready = sem("y_ln_ready")
        y_seed_ready = sem("y_seed_ready")
        y_newton = sem("y_newton")
        x1_ready = sem("x1_ready")
        x1_saved = sem("x1_saved")
        route_v = sem("route_v")
        route_a = sem("route_a")
        route_p = sem("route_p")
        rows_max = sem("rows_max")
        wait_passed = sem("wait_passed")
        send_passed = sem("send_passed")
        choice_ready = sem("choice_ready")
        iotas_ready = sem("iotas_ready")
        x1_loaded = sem("x1_loaded")
        scattered = [sem(f"scattered{k}") for k in range(K)]
        rows_named = sem("rows_named")
        slots_ready = sem("slots_ready")
        tiles_ready = sem("tiles_ready")
        xg_loaded = [sem(f"xg_loaded{i}") for i in range(4)]
        xg_turned = sem("xg_turned")
        xgT_ready = sem("xgT_ready")
        g_full = sem("g_full")
        p_full = sem("p_full")
        relu_ready = sem("relu_ready")
        hid_ready = sem("hid_ready")
        hid_turned = sem("hid_turned")
        hidT_ready = sem("hidT_ready")
        yo_full = sem("yo_full")
        yo_ready = sem("yo_ready")
        yo_sent = [sem(f"yo_sent{i}") for i in range(2)]
        yt_loaded = [sem(f"yt_loaded{i}") for i in range(4)]
        comb_a = sem("comb_a")
        comb_b = sem("comb_b")
        comb_stats = sem("comb_stats")
        comb_mv = sem("comb_mv")
        comb_ln = sem("comb_ln")
        comb_seed = sem("comb_seed")
        comb_newton = sem("comb_newton")
        comb_ready = sem("comb_ready")
        stored = [sem(f"stored{i}") for i in range(4)]

        PARAMS = 11

        def batch(b, follow, scores, values, project, turn, maxima, finish_half, finish_batch):
            for half in range(2):
                nb, nh = (b, 1) if half == 0 else (b + 1, 0)
                more = half == 0 or follow
                scores(b, half, 0)
                for p in range(PAIRS):
                    if p + 1 < PAIRS:
                        scores(b, half, p + 1)
                    values(b, half, p)
                    if more and p == 0:
                        project(nb, nh)
                    if more and p == 2:
                        turn(nb, nh)
                        maxima(nb, nh, 0)
                        maxima(nb, nh, 1)
                    if more and p == 3:
                        maxima(nb, nh, 2)
                        maxima(nb, nh, 3)
                finish_half(b, half)
            finish_batch(b)

        def all_batches(engine, *stages):
            project, turn, maxima = stages[2:5]
            project(0, 0)
            turn(0, 0)
            for p in range(PAIRS):
                maxima(0, 0, p)
            batch(0, True, *stages)
            with engine.Fori(1, NB - 1) as b:
                batch(b, True, *stages)
            batch(NB - 1, False, *stages)

        def prep_step(b, half, step):
            i = step if half == 0 else EC + STEPS_HALF + step
            return STEPS_BATCH * b + i, i % 2, STEPS_BATCH // 2 * b + i // 2

        def at_project(b, half, t):
            return prep_step(b, half, (EC if half == 0 else 0) + t)

        def at_turn(b, half, qk, p):
            return prep_step(b, half, (EC if half == 0 else 0) + TT + (1 - qk) * PAIRS + p)

        def at_maxima(b, half, p, i):
            return prep_step(b, half, (EC if half == 0 else 0) + TT + 2 * PAIRS + MAXB * p + i)

        def routed(i, k):
            return 1 + 7 * i + k

        MAX_REGIONS = [[(0, 3, 0)], [(1, 3, 0)], [(0, 2, 0), (0, 0, 384)], [(1, 2, 0), (1, 0, 384)],
                       [(0, 1, 0)], [(1, 1, 0)]]
        ST_REGIONS = [[(0, 0, 0)], [(1, 0, 0)], [(0, 1, 0), (0, 3, 384)], [(1, 1, 0), (1, 3, 384)],
                      [(0, 2, 0)], [(1, 2, 0)]]
        WIDTH = [512, 512, 512, 512, 256, 256]
        PLACE = {(h, j): (i, c) for i, regions in enumerate(ST_REGIONS) for h, j, c in regions}

        def prep_done(engine, step):
            _, k, uses = step
            engine.wait_ge(prep_taken[k], uses + 1)

        block = ctx.enter_context(nc.Block())

        @block.sync
        def _(sp):
            for i, w in enumerate((Wq, Wk, Wv, Wo)):
                sp.dma_start(w_rows[:, i, :, :], w.rearrange("(c p) e -> p c e", p=P)).then_inc(inputs_loaded, 16)
            sp.dma_start(x_in[:, :, :], x_tiles[0]).then_inc(x_loaded, 16)
            sp.dma_start(rw_rows[:, :], router_w).then_inc(inputs_loaded, 16)
            rows = ((gains[:, 0, :], qln_g), (gains[:, 1, :], kln_g), (shifts[:, 0, :], qln_b),
                    (shifts[:, 1, :], kln_b), (bo_row[:, :], bo), (rb_row[:, :], router_b))
            for to, row in rows:
                sp.dma_start(to, row.partition_broadcast(P)).then_inc(inputs_loaded, 16)
            sp.dma_start(temp_col[:, :], temperature.partition_broadcast(P)).then_inc(inputs_loaded, 16)
            sp.dma_start(x_res[:, :, :], x_tiles[0]).then_inc(res_loaded, 16)
            for i in range(2):
                sp.wait_ge(slots_imaged, i + 2)
                sp.dma_start(xs_dram.rearrange("(i t p) w -> i p t w", i=2, p=P)[i], empty_slots).then_inc(
                    slots_emptied, 16)

            def load_x(b):
                sp.wait_ge(prep_full, STEPS_BATCH * (b - 1) + EC)
                sp.dma_start(x_in[:, :, :], x_tiles[bass.ds(b, 1)].rearrange("o p t e -> (o p) t e")).then_inc(
                    x_loaded, 16)

            def batch_io(b, last):
                if not last:
                    sp.wait_ge(out_taken, OUT_BATCH * b + 2 * OUT_HALF + 2)
                    sp.dma_start(x_res[:, :, :], x_tiles[bass.ds(b + 1, 1)].rearrange(
                        "o p t e -> (o p) t e")).then_inc(res_loaded, 16)
                sp.wait_ge(x1_ready, TT * (b + 1))
                sp.dma_start(x1_dram[bass.ds(b, 1)].rearrange("o p t e -> (o p) t e"), x1[:, :, :]).then_inc(
                    x1_saved, 16)

            with sp.Fori(0, NB - 1) as b:
                load_x(b + 1)
                batch_io(b, False)
            batch_io(NB - 1, True)

            sp.wait_ge(slots_emptied, 32)
            for to, w, c in ((wg_sb, wg, EC), (wp_sb, wp, EC), (wo_sb, wo, FC)):
                if w is wo:
                    sp.wait_ge(x1_saved, 16 * NB)
                    sp.wait_ge(out_taken, OUT_BATCH * NB)
                for e in range(E):
                    sp.dma_start(to[:, e, :].rearrange("p (c n) -> p c n", c=c),
                                 w[e].rearrange("(c p) n -> p c n", p=P)).then_inc(experts_loaded, 16)
            for b in range(NB):
                sp.dma_start(x1_all[:, b * TT:(b + 1) * TT, 0:EMB], x1_dram[b]).then_inc(x1_loaded, 16)

            for k in range(K):
                sp.wait_ge(scattered[k], 16 * NT)

            def load_slots(i, k):
                t = 4 * i + k
                sp.dma_start(xg[k][:, :], xs_dram[bass.ds(t * P, P), :]).then_inc(xg_loaded[k], 16)

            for k in range(4):
                load_slots(0, k)
            with sp.Fori(1, SLOT_TILES // 4) as i:
                for k in range(4):
                    sp.wait_ge(yo_ready, 2 * (4 * (i - 1) + k + 1))
                    load_slots(i, k)

            for par in range(2):
                sp.wait_ge(yo_sent[par], 16 * (SLOT_TILES // 2))
            y_rows = ys_dram[0:NB * T * K, :].rearrange("(t p k) e -> t p k e", p=P, k=K)

            def load_two(g, j):
                sp.dma_start(y_two[j][:, :, :], y_rows[bass.ds(4 * g + j, 1)].rearrange(
                    "o p k e -> (o p) k e")).then_inc(yt_loaded[j], 16)

            def store(g, j):
                sp.wait_ge(comb_ready, 4 * g + j + 1)
                sp.dma_start(out_tiles[bass.ds(4 * g + j, 1)].rearrange("o p e -> (o p) e"),
                             acc[j][:, :]).then_inc(stored[j], 16)

            for j in range(4):
                load_two(0, j)
            with sp.Fori(0, NT // 4 - 1) as g:
                for j in range(4):
                    sp.wait_ge(comb_b, 4 * g + j + 1)
                    load_two(g + 1, j)
                for j in range(4):
                    store(g, j)
            for j in range(4):
                store(NT // 4 - 1, j)
            for j in range(4):
                sp.wait_ge(stored[j], 16 * (NT // 4))

        @block.gpsimd
        def _(pool):
            pool.memset(ident[:, :], 0.0).then_inc(consts_ready, 1)
            pool.memset(ones[:, :], 1.0).then_inc(consts_ready, 1)
            pool.memset(ones_b[:, :], 1.0).then_inc(consts_ready, 1)
            pool.memset(mask_ij[:, :], 0.0).then_inc(consts_ready, 1)
            pool.memset(mask_ji[:, :], 0.0).then_inc(consts_ready, 1)
            pool.memset(eps_col[:, :], EPS).then_inc(consts_ready, 1)
            pool.memset(eps4_col[:, :], EPS / 4).then_inc(consts_ready, 1)
            pool.wait_ge(consts_ready, 7)
            pool.affine_select(out=ident[:, :], in_=ident[:, :], compare_op=ALU.not_equal, fill=1.0, base=0,
                               pattern=[[-1, P]], channel_multiplier=1).then_inc(consts_ready, 1)
            pool.affine_select(out=mask_ij[:, :], in_=mask_ij[:, :], compare_op=ALU.is_ge, fill=MASKED, base=0,
                               pattern=[[-1, P]], channel_multiplier=1).then_inc(consts_ready, 1)
            pool.affine_select(out=mask_ji[:, :], in_=mask_ji[:, :], compare_op=ALU.is_ge, fill=MASKED, base=0,
                               pattern=[[1, P]], channel_multiplier=-1).then_inc(consts_ready, 1)
            pool.affine_select(out=before_b[:, :], in_=ones_b[:, :], compare_op=ALU.is_gt, fill=0.0, base=0,
                               pattern=[[1, P]], channel_multiplier=-1).then_inc(consts_ready, 1)
            pool.wait_ge(consts_ready, 8)
            pool.tensor_copy(ident_b[:, :], ident[:, :]).then_inc(consts_ready, 1)
            for i in range(2):
                pool.memset(stack[i][:, :, :, :, 32:48].bitcast(F32), 0.0).then_inc(consts_ready, 1)
                pool.memset(v_aug[i][:, :, :, D:D + 1], 1.0).then_inc(consts_ready, 1)
            pool.wait_ge(consts_ready, 16)
            for i in range(2):
                pool.memset(stack[i][:, :, 1, :, 32:34].bitcast(F32), 1.0).then_inc(consts_ready, 1)

            def project(b, half):
                u = 2 * b + half
                pool.wait_ge(raw_ready, TT * (u + 1))
                at_least(pool, low_ready, 2 * u)
                pool.tensor_tensor(squares[:, :, :], raw[:, :, :], raw[:, :, :], ALU.mult).then_inc(squares_ready, 1)
                pool.memset(stack[half][:, :, 0, :, 32:34].bitcast(F32), 0.0).then_inc(max_cleared, 1)
                pool.wait_ge(normed_ready, u + 1)
                n4 = normed[:, :, :].rearrange("p t (s n) -> p (t s) n", n=D)
                for s in range(2):
                    v = normed[:, :, s * P:(s + 1) * P].rearrange("p t (h d) -> p t h d", d=D)
                    g = gains[:, s:s + 1, :].unsqueeze(2).broadcast_to([P, TT, HH, D])
                    pool.tensor_tensor(v, v, g, ALU.mult).then_inc(gained, 1)
                pool.wait_ge(gained, 2 * (u + 1))
                for s in range(2):
                    v = normed[:, :, s * P:(s + 1) * P].rearrange("p t (h d) -> p t h d", d=D)
                    g = shifts[:, s:s + 1, :].unsqueeze(2).broadcast_to([P, TT, HH, D])
                    pool.tensor_tensor(v, v, g, ALU.add).then_inc(shifted, 1)

            def nothing(*_):
                pass

            def finish_half(b, half):
                if half == 0:
                    pool.wait_ge(res_loaded, 16 * (b + 1))
                    pool.tensor_tensor(x_res[:, :, :], x_res[:, :, :],
                                       bo_row[:, :].unsqueeze(1).broadcast_to([P, TT, EMB]), ALU.add).then_inc(
                        res_ready, 1)

            pool.wait_ge(w_ready, 3)
            pool.memset(empty_slots, 0.0).then_inc(slots_imaged, 1)
            pool.wait_ge(slots_imaged, 1)
            for i in range(2):
                if i > 0:
                    pool.wait_ge(slots_emptied, 16)
                pool.iota(empty_slots[:, :, EMB:EMB + 1].bitcast(I32), [[P, SLOT_TILES // 2], [1, 1]],
                          base=NB * T * K + i * SLOTS // 2, channel_multiplier=1).then_inc(slots_imaged, 1)
            all_batches(pool, nothing, nothing, project, nothing, nothing, finish_half, nothing)

            pool.wait_ge(out_taken, OUT_BATCH * NB)
            pool.wait_ge(x1_saved, 16 * NB)
            pool.iota(expert_iota[:, :], [[1, E]], base=0, channel_multiplier=0,
                      allow_small_or_imprecise_dtypes=True).then_inc(iotas_ready, 1)
            pool.iota(tile_iota[:, :], [[1, SLOT_TILES]], base=0, channel_multiplier=0,
                      allow_small_or_imprecise_dtypes=True).then_inc(iotas_ready, 1)
            pool.iota(result_row[:, :].bitcast(I32), [[K * P, NT]], base=0, channel_multiplier=K).then_inc(
                iotas_ready, 1)
            pool.wait_ge(slots_emptied, 32)
            pool.wait_ge(x1_loaded, 16 * NB)
            for k in range(K):
                pool.wait_ge(rows_named, k + 1)
                if k == 0:
                    pool.wait_ge(slots_ready, 1)
                for t in range(NT):
                    pool.indirect_dma_start(xs_dram, bass.IndirectOffsetOnAxis(slot_u[:, k, t % TT * NB + t // TT:t % TT * NB + t // TT + 1], 0),
                                            x1_all[:, t, :], None).then_inc(scattered[k], 16)

            with pool.Fori(0, SLOT_TILES // 2) as i:
                for par in range(2):
                    pool.wait_ge(yo_ready, 2 * (2 * i + par + 1))
                    pool.sem_inc(send_passed, 1)
                    pool.indirect_dma_start(ys_dram, bass.IndirectOffsetOnAxis(y_at[par][:, 0:1], 0),
                                            y_out[par][:, :], None).then_inc(yo_sent[par], 16)

        @block.scalar
        def _(act):
            act.preload_act_table_set("natural_log_exp_and_others")

            def scores(b, half, p):
                u = 2 * b + half
                act.wait_ge(out_full, OUT_BATCH * b + OUT_HALF * half + p + 1)
                act.copy(qT[half][:, p, :], out_bank[:, :]).then_inc(out_taken, 1)
                for i in range(6):
                    idx = 6 * p + i
                    if i == 0:
                        at_least(act, pv_done, PAIRS * u + p - 1)
                    act.wait_ge(st_full, PIECES * u + idx + 1)
                    act.activation(probsT[p % 2][:, i, 0:WIDTH[i]], st_bank[idx % 4][:, 0:WIDTH[i]], ACT.Exp).then_inc(st_taken[idx % 4], 1)

            def project(b, half):
                u = 2 * b + half
                if half == 0:
                    for c in range(EC):
                        n, k, _ = prep_step(b, 0, c)
                        act.wait_ge(prep_full, n + 1)
                        act.copy(xT[:, c, :], prep_bank[k][:, :]).then_inc(prep_taken[k], 1)
                at_least(act, normed_ready, u)
                for t in range(TT):
                    n, k, _ = at_project(b, half, t)
                    act.wait_ge(prep_full, n + 1)
                    act.copy(raw[:, t, :], prep_bank[k][:, 0:2 * P]).then_inc(raw_ready, 1)
                    act.copy(v_aug[half][:, t, :, 0:D],
                             prep_bank[k][:, 2 * P:3 * P].rearrange("p (h d) -> p h d", d=D)).then_inc(
                        prep_taken[k], 1)
                act.wait_ge(ssum_ready, u + 1)
                act.activation(nt[0][:, :, :], ssum[:, :, :], ACT.Ln, bias=eps_col[:, :],
                               scale=1.0 / D).then_inc(ln_ready, 1)
                act.wait_ge(ln_ready, u + 1)
                act.activation(nt[1][:, :, :], nt[0][:, :, :], ACT.Exp, scale=-0.5).then_inc(seed_ready, 1)

            def turn(b, half):
                u = 2 * b + half
                act.wait_ge(high_ready, u + 1)
                act.copy(stack[half][:, :, 0, :, 48:64], stack[half][:, :, 0, :, 0:D].bitcast(F32)).then_inc(
                    again_ready, 1)
                act.copy(stack[half][:, :, 1, :, 16:32], stack[half][:, :, 1, :, 0:D].bitcast(F32)).then_inc(
                    again_ready, 1)
                for p in range(PAIRS):
                    n, k, _ = at_turn(b, half, 1, p)
                    act.wait_ge(prep_full, n + 1)
                    act.copy(kT[half][:, p, :], prep_bank[k][:, :]).then_inc(prep_taken[k], 1)

            def nothing(*_):
                pass

            def finish_half(b, half):
                act.wait_ge(out_full, OUT_BATCH * b + OUT_HALF * half + PAIRS + 1)
                act.copy(headsT[:, half, :], out_bank[:, :]).then_inc(out_taken, 1)

            def finish_batch(b):
                act.wait_ge(y_mv_ready, TT * (b + 1))
                act.activation(yn[0][:, :], y_mv[:, :, 1], ACT.Ln, bias=eps_col[:, :]).then_inc(y_ln_ready, 1)
                act.wait_ge(y_ln_ready, b + 1)
                act.activation(yn[1][:, :], yn[0][:, :], ACT.Exp, scale=-0.5).then_inc(y_seed_ready, 1)
                for c in range(EC):
                    act.wait_ge(out_full, OUT_BATCH * b + 2 * OUT_HALF + 2 + c + 1)
                    act.copy(x1T[:, c, :], out_bank[:, :]).then_inc(out_taken, 1)

            act.wait_ge(consts_ready, 18)
            all_batches(act, scores, nothing, project, turn, nothing, finish_half, finish_batch)

            for i in range(ITERS):
                act.wait_ge(route_v, routed(i, 1))
                act.activation(exps[:, :, :], logits[:, :, :, :].rearrange("p t b e -> p (t b) e"),
                               ACT.Exp).then_inc(route_a, 1)
                act.wait_ge(route_v, routed(i, 2))
                act.activation(row_b[:, :], row_a[:, :], ACT.Ln).then_inc(route_a, 1)
                act.wait_ge(route_v, routed(i, 4))
                act.activation(col_exps[:, :], st_bank[0][0:NB * E, :], ACT.Exp, bias=col_nmax[:, :],
                               accum_out=col_sum[:, :]).then_inc(route_a, 1)
                act.wait_ge(route_a, 4 * i + 3)
                act.activation(col_ln[:, :], col_sum[:, :], ACT.Ln).then_inc(route_a, 1)
            act.wait_ge(route_v, routed(ITERS, 0))
            act.activation(gates[:, :, :], logits[:, :, :, :].rearrange("p t b e -> p (t b) e"),
                           ACT.Exp).then_inc(route_a, 1)

            def turned(t, par):
                act.wait_ge(xg_turned, t + 1)
                act.copy(xgT[par][:, :, :], x_bank[:, 0:EMB].rearrange("p (c n) -> p c n", c=EC)).then_inc(
                    xgT_ready, 1)

            def gate(t, par):
                act.wait_ge(g_full, t + 1)
                act.activation(gate_act[par][:, :], g_bank[:, :], ACT.Relu).then_inc(relu_ready, 1)

            def hidden(t, par):
                act.wait_ge(hid_turned, t + 1)
                act.copy(hidT[par][:, :, :], h_bank[:, :].rearrange("p (c n) -> p c n", c=FC)).then_inc(
                    hidT_ready, 1)

            turned(0, 0)
            gate(0, 0)
            turned(1, 1)
            with act.Fori(0, SLOT_TILES // 2 - 1) as i:
                for par in range(2):
                    t = 2 * i + par
                    hidden(t, par)
                    gate(t + 1, 1 - par)
                    turned(t + 2, par)
            hidden(SLOT_TILES - 2, 0)
            gate(SLOT_TILES - 1, 1)
            hidden(SLOT_TILES - 1, 1)

            with act.Fori(0, NT // 4) as g:
                act.wait_ge(comb_mv, 4 * (g + 1))
                act.activation(zn[0][:, :], z_mv[:, :, 1], ACT.Ln, bias=eps4_col[:, :]).then_inc(comb_ln, 1)
                act.wait_ge(comb_ln, g + 1)
                act.activation(zn[1][:, :], zn[0][:, :], ACT.Exp, scale=-0.5).then_inc(comb_seed, 1)

        @block.vector
        def _(dve):
            def rsqrt_newton(seed, half_v, t2, t3, to, var, scale, chain, count, ready, at, eps=EPS):
                dve.tensor_scalar(half_v, var, -0.5 * scale, -0.5 * eps, ALU.mult, ALU.add).then_inc(chain, 1)
                dve.wait_ge(ready, at)
                dve.wait_ge(chain, count + 1)
                dve.tensor_tensor(t2, half_v, seed, ALU.mult).then_inc(chain, 1)
                dve.wait_ge(chain, count + 2)
                dve.tensor_tensor(t3, t2, seed, ALU.mult).then_inc(chain, 1)
                dve.wait_ge(chain, count + 3)
                dve.scalar_tensor_tensor(out=to, in0=t3, scalar=1.5, in1=seed, op0=ALU.add,
                                         op1=ALU.mult).then_inc(chain, 1)
                dve.wait_ge(chain, count + 4)

            dve.wait_ge(inputs_loaded, 16 * 12)
            dve.tensor_scalar(gains[:, :, :], gains[:, :, :], QK_SCALE, None, ALU.mult).then_inc(w_ready, 1)
            dve.tensor_scalar(shifts[:, :, :], shifts[:, :, :], QK_SCALE, None, ALU.mult).then_inc(w_ready, 1)
            dve.tensor_scalar(inv_temp[:, :], temp_col[:, :], 0.1, None, ALU.max).then_inc(w_ready, 1)
            dve.wait_ge(w_ready, 3)
            dve.reciprocal(inv_temp[:, :], inv_temp[:, :]).then_inc(w_ready, 1)
            for i in range(4):
                dve.wait_ge(w_turned, i + 1)
                for c in range(EC):
                    src = st_bank[i][:, c * EMB:(c + 1) * EMB]
                    if i < 3:
                        dve.tensor_copy(w_qkvT[:, c, :, i, :], src.rearrange("p (h n) -> p h n", h=2)).then_inc(
                            w_copied, 1)
                    else:
                        dve.tensor_copy(w_oT[:, c, :], src).then_inc(w_copied, 1)
            dve.wait_ge(w_turned, 5)
            dve.tensor_copy(rwT[:, :, :], out_bank[:, 0:EC * E].rearrange("p (c e) -> p c e", c=EC)).then_inc(
                w_copied, 1)
            dve.wait_ge(w_copied, 9)
            for i in range(2):
                for c in range(EC):
                    dve.tensor_reduce(w_mean[:, i, c, :], w_qkvT[:, c, :, i, :].rearrange(
                        "p h (g d) -> p h g d", d=D), AX, ALU.add).then_inc(w_mean_done, 1)
            dve.wait_ge(w_mean_done, 4)
            for i in range(2):
                for c in range(EC):
                    for h in range(2):
                        v = w_qkvT[:, c, h, i, :].rearrange("p (g d) -> p g d", d=D)
                        m = w_mean[:, i, c, h * HH:(h + 1) * HH].unsqueeze(2).broadcast_to([P, HH, D])
                        dve.scalar_tensor_tensor(out=v, in0=m, scalar=-1.0 / D, in1=v, op0=ALU.mult,
                                                 op1=ALU.add).then_inc(w_ready, 1)

            def values(b, half, p):
                u = 2 * b + half
                if p % 2 == 0:
                    return
                g = p // 2
                o = pv_bank[:, 0:TT * 4 * (D + 1)].rearrange("p (t h d) -> p t h d", t=TT, h=4)
                dve.wait_ge(pv_done, PAIRS * u + p + 1)
                dve.reciprocal(recip[:, :, :], o[:, :, :, D]).then_inc(recip_ready, 1)
                dve.wait_ge(recip_ready, 2 * u + g + 1)
                dve.tensor_tensor(heads[:, :, g * 4 * D:(g + 1) * 4 * D].rearrange("p t (h d) -> p t h d", h=4),
                                  o[:, :, :, 0:D], recip[:, :, :].unsqueeze(3).broadcast_to([P, TT, 4, D]),
                                  ALU.mult).then_inc(heads_ready, 1)

            def project(b, half):
                u = 2 * b + half
                dve.wait_ge(squares_ready, u + 1)
                dve.tensor_reduce(ssum[:, :, :], squares[:, :, :].rearrange("p t (h d) -> p t h d", d=D), AX,
                                  ALU.add).then_inc(ssum_ready, 1)
                dve.wait_ge(ssum_ready, u + 1)
                rsqrt_newton(nt[1][:, :, :], nt[2][:, :, :], nt[3][:, :, :], nt[4][:, :, :], rstd[:, :, :],
                             ssum[:, :, :], 1.0 / D, newton, 4 * u, seed_ready, u + 1)
                dve.tensor_tensor(normed[:, :, :].rearrange("p t (h d) -> p t h d", d=D),
                                  raw[:, :, :].rearrange("p t (h d) -> p t h d", d=D),
                                  rstd[:, :, :].unsqueeze(3).broadcast_to([P, TT, 2 * HH, D]),
                                  ALU.mult).then_inc(normed_ready, 1)

            def turn(b, half):
                u = 2 * b + half
                st = stack[half]
                n5 = normed[:, :, :].rearrange("p t (h d) -> p (t h) d", d=D)
                s5 = st[:, :, :, :, :].rearrange("p t s h w -> p (t s h) w")
                dve.wait_ge(shifted, 2 * (u + 1))
                dve.tensor_copy(s5[:, :, 0:D], n5).then_inc(high_ready, 1)
                dve.wait_ge(high_ready, u + 1)
                for s, at in ((0, 16), (1, 48)):
                    nrm = normed[:, :, s * P:(s + 1) * P].rearrange("p t (h d) -> p t h d", d=D)
                    dve.tensor_tensor(st[:, :, s, :, at:at + D], nrm, st[:, :, s, :, 0:D].bitcast(F32),
                                      ALU.subtract).then_inc(low_ready, 1)
                for p in range(PAIRS):
                    n, k, _ = at_turn(b, half, 0, p)
                    dve.wait_ge(prep_full, n + 1)
                    dve.tensor_copy(qT[half][:, p, :], prep_bank[k][:, :]).then_inc(prep_taken[k], 1)

            def maxima(b, half, p):
                u = 2 * b + half
                h0 = 2 * p
                for i, regions in enumerate(MAX_REGIONS):
                    n, k, _ = at_maxima(b, half, p, i)
                    dve.wait_ge(prep_full, n + 1)
                    s = prep_bank[k]
                    for h, t, c in regions:
                        last = dve.tensor_reduce(neg_max[:, t, h0 + h:h0 + h + 1], s[:, c:c + (t + 1) * P], AX,
                                                 ALU.max, negate=True)
                    last.then_inc(prep_taken[k], 1)
                prep_done(dve, at_maxima(b, half, p, MAXB - 1))
                m = neg_max[:, :, h0:h0 + 2]
                high = stack[half][:, :, 0, h0:h0 + 2, 32]
                dve.tensor_copy(high, m).then_inc(max_high, 1)
                dve.wait_ge(max_high, PAIRS * u + p + 1)
                dve.tensor_tensor(stack[half][:, :, 0, h0:h0 + 2, 33], m, high.bitcast(F32),
                                  ALU.subtract).then_inc(max_ready, 1)

            def nothing(*_):
                pass

            def finish_batch(b):
                dve.wait_ge(res_ready, b + 1)
                for i in range(2):
                    dve.wait_ge(out_full, OUT_BATCH * b + 2 * OUT_HALF + i + 1)
                    dve.tensor_tensor(y[:, 2 * i:2 * i + 2, :], out_bank[:, :].rearrange("p (t e) -> p t e", t=2),
                                      x_res[:, 2 * i:2 * i + 2, :], ALU.add).then_inc(
                        out_taken, 1)
                dve.wait_ge(out_taken, OUT_BATCH * b + 2 * OUT_HALF + 2)
                for t in range(TT):
                    dve.bn_stats(y_stats[:, t, :], y[:, t, :]).then_inc(y_stats_ready, 1)
                dve.wait_ge(y_stats_ready, TT * (b + 1))
                dve.sem_inc(wait_passed, 1)
                for t in range(TT):
                    dve.bn_aggr(y_mv[:, t, :], y_stats[:, t, :]).then_inc(y_mv_ready, 1)
                dve.wait_ge(y_mv_ready, TT * (b + 1))
                rsqrt_newton(yn[1][:, :], yn[2][:, :], yn[3][:, :], yn[4][:, :], y_rstd[:, :], y_mv[:, :, 1], 1.0,
                             y_newton, 4 * b, y_seed_ready, b + 1)
                at_least(dve, x1_saved, 16 * b)
                for t in range(TT):
                    dve.tensor_scalar(x1[:, t, :], y[:, t, :], y_mv[:, t, 0:1], y_rstd[:, t:t + 1], ALU.subtract,
                                      ALU.mult).then_inc(x1_ready, 1)
                dve.wait_ge(out_full, OUT_BATCH * (b + 1))
                dve.tensor_tensor(logits[:, :, bass.ds(b, 1), :].rearrange("p t o e -> p (t o) e"),
                                  out_bank[:, 0:TT * E].rearrange("p (t e) -> p t e", e=E),
                                  rb_row[:, :].unsqueeze(1).broadcast_to([P, TT, E]), ALU.add).then_inc(
                    out_taken, 1)

            all_batches(dve, nothing, values, project, turn, maxima, nothing, finish_batch)

            lg = logits[:, :, :, :].rearrange("p t b e -> p (t b) e")
            dve.wait_ge(out_taken, OUT_BATCH * NB)
            dve.tensor_scalar(lg, lg, inv_temp[:, 0:1], None, ALU.mult).then_inc(route_v, 1)
            for i in range(ITERS):
                dve.wait_ge(route_v, routed(i, 0))
                dve.tensor_reduce(row_a[:, :], lg, AX, ALU.max).then_inc(rows_max, 1)
                dve.wait_ge(rows_max, i + 1)
                dve.tensor_tensor(lg, lg, row_a[:, :].unsqueeze(2).broadcast_to([P, NT, E]), ALU.subtract).then_inc(
                    route_v, 1)
                dve.wait_ge(route_a, 4 * i + 1)
                dve.tensor_reduce(row_a[:, :], exps[:, :, :], AX, ALU.add).then_inc(route_v, 1)
                dve.wait_ge(route_a, 4 * i + 2)
                dve.tensor_tensor(lg, lg, row_b[:, :].unsqueeze(2).broadcast_to([P, NT, E]), ALU.subtract).then_inc(
                    route_v, 1)
                dve.wait_ge(route_p, 2 * i + 1)
                dve.tensor_reduce(col_nmax[:, :], st_bank[0][0:NB * E, :], AX, ALU.max, negate=True).then_inc(
                    route_v, 1)
                dve.wait_ge(route_a, 4 * i + 4)
                dve.tensor_tensor(col_lse[:, :], col_ln[:, :], col_nmax[:, :], ALU.subtract).then_inc(route_v, 1)
                dve.wait_ge(route_v, routed(i, 5))
                dve.tensor_scalar(col_diag[:, :], ident[0:NB * E, 0:NB * E], col_lse[:, 0:1], None,
                                  ALU.mult).then_inc(route_v, 1)
                dve.wait_ge(route_p, 2 * i + 2)
                cols = st_bank[1][:, 0:NB * E].rearrange("p (b e) -> p b e", b=NB).unsqueeze(1).broadcast_to(
                    [P, TT, NB, E])
                dve.tensor_tensor(logits[:, :, :, :], logits[:, :, :, :], cols, ALU.subtract).then_inc(route_v, 1)
            done = routed(ITERS, 0)
            dve.wait_ge(route_a, 4 * ITERS + 1)
            link = Chain(dve, route_v, done)
            link(dve.tensor_reduce(row_a[:, :], gates[:, :, :], AX, ALU.add))
            link(dve.tensor_scalar(row_a[:, :], row_a[:, :], 1e-8, None, ALU.add))
            link(dve.reciprocal(row_b[:, :], row_a[:, :]))
            link(dve.tensor_tensor(gates[:, :, :], gates[:, :, :], row_b[:, :].unsqueeze(2).broadcast_to([P, NT, E]),
                                   ALU.mult))
            for t in range(NT):
                last = dve.max(best[:, t, :], gates[:, t, :])
            link(last)
            for t in range(NT):
                last = dve.max_index(best_at[:, t, :], best[:, t, :], gates[:, t, :])
            link(last)
            link(dve.tensor_copy(best_atf[:, :, :], best_at[:, :, 0:K]))
            dve.wait_ge(iotas_ready, 3)
            for k in range(K):
                link(dve.tensor_tensor(chosen[k][:, :, :], best_atf[:, :, k:k + 1].broadcast_to([P, NT, E]),
                                       expert_iota[:, :].unsqueeze(1).broadcast_to([P, NT, E]), ALU.is_equal))
            dve.tensor_tensor(chosen_b[:, :, :], chosen[0][:, :, :], chosen[1][:, :, :], ALU.add).then_inc(choice_ready, 1)
            dve.wait_ge(route_p, 2 * ITERS + 1)
            link(dve.tensor_copy(counts[:, :, :], st_bank[3][:, 0:NT * E].rearrange("p (t e) -> p t e", e=E)))
            src, step, n = counts, 1, 0
            while step < NT:
                dst = scan[n % 2]
                link(dve.tensor_copy(dst[:, 0:step, :], src[:, 0:step, :]))
                link(dve.tensor_tensor(dst[:, step:, :], src[:, step:, :], src[:, 0:NT - step, :], ALU.add))
                src, step, n = dst, 2 * step, n + 1
            upto, other = src, scan[n % 2]
            link(dve.tensor_scalar(n_tiles_i[:, :], upto[:, NT - 1, :], float(P - 1), None, ALU.add))
            link(dve.tensor_scalar(n_tiles_j[:, :], n_tiles_i[:, :], 7, None, ALU.arith_shift_right))
            link(dve.tensor_copy(n_tiles[:, :], n_tiles_j[:, :]))
            src_e, step, n = n_tiles, 1, 0
            while step < E:
                dst = escan[n % 2]
                link(dve.tensor_copy(dst[:, 0:step], src_e[:, 0:step]))
                link(dve.tensor_tensor(dst[:, step:], src_e[:, step:], src_e[:, 0:E - step], ALU.add))
                src_e, step, n = dst, 2 * step, n + 1
            link(dve.tensor_tensor(first_slot[:, :], src_e[:, :], n_tiles[:, :], ALU.subtract))
            link(dve.tensor_scalar(first_slot[:, :], first_slot[:, :], float(P), None, ALU.mult))
            link(dve.tensor_tensor(past[:, :, :], src_e[0:1, :].unsqueeze(1).broadcast_to([1, SLOT_TILES, E]),
                                   tile_iota[:, :].unsqueeze(2).broadcast_to([1, SLOT_TILES, E]), ALU.is_le))
            link(dve.tensor_reduce(tile_ef[:, :], past[:, :, :], AX, ALU.add))
            dve.tensor_scalar(tile_e[:, :], tile_ef[:, :], float(E - 1), None, ALU.min).then_inc(tiles_ready, 1)
            link(dve.tensor_tensor(other[:, :, :], upto[:, :, :], counts[:, :, :], ALU.subtract))
            link(dve.tensor_tensor(other[:, :, :], other[:, :, :],
                                   st_bank[2][:, 0:NT * E].rearrange("p (t e) -> p t e", e=E), ALU.add))
            link(dve.tensor_tensor(slot_all[:, :, :], other[:, :, :],
                                   first_slot[:, :].unsqueeze(1).broadcast_to([P, NT, E]), ALU.add))
            for k in range(K):
                link(dve.tensor_tensor(slot_of[k][:, :, :], slot_all[:, :, :], chosen[k][:, :, :], ALU.mult))
                link(dve.tensor_reduce(slot_f[:, k, :], slot_of[k][:, :, :], AX, ALU.add))
            dve.tensor_copy(slot_u[:, :, :], slot_f[:, :, :]).then_inc(slots_ready, 1)
            dve.wait_ge(x1_loaded, 16 * NB)
            dve.tensor_copy(x1_all[:, :, EMB].bitcast(U32), result_row[:, :]).then_inc(rows_named, 1)
            link(dve.tensor_tensor(top_sum[:, :], best[:, :, 0], best[:, :, 1], ALU.add))
            link(dve.tensor_scalar(top_sum[:, :], top_sum[:, :], 1e-8, None, ALU.add))
            link(dve.reciprocal(top_sum[:, :], top_sum[:, :]))
            link(dve.tensor_scalar(top_sum[:, :], top_sum[:, :], 0.5, None, ALU.mult))
            link(dve.tensor_tensor(top_gate[:, :, :].rearrange("p (b t) k -> p t b k", b=NB),
                                   best[:, :, 0:K].rearrange("p (t b) k -> p t b k", b=NB),
                                   top_sum[:, :].rearrange("p (t b) -> p t b", b=NB).unsqueeze(3).broadcast_to(
                                       [P, TT, NB, K]), ALU.mult))
            dve.wait_ge(scattered[0], 16 * NT)
            dve.tensor_scalar(x1_all[:, :, EMB].bitcast(U32), result_row[:, :], 1.0, None, ALU.add).then_inc(
                rows_named, 1)

            def hidden(t, par):
                dve.wait_ge(relu_ready, t + 1)
                dve.wait_ge(p_full, t + 1)
                dve.tensor_tensor(hid[par][:, :], gate_act[par][:, :], p_bank[:, :], ALU.mult).then_inc(hid_ready, 1)

            def result(i, k):
                t, par = 4 * i + k, k % 2
                dve.wait_ge(yo_full, t + 1)
                at_least(dve, yo_sent[par], 16 * (2 * i + k // 2))
                dve.tensor_copy(y_out[par][:, :], y_bank[:, 0:EMB]).then_inc(yo_ready, 1)
                dve.tensor_copy(y_at[par][:, :], xg[k][:, EMB:EMB + 1].bitcast(U32)).then_inc(yo_ready, 1)

            def four_tiles(i, last=False):
                for k in range(4):
                    if not (last and k == 3):
                        hidden(4 * i + k + 1, (k + 1) % 2)
                    result(i, k)

            hidden(0, 0)
            four_tiles(0)
            with dve.Fori(1, SLOT_TILES // 4 - 1) as i:
                four_tiles(i)
            four_tiles(SLOT_TILES // 4 - 1, True)

            def four(g, first):
                for j in range(4):
                    dve.wait_ge(yt_loaded[j], 16 * (g + 1))
                    if not first:
                        dve.wait_ge(stored[j], 16 * g)
                    dve.scalar_tensor_tensor(out=acc[j][:, :], in0=y_two[j][:, 0, :],
                                             scalar=top_gate[:, bass.ds(4 * g + j, 1), 0],
                                             in1=x1_all[:, bass.ds(4 * g + j, 1), 0:EMB].rearrange(
                                                 "p o e -> p (o e)"), op0=ALU.mult, op1=ALU.add).then_inc(comb_a, 1)
                for j in range(4):
                    dve.wait_ge(comb_a, 4 * g + j + 1)
                    dve.scalar_tensor_tensor(out=acc[j][:, :], in0=y_two[j][:, 1, :],
                                             scalar=top_gate[:, bass.ds(4 * g + j, 1), 1], in1=acc[j][:, :],
                                             op0=ALU.mult, op1=ALU.add).then_inc(comb_b, 1)
                for j in range(4):
                    dve.wait_ge(comb_b, 4 * g + j + 1)
                    dve.bn_stats(z_stats[:, j, :], acc[j][:, :]).then_inc(comb_stats, 1)
                dve.wait_ge(comb_stats, 4 * (g + 1))
                dve.sem_inc(wait_passed, 1)
                for j in range(4):
                    dve.bn_aggr(z_mv[:, j, :], z_stats[:, j, :]).then_inc(comb_mv, 1)
                dve.wait_ge(comb_mv, 4 * (g + 1))
                rsqrt_newton(zn[1][:, :], zn[2][:, :], zn[3][:, :], zn[4][:, :], z_rstd[:, :], z_mv[:, :, 1], 1.0,
                             comb_newton, 4 * g, comb_seed, g + 1, EPS / 4)
                for j in range(4):
                    dve.tensor_scalar(acc[j][:, :], acc[j][:, :], z_mv[:, j, 0:1], z_rstd[:, j:j + 1], ALU.subtract,
                                      ALU.mult).then_inc(comb_ready, 1)

            four(0, True)
            with dve.Fori(1, NT // 4) as g:
                four(g, False)

        @block.tensor
        def _(pe):
            pe.wait_ge(consts_ready, 18)
            pe.wait_ge(inputs_loaded, 16 * 12)
            for i in range(4):
                for c in range(EC):
                    for r in range(2):
                        last = pe.transpose(st_bank[i][:, c * EMB + r * P:c * EMB + (r + 1) * P],
                                            w_rows[:, i, r, c * P:(c + 1) * P], ident[:, :])
                last.then_inc(w_turned, 1)
            for c in range(EC):
                last = pe.transpose(out_bank[:, c * E:(c + 1) * E], rw_rows[:, c * P:(c + 1) * P], ident[0:E, 0:E])
            last.then_inc(w_turned, 1)
            pe.wait_ge(w_ready, 12)

            def prep_wait(n, k, uses):
                at_least(pe, prep_taken[k], uses)
                return prep_bank[k]

            def project(b, half):
                if half == 0:
                    pe.wait_ge(x_loaded, 16 * (b + 1))
                    for c in range(EC):
                        step = prep_step(b, 0, c)
                        to = prep_wait(*step)
                        for t in range(TT):
                            last = pe.transpose(to[:, t * P:(t + 1) * P], x_in[:, t, c * P:(c + 1) * P], ident[:, :])
                        last.then_inc(prep_full, 1)
                    for c in range(EC):
                        prep_done(pe, prep_step(b, 0, c))
                for t in range(TT):
                    to = prep_wait(*at_project(b, half, t))
                    for c in range(EC):
                        last = pe.matmul(to[:, 0:3 * P], xT[:, c, t * P:(t + 1) * P],
                                         w_qkvT[:, c, half, :, :].rearrange("p s n -> p (s n)"),
                                         start=c == 0, stop=c == EC - 1)
                    last.then_inc(prep_full, 1)

            def turn(b, half):
                u = 2 * b + half
                pe.wait_ge(low_ready, 2 * (u + 1))
                pe.wait_ge(again_ready, 2 * (u + 1))
                pe.wait_ge(max_cleared, u + 1)
                for s in (1, 0):
                    for p in range(PAIRS):
                        to = prep_wait(*at_turn(b, half, s, p))
                        for t in range(TT):
                            last = pe.transpose(to[:, t * P:(t + 1) * P],
                                                stack[half][:, t, s, 2 * p:2 * p + 2, :].rearrange(
                                                    "p h w -> p (h w)").bitcast(F32), ident[:, :])
                        last.then_inc(prep_full, 1)

            def maxima(b, half, p):
                u = 2 * b + half
                prep_done(pe, at_turn(b, half, 1, p))
                prep_done(pe, at_turn(b, half, 0, p))
                for i, regions in enumerate(MAX_REGIONS):
                    to = prep_wait(*at_maxima(b, half, p, i))
                    for n, (h, t, c) in enumerate(regions):
                        rows = slice(h * SW, (h + 1) * SW)
                        pe.matmul(to[:, c:c + (t + 1) * P], qT[half][rows, p, t * P:(t + 1) * P],
                                  kT[half][rows, p, 0:(t + 1) * P], start=n == 0, stop=False, skip_group_check=True)
                        last = pe.matmul(to[:, c + t * P:c + (t + 1) * P], ident_b[:, :], mask_ij[:, :], start=False,
                                         stop=n == len(regions) - 1, skip_group_check=True)
                    last.then_inc(prep_full, 1)

            def scores(b, half, p):
                u = 2 * b + half
                pe.wait_ge(max_ready, PAIRS * u + p + 1)
                at_least(pe, out_taken, OUT_BATCH * b + OUT_HALF * half + p)
                for t in range(TT):
                    last = pe.transpose(out_bank[:, t * P:(t + 1) * P],
                                        stack[half][:, t, 0, 2 * p:2 * p + 2, :].rearrange(
                                            "p h w -> p (h w)").bitcast(F32), ident[:, :])
                last.then_inc(out_full, 1)
                pe.wait_ge(out_taken, OUT_BATCH * b + OUT_HALF * half + p + 1)
                for i, regions in enumerate(ST_REGIONS):
                    idx = 6 * p + i
                    to = st_bank[idx % 4]
                    at_least(pe, st_taken[idx % 4], PIECES // 4 * u + idx // 4)
                    for n, (h, j, c) in enumerate(regions):
                        rows = slice(h * SW, (h + 1) * SW)
                        w = (TT - j) * P
                        pe.matmul(to[:, c:c + w], kT[half][rows, p, j * P:(j + 1) * P],
                                  qT[half][rows, p, j * P:T], start=n == 0, stop=False, skip_group_check=True)
                        last = pe.matmul(to[:, c:c + P], ident_b[:, :], mask_ji[:, :], start=False,
                                         stop=n == len(regions) - 1, skip_group_check=True)
                    last.then_inc(st_full, 1)

            def values(b, half, p):
                u = 2 * b + half
                prep_done(pe, at_project(b, half, TT - 1))
                pe.wait_ge(st_taken[(6 * p + 5) % 4], PIECES // 4 * u + (6 * p + 5) // 4 + 1)
                if p % 2 == 0:
                    at_least(pe, heads_ready, 2 * u + p // 2)
                for h in range(2):
                    h4 = (2 * p + h) % 4
                    for t in range(TT):
                        at = (t * 4 + h4) * (D + 1)
                        for j in range(t + 1):
                            i, c = PLACE[h, j]
                            c += (t - j) * P
                            last = pe.matmul(pv_bank[:, at:at + D + 1], probsT[p % 2][:, i, c:c + P],
                                             v_aug[half][:, j, 2 * p + h, :], start=j == 0, stop=j == t)
                last.then_inc(pv_done, 1)

            def finish_half(b, half):
                u = 2 * b + half
                pe.wait_ge(heads_ready, 2 * (u + 1))
                at_least(pe, out_taken, OUT_BATCH * b + OUT_HALF * half + PAIRS)
                for t in range(TT):
                    last = pe.transpose(out_bank[:, t * P:(t + 1) * P], heads[:, t, :], ident[:, :])
                last.then_inc(out_full, 1)

            def finish_batch(b):
                at = OUT_BATCH * b + 2 * OUT_HALF
                pe.wait_ge(out_taken, at)
                for i in range(2):
                    pe.wait_ge(out_taken, at + i)
                    for t in range(2):
                        for c in range(EC):
                            last = pe.matmul(out_bank[:, t * EMB:(t + 1) * EMB],
                                             headsT[:, c, (2 * i + t) * P:(2 * i + t + 1) * P], w_oT[:, c, :],
                                             start=c == 0, stop=c == EC - 1)
                    last.then_inc(out_full, 1)
                pe.wait_ge(x1_ready, TT * (b + 1))
                for c in range(EC):
                    pe.wait_ge(out_taken, at + 2 + c)
                    for t in range(TT):
                        last = pe.transpose(out_bank[:, t * P:(t + 1) * P], x1[:, t, c * P:(c + 1) * P], ident[:, :])
                    last.then_inc(out_full, 1)
                pe.wait_ge(out_taken, at + 2 + EC)
                for t in range(TT):
                    for c in range(EC):
                        last = pe.matmul(out_bank[:, t * E:(t + 1) * E], x1T[:, c, t * P:(t + 1) * P], rwT[:, c, :],
                                         start=c == 0, stop=c == EC - 1)
                last.then_inc(out_full, 1)

            all_batches(pe, scores, values, project, turn, maxima, finish_half, finish_batch)

            for i in range(ITERS):
                pe.wait_ge(route_v, routed(i, 3))
                for t in range(TT):
                    last = pe.transpose(st_bank[0][0:NB * E, t * P:(t + 1) * P], logits[:, t, :, :].rearrange("p b e -> p (b e)"), ident[:, :])
                last.then_inc(route_p, 1)
                pe.wait_ge(route_v, routed(i, 6))
                pe.matmul(st_bank[1][:, 0:NB * E], ones[0:NB * E, :], col_diag[:, :], start=True,
                          stop=True).then_inc(route_p, 1)
            pe.wait_ge(choice_ready, 1)
            pe.matmul(st_bank[2][:, 0:NT * E], before_b[:, :], chosen_b[:, :, :].rearrange("p t e -> p (t e)"),
                      start=True, stop=True)
            pe.matmul(st_bank[3][:, 0:NT * E], ones_b[:, :], chosen_b[:, :, :].rearrange("p t e -> p (t e)"),
                      start=True, stop=True).then_inc(route_p, 1)

            def turn_x(i, k):
                t = 4 * i + k
                pe.wait_ge(xg_loaded[k % 4], 16 * (i + k // 4 + 1))
                at_least(pe, xgT_ready, t)
                for c in range(EC):
                    last = pe.transpose(x_bank[:, c * P:(c + 1) * P], xg[k % 4][:, c * P:(c + 1) * P], ident[:, :])
                last.then_inc(xg_turned, 1)

            def up(i, k):
                t = 4 * i + k
                e = pe.value_load(tile_e[0:1, bass.ds(t, 1)], min_val=0, max_val=E - 1)
                pe.wait_ge(xgT_ready, t + 1)
                at_least(pe, hid_ready, t)
                for w, to, full in ((wg_sb, g_bank, g_full), (wp_sb, p_bank, p_full)):
                    for c in range(EC):
                        last = pe.matmul(to[:, :], xgT[k % 2][:, c, :],
                                         w[:, bass.ds(e, 1), c * FF:(c + 1) * FF].rearrange("p o n -> p (o n)"),
                                         start=c == 0, stop=c == EC - 1)
                    last.then_inc(full, 1)

            def turn_h(i, k):
                t = 4 * i + k
                pe.wait_ge(hid_ready, t + 1)
                at_least(pe, hidT_ready, t)
                for c in range(FC):
                    last = pe.transpose(h_bank[:, c * P:(c + 1) * P], hid[k % 2][:, c * P:(c + 1) * P], ident[:, :])
                last.then_inc(hid_turned, 1)

            def down(i, k):
                t = 4 * i + k
                e = pe.value_load(tile_e[0:1, bass.ds(t, 1)], min_val=0, max_val=E - 1)
                pe.wait_ge(hidT_ready, t + 1)
                at_least(pe, yo_ready, 2 * t)
                for c in range(FC):
                    last = pe.matmul(y_bank[:, 0:EMB], hidT[k % 2][:, c, :],
                                     wo_sb[:, bass.ds(e, 1), c * EMB:(c + 1) * EMB].rearrange("p o n -> p (o n)"),
                                     start=c == 0, stop=c == FC - 1)
                last.then_inc(yo_full, 1)

            def four_tiles(i, last=False):
                for k in range(4):
                    turn_h(i, k)
                    if not (last and k == 3):
                        up(i, k + 1)
                    if not (last and k >= 2):
                        turn_x(i, k + 2)
                    down(i, k)

            pe.wait_ge(tiles_ready, 1)
            pe.wait_ge(slots_ready, 1)
            pe.wait_ge(experts_loaded, 16 * 3 * E)
            turn_x(0, 0)
            up(0, 0)
            turn_x(0, 1)
            four_tiles(0)
            with pe.Fori(1, SLOT_TILES // 4 - 1) as i:
                four_tiles(i)
            four_tiles(SLOT_TILES // 4 - 1, True)


_INS = ["L0_attn_x", "L0_attn_Wk", "L0_attn_Wq", "L0_attn_Wv", "L0_attn_Wo", "L0_attn_bo", "L0_attn_kln_g",
        "L0_attn_kln_b", "L0_attn_qln_g", "L0_attn_qln_b", "L0_ffn_router_w", "L0_ffn_router_b",
        "L0_ffn_temperature", "L0_ffn_wg", "L0_ffn_wp", "L0_ffn_wo"]


def kernel(**inputs):
    import numpy as np
    import concourse.bacc as bacc
    from concourse.bass_utils import run_bass_kernel_spmd

    nc = bacc.Bacc("TRN2", target_bir_lowering=False, num_devices=1)
    arrays, args = {}, []
    for name in _INS:
        v = np.ascontiguousarray(inputs[name])
        arrays[f"in_{name}"] = v
        args.append(nc.dram_tensor(f"in_{name}", v.shape, mybir.dt.from_np(v.dtype), kind="ExternalInput").ap())
    args.append(nc.dram_tensor("out_dram", (NB, T, EMB), F32, kind="ExternalOutput").ap())
    layer(nc, *args)
    r = run_bass_kernel_spmd(nc, [arrays], core_ids=[0])
    return r.results[0]["out_dram"]
```

```python
from contextlib import ExitStack

import concourse.bass as bass
from concourse import mybir

P = 128
NB, T, EMB = 8, 512, 256
H, D = 16, 16
E, FF, K = 8, 512, 2
TT = T // P
NT = NB * TT
EC = EMB // P
FC = FF // P
HH = H // 2
PAIRS = HH // 2
SW = 64
EPS = 1e-5
QK_SCALE = EMB ** -0.25
MASKED = -1e30
SLOT_TILES = NB * T * K // P + E
SLOTS = SLOT_TILES * P
XW = EMB + 1
ITERS = 3

ALU = mybir.AluOpType
ACT = mybir.ActivationFunctionType
AX = mybir.AxisListType.X
F32 = mybir.dt.float32
F32R = mybir.dt.float32r
BF16 = mybir.dt.bfloat16
I32 = mybir.dt.int32
U32 = mybir.dt.uint32

MAXB = 6
VW = 32
PIECES = 6
STB = 3


def at_least(engine, semaphore, value):
    if not isinstance(value, int) or value > 0:
        engine.wait_ge(semaphore, value)


class Batch:

    def __init__(self, at, like=None):
        self.at, self.like = at, at if like is None else like

    def after(self, n):
        return Batch(self.at + n, self.like + n)


class Order:

    def __init__(self, steps, banks):
        self.number = {step: n for n, step in enumerate(steps)}
        self.banks = banks
        per = [self.number[s] - self.number[(s[0], s[1] - 1) + s[2:]] for s in steps if s[1] == 3]
        assert len(set(per)) == 1 and per[0] % banks == 0
        self.per_batch = per[0]

    def __call__(self, kind, b, half, i):
        n = self.number[kind, b.like, half, i]
        ahead = b.at - b.like
        return (self.per_batch * ahead + n, n % self.banks, self.per_batch // self.banks * ahead + n // self.banks)


class Chain:

    def __init__(self, engine, semaphore, count):
        self.engine, self.semaphore, self.count = engine, semaphore, count

    def __call__(self, instruction):
        self.count += 1
        instruction.then_inc(self.semaphore, 1)
        self.engine.wait_ge(self.semaphore, self.count)


def layer(nc, x, Wk, Wq, Wv, Wo, bo, kln_g, kln_b, qln_g, qln_b, router_w, router_b,
          temperature, wg, wp, wo, out):
    x_tiles = x.rearrange("b (t p) e -> b p t e", p=P)
    out_tiles = out.rearrange("b (t p) e -> (b t) p e", p=P)
    x1_dram = nc.dram_tensor("x1_dram", [NB, P, TT, EMB], F32, kind="Internal").ap()
    xs_dram = nc.dram_tensor("xs_dram", [SLOTS, XW], F32, kind="Internal").ap()
    ys_dram = nc.dram_tensor("ys_dram", [NB * T * K + SLOTS, EMB], F32, kind="Internal").ap()

    with ExitStack() as ctx:
        def sb(name, shape, dt=F32, where=ctx):
            return where.enter_context(nc.sbuf_tensor(name, shape, dt))

        def bank(name, shape=(P, 512), dt=F32, where=ctx):
            return where.enter_context(nc.psum_tensor(name, list(shape), dt))

        def sem(name):
            return ctx.enter_context(nc.semaphore(name))

        experts = sb("experts", [P, 2, E * EC * FF])
        wg_sb = experts[:, 0, :].rearrange("p (e n) -> p e n", e=E)
        wp_sb = experts[:, 1, :].rearrange("p (e n) -> p e n", e=E)
        flat = experts[:, :, :].rearrange("p a n -> p (a n)")
        w_rows = flat[:, 2 * E * EC * FF - 8 * EMB:].rearrange("p (i c e) -> p i c e", i=4, c=2)
        empty_slots = flat[:, 0:SLOT_TILES // 2 * XW].rearrange("p (t w) -> p t w", w=XW)
        ident = sb("ident", [P, P])
        ident_b = sb("ident_b", [P, P], BF16)
        ones = sb("ones", [P, P])
        ones_b = sb("ones_b", [P, P], BF16)
        before_b = sb("before_b", [P, P], BF16)
        mask_ij = sb("mask_ij", [P, P], BF16)
        mask_ji = sb("mask_ji", [P, P], BF16)
        eps_col = sb("eps_col", [P, 1])
        eps4_col = sb("eps4_col", [P, 1])
        logits = sb("logits", [P, TT, NB, E])
        rb_row = sb("rb_row", [P, E])
        temp_col = sb("temp_col", [P, 1])
        inv_temp = sb("inv_temp", [P, 1])

        spare = flat[:, SLOT_TILES // 2 * XW:2 * E * EC * FF - 8 * EMB]
        x_in, x_res, y, x1 = (spare[:, i * TT * EMB:(i + 1) * TT * EMB].rearrange("p (t e) -> p t e", e=EMB)
                              for i in range(4))

        att_mem = ExitStack()
        a = lambda name, shape, dt=F32: sb(name, shape, dt, att_mem)
        w_qkvT = a("w_qkvT", [P, EC, 2, 3, P])
        w_oT = a("w_oT", [P, EC, EMB])
        w_mean = a("w_mean", [P, 2, EC, H])
        rw_rows = a("rw_rows", [E, EMB])
        rwT = a("rwT", [P, EC, E])
        gains = a("gains", [P, 2, D])
        shifts = a("shifts", [P, 2, D])
        bo_row = a("bo_row", [P, EMB])
        xT = a("xT", [P, EC, T])
        raw = a("raw", [P, TT, 2 * P])
        normed = a("normed", [P, TT, 2 * P])
        squares = normed
        ssum = a("ssum", [P, TT, 2 * HH])
        nt = [a(f"nt{i}", [P, TT, 2 * HH]) for i in range(5)]
        rstd = a("rstd", [P, TT, 2 * HH])
        stack = [a(f"stack{i}", [P, TT, 2, HH, SW], F32R) for i in range(2)]
        kT = [a(f"kT{i}", [P, PAIRS, T], F32R) for i in range(2)]
        qT = [a(f"qT{i}", [P, PAIRS, T], F32R) for i in range(2)]
        v_aug = [a(f"v_aug{i}", [P, TT, HH, VW]) for i in range(2)]
        neg_max = a("neg_max", [P, TT, HH])
        probsT = [a(f"probsT{i}", [P, 6, 512]) for i in range(2)]
        sumsT = a("sumsT", [P, T])
        recip = a("recip", [P, TT, 4])
        heads = a("heads", [P, TT, P])
        headsT = a("headsT", [P, 2, T])
        y_stats = a("y_stats", [P, TT, 6])
        y_mv = a("y_mv", [P, TT, 2])
        yn = [a(f"yn{i}", [P, TT]) for i in range(5)]
        y_rstd = a("y_rstd", [P, TT])
        x1T = headsT
        att_mem.close()

        ffn_mem = ExitStack()
        f = lambda name, shape, dt=F32: sb(name, shape, dt, ffn_mem)
        x1_all = f("x1_all", [P, NT, XW])
        wo_sb = f("wo_sb", [P, E, FC * EMB])
        row_a = f("row_a", [P, NT])
        row_b = f("row_b", [P, NT])
        exps = f("exps", [P, NT, E])
        col_nmax = f("col_nmax", [NB * E, 1])
        col_exps = f("col_exps", [NB * E, T])
        col_sum = f("col_sum", [NB * E, 1])
        col_ln = f("col_ln", [NB * E, 1])
        col_lse = f("col_lse", [NB * E, 1])
        col_diag = f("col_diag", [NB * E, NB * E])
        gates = f("gates", [P, NT, E])
        best = f("best", [P, NT, 8])
        best_at = f("best_at", [P, NT, 8], U32)
        best_atf = f("best_atf", [P, NT, K])
        expert_iota = f("expert_iota", [P, E])
        chosen = [f(f"chosen{k}", [P, NT, E]) for k in range(K)]
        chosen_b = f("chosen_b", [P, NT, E], BF16)
        counts = f("counts", [P, NT, E])
        scan = [f(f"scan{i}", [P, NT, E]) for i in range(2)]
        n_tiles_i = f("n_tiles_i", [P, E], I32)
        n_tiles_j = f("n_tiles_j", [P, E], I32)
        n_tiles = f("n_tiles", [P, E])
        escan = [f(f"escan{i}", [P, E]) for i in range(2)]
        first_slot = f("first_slot", [P, E])
        slot_all = f("slot_all", [P, NT, E])
        slot_of = [f(f"slot_of{k}", [P, NT, E]) for k in range(K)]
        slot_f = f("slot_f", [P, K, NT])
        slot_u = f("slot_u", [P, K, NT], U32)
        top_sum = f("top_sum", [P, NT])
        top_gate = f("top_gate", [P, NT, K])
        result_row = f("result_row", [P, NT], U32)
        tile_iota = f("tile_iota", [1, SLOT_TILES])
        past = f("past", [1, SLOT_TILES, E])
        tile_ef = f("tile_ef", [1, SLOT_TILES])
        tile_e = f("tile_e", [1, SLOT_TILES], I32)
        xg = [f(f"xg{i}", [P, XW]) for i in range(4)]
        xgT = [f(f"xgT{i}", [P, EC, P]) for i in range(2)]
        gate_act = [f(f"gate_act{i}", [P, FF]) for i in range(2)]
        hid = [f(f"hid{i}", [P, FF]) for i in range(2)]
        hidT = [f(f"hidT{i}", [P, FC, P]) for i in range(2)]
        y_out = [f(f"y_out{i}", [P, EMB]) for i in range(2)]
        y_at = [f(f"y_at{i}", [P, 1], U32) for i in range(2)]
        y_two = [f(f"y_two{i}", [P, K, EMB]) for i in range(4)]
        acc = [f(f"acc{i}", [P, EMB]) for i in range(4)]
        z_stats = f("z_stats", [P, 4, 6])
        z_mv = f("z_mv", [P, 4, 2])
        zn = [f(f"zn{i}", [P, 4]) for i in range(5)]
        z_rstd = f("z_rstd", [P, 4])
        ffn_mem.close()

        psum_a = ExitStack()
        st_bank = [bank(f"st_bank{i}", where=psum_a) for i in range(STB)]
        pv_bank = [bank(f"pv_bank{i}", where=psum_a) for i in range(2)]
        prep_bank = [bank(f"prep_bank{i}", where=psum_a) for i in range(2)]
        out_bank = bank("out_bank", where=psum_a)
        other_bank = st_bank + pv_bank[0:1]
        g_bank, p_bank, h_bank, y_bank = other_bank
        x_bank = prep_bank[0]

        consts_ready = sem("consts_ready")
        inputs_loaded = sem("inputs_loaded")
        w_turned = sem("w_turned")
        w_copied = sem("w_copied")
        w_mean_done = sem("w_mean_done")
        w_ready = sem("w_ready")
        slots_imaged = sem("slots_imaged")
        slots_emptied = sem("slots_emptied")
        experts_loaded = sem("experts_loaded")
        x_loaded = sem("x_loaded")
        res_loaded = sem("res_loaded")
        res_ready = sem("res_ready")
        prep_full = sem("prep_full")
        prep_taken = [sem(f"prep_taken{i}") for i in range(2)]
        raw_ready = sem("raw_ready")
        squares_ready = sem("squares_ready")
        ssum_ready = sem("ssum_ready")
        ln_ready = sem("ln_ready")
        seed_ready = sem("seed_ready")
        newton = sem("newton")
        normed_ready = sem("normed_ready")
        gained_q = sem("gained_q")
        gained_k = sem("gained_k")
        shifted_q = sem("shifted_q")
        shifted_k = sem("shifted_k")
        high_ready = sem("high_ready")
        low_ready = sem("low_ready")
        again_ready = sem("again_ready")
        max_cleared = sem("max_cleared")
        max_high = sem("max_high")
        max_ready = sem("max_ready")
        out_full = sem("out_full")
        out_taken = sem("out_taken")
        st_full = sem("st_full")
        st_taken = [sem(f"st_taken{i}") for i in range(STB)]
        pv_done = sem("pv_done")
        sumsT_ready = sem("sumsT_ready")
        recip_ready = sem("recip_ready")
        y_stats_ready = sem("y_stats_ready")
        y_mv_ready = sem("y_mv_ready")
        y_ln_ready = sem("y_ln_ready")
        y_seed_ready = sem("y_seed_ready")
        y_newton = sem("y_newton")
        x1_ready = sem("x1_ready")
        x1_saved = sem("x1_saved")
        route_v = sem("route_v")
        route_a = sem("route_a")
        route_p = sem("route_p")
        rows_max = sem("rows_max")
        wait_passed = sem("wait_passed")
        send_passed = sem("send_passed")
        choice_ready = sem("choice_ready")
        iotas_ready = sem("iotas_ready")
        x1_loaded = sem("x1_loaded")
        scattered = [sem(f"scattered{k}") for k in range(K)]
        rows_named = sem("rows_named")
        slots_ready = sem("slots_ready")
        tiles_ready = sem("tiles_ready")
        xg_loaded = [sem(f"xg_loaded{i}") for i in range(4)]
        xg_turned = sem("xg_turned")
        xgT_ready = sem("xgT_ready")
        g_full = sem("g_full")
        p_full = sem("p_full")
        relu_ready = sem("relu_ready")
        hid_ready = sem("hid_ready")
        hid_turned = sem("hid_turned")
        hidT_ready = sem("hidT_ready")
        yo_full = sem("yo_full")
        yo_ready = sem("yo_ready")
        yo_sent = [sem(f"yo_sent{i}") for i in range(2)]
        yt_loaded = [sem(f"yt_loaded{i}") for i in range(4)]
        comb_a = sem("comb_a")
        comb_b = sem("comb_b")
        comb_stats = sem("comb_stats")
        comb_mv = sem("comb_mv")
        comb_ln = sem("comb_ln")
        comb_seed = sem("comb_seed")
        comb_newton = sem("comb_newton")
        comb_ready = sem("comb_ready")
        stored = [sem(f"stored{i}") for i in range(4)]

        PARAMS = 11

        def half_of(b, half, first, last, do):
            nb, nh = (b, 1) if half == 0 else (b.after(1), 0)
            pb, ph = (b, 0) if half == 1 else (b.after(-1), 1)
            more = not (last and half == 1)
            done = not (first and half == 0)
            ends = done and half == 0
            for p in range(PAIRS):
                following = [(b, half, q) for q in range(p + 1, PAIRS)]
                if more:
                    following += [(nb, nh, q) for q in range(2)]
                following += [None, None]
                if p == 0:
                    if more and nh == 0:
                        do.take_x(nb)
                    if half == 1 and not first:
                        do.route_logits(b.after(-1))
                    if more:
                        do.project(nb, nh)
                if p == 1:
                    if more:
                        do.norm(nb, nh)
                    if done:
                        do.join(pb, ph)
                if p == 2:
                    if ends:
                        do.project_out(pb, 1)
                    if more:
                        do.turn(nb, nh, 0)
                if p == 3:
                    if more:
                        do.turn(nb, nh, 2)
                    if ends:
                        do.turn_x1(pb, 0)
                do.values(b, half, p, following[0], following[1])
                if p == 0:
                    if done:
                        do.heads(pb, ph, 1)
                    if more:
                        do.sums(nb, nh)
                if p == 1:
                    if ends:
                        do.project_out(pb, 0)
                    if more:
                        do.split(nb, nh)
                if p == 2:
                    if more:
                        do.turn(nb, nh, 1)
                    do.heads(b, half, 0)
                    if ends:
                        do.norm_x1(pb)
                if p == 3:
                    if more:
                        do.turn(nb, nh, 3)
                    if ends:
                        do.turn_x1(pb, 1)
                do.more_values(b, half, p, following[0])

        def attention(engine, do):
            first = Batch(0)
            do.take_x(first)
            do.project(first, 0)
            do.sums(first, 0)
            do.norm(first, 0)
            do.split(first, 0)
            for p in range(PAIRS):
                do.turn(first, 0, p)
            for p in range(2):
                do.maxima(first, 0, p)
            do.with_maxima(first, 0, 0)
            do.scores(first, 0, 0)
            half_of(first, 0, True, False, do)
            half_of(first, 1, True, False, do)
            if engine is None:
                for b in range(1, NB - 1):
                    half_of(Batch(b), 0, False, False, do)
                    half_of(Batch(b), 1, False, False, do)
            else:
                with engine.Fori(1, NB - 1) as at:
                    half_of(Batch(at, 2), 0, False, False, do)
                    half_of(Batch(at, 2), 1, False, False, do)
            last = Batch(NB - 1)
            half_of(last, 0, False, True, do)
            half_of(last, 1, False, True, do)
            do.heads(last, 1, 1)
            do.join(last, 1)
            for i in range(2):
                do.project_out(last, i)
            do.norm_x1(last)
            for c in range(EC):
                do.turn_x1(last, c)
            do.route_logits(last)

        def nothing(*_):
            pass

        class Steps:

            def __init__(self, take_x=nothing, project=nothing, sums=nothing, norm=nothing, split=nothing,
                         turn=nothing, maxima=nothing, with_maxima=nothing, scores=nothing, values=nothing,
                         more_values=nothing, heads=nothing, join=nothing, project_out=nothing, norm_x1=nothing,
                         turn_x1=nothing, route_logits=nothing):
                self.take_x = take_x
                self.project = project
                self.sums = sums
                self.norm = norm
                self.split = split
                self.turn = turn
                self.maxima = maxima
                self.with_maxima = with_maxima
                self.scores = scores
                self.values = values
                self.more_values = more_values
                self.heads = heads
                self.join = join
                self.project_out = project_out
                self.norm_x1 = norm_x1
                self.turn_x1 = turn_x1
                self.route_logits = route_logits

        prep_steps, out_steps = [], []

        def note_maxima(b, half, p):
            prep_steps.extend(("max", b.at, half, MAXB * p + i) for i in range(MAXB))

        def note_with_maxima(b, half, p):
            out_steps.append(("q", b.at, half, p))

        def note_values(b, half, p, ahead, beside):
            if beside:
                note_maxima(*beside)
            if ahead:
                note_with_maxima(*ahead)

        attention(None, Steps(
            take_x=lambda b: prep_steps.extend(("x", b.at, 0, c) for c in range(EC)),
            project=lambda b, half: prep_steps.extend(("project", b.at, half, t) for t in range(TT)),
            turn=lambda b, half, p: prep_steps.extend((kind, b.at, half, p) for kind in ("k", "q")),
            maxima=note_maxima, with_maxima=note_with_maxima, values=note_values,
            heads=lambda b, half, g: out_steps.append(("heads", b.at, half, g)),
            join=lambda b, half: out_steps.append(("join", b.at, half, 0)),
            project_out=lambda b, i: out_steps.append(("y", b.at, 1, i)),
            turn_x1=lambda b, c: out_steps.append(("x1", b.at, 1, c)),
            route_logits=lambda b: out_steps.append(("logits", b.at, 1, 0))))
        prep = Order(prep_steps, 2)
        outs = Order(out_steps, 1)

        def routed(i, k):
            return 1 + 7 * i + k

        MAX_REGIONS = [[(0, 3, 0)], [(1, 3, 0)], [(0, 2, 0), (0, 0, 384)], [(1, 2, 0), (1, 0, 384)],
                       [(0, 1, 0)], [(1, 1, 0)]]
        ST_REGIONS = [[(0, 0, 0)], [(1, 0, 0)], [(0, 1, 0), (0, 3, 384)], [(1, 1, 0), (1, 3, 384)],
                      [(0, 2, 0)], [(1, 2, 0)]]
        WIDTH = [512, 512, 512, 512, 256, 256]
        PLACE = {(h, j): (i, c) for i, regions in enumerate(ST_REGIONS) for h, j, c in regions}

        def out_done(engine, step, after=1):
            engine.wait_ge(out_taken, step[0] + after)

        def prep_done(engine, step):
            _, k, uses = step
            engine.wait_ge(prep_taken[k], uses + 1)

        def scale_shift(engine, s, gained, shifted, u):
            v = normed[:, :, s * P:(s + 1) * P].rearrange("p t (h d) -> p t h d", d=D)
            engine.tensor_tensor(v, v, gains[:, s:s + 1, :].unsqueeze(2).broadcast_to([P, TT, HH, D]),
                                 ALU.mult).then_inc(gained, 1)
            engine.wait_ge(gained, u + 1)
            engine.tensor_tensor(v, v, shifts[:, s:s + 1, :].unsqueeze(2).broadcast_to([P, TT, HH, D]),
                                 ALU.add).then_inc(shifted, 1)

        block = ctx.enter_context(nc.Block())

        @block.sync
        def _(sp):
            for i, w in enumerate((Wq, Wk, Wv, Wo)):
                sp.dma_start(w_rows[:, i, :, :], w.rearrange("(c p) e -> p c e", p=P)).then_inc(inputs_loaded, 16)
            sp.dma_start(x_in[:, :, :], x_tiles[0]).then_inc(x_loaded, 16)
            sp.dma_start(rw_rows[:, :], router_w).then_inc(inputs_loaded, 16)
            rows = ((gains[:, 0, :], qln_g), (gains[:, 1, :], kln_g), (shifts[:, 0, :], qln_b),
                    (shifts[:, 1, :], kln_b), (bo_row[:, :], bo), (rb_row[:, :], router_b))
            for to, row in rows:
                sp.dma_start(to, row.partition_broadcast(P)).then_inc(inputs_loaded, 16)
            sp.dma_start(temp_col[:, :], temperature.partition_broadcast(P)).then_inc(inputs_loaded, 16)
            sp.dma_start(x_res[:, :, :], x_tiles[0]).then_inc(res_loaded, 16)
            for i in range(2):
                sp.wait_ge(slots_imaged, i + 2)
                sp.dma_start(xs_dram.rearrange("(i t p) w -> i p t w", i=2, p=P)[i], empty_slots).then_inc(
                    slots_emptied, 16)

            def batch_io(b, more=True):
                if more:
                    sp.wait_ge(prep_full, prep("x", b, 0, EC - 1)[0] + 1)
                    sp.dma_start(x_in[:, :, :], x_tiles[bass.ds(b.at + 1, 1)].rearrange(
                        "o p t e -> (o p) t e")).then_inc(x_loaded, 16)
                    out_done(sp, outs("y", b, 1, 1))
                    sp.dma_start(x_res[:, :, :], x_tiles[bass.ds(b.at + 1, 1)].rearrange(
                        "o p t e -> (o p) t e")).then_inc(res_loaded, 16)
                sp.wait_ge(x1_ready, TT * (b.at + 1))
                sp.dma_start(x1_dram[bass.ds(b.at, 1)].rearrange("o p t e -> (o p) t e"), x1).then_inc(
                    x1_saved, 16)

            batch_io(Batch(0))
            with sp.Fori(1, NB - 1) as at:
                batch_io(Batch(at, 2))
            batch_io(Batch(NB - 1), False)

            sp.wait_ge(slots_emptied, 32)
            sp.wait_ge(x1_saved, 16 * NB)
            sp.wait_ge(out_taken, len(out_steps))
            for to, w, c in ((wg_sb, wg, EC), (wp_sb, wp, EC), (wo_sb, wo, FC)):
                for e in range(E):
                    sp.dma_start(to[:, e, :].rearrange("p (c n) -> p c n", c=c),
                                 w[e].rearrange("(c p) n -> p c n", p=P)).then_inc(experts_loaded, 16)
            for b in range(NB):
                sp.dma_start(x1_all[:, b * TT:(b + 1) * TT, 0:EMB], x1_dram[b]).then_inc(x1_loaded, 16)

            for k in range(K):
                sp.wait_ge(scattered[k], 16 * NT)

            def load_slots(i, k):
                t = 4 * i + k
                sp.dma_start(xg[k][:, :], xs_dram[bass.ds(t * P, P), :]).then_inc(xg_loaded[k], 16)

            for k in range(4):
                load_slots(0, k)
            with sp.Fori(1, SLOT_TILES // 4) as i:
                for k in range(4):
                    sp.wait_ge(yo_ready, 2 * (4 * (i - 1) + k + 1))
                    load_slots(i, k)

            for par in range(2):
                sp.wait_ge(yo_sent[par], 16 * (SLOT_TILES // 2))
            y_rows = ys_dram[0:NB * T * K, :].rearrange("(t p k) e -> t p k e", p=P, k=K)

            def load_two(g, j):
                sp.dma_start(y_two[j][:, :, :], y_rows[bass.ds(4 * g + j, 1)].rearrange(
                    "o p k e -> (o p) k e")).then_inc(yt_loaded[j], 16)

            def store(g, j):
                sp.wait_ge(comb_ready, 4 * g + j + 1)
                sp.dma_start(out_tiles[bass.ds(4 * g + j, 1)].rearrange("o p e -> (o p) e"),
                             acc[j][:, :]).then_inc(stored[j], 16)

            for j in range(4):
                load_two(0, j)
            with sp.Fori(0, NT // 4 - 1) as g:
                for j in range(4):
                    sp.wait_ge(comb_b, 4 * g + j + 1)
                    load_two(g + 1, j)
                for j in range(4):
                    store(g, j)
            for j in range(4):
                store(NT // 4 - 1, j)
            for j in range(4):
                sp.wait_ge(stored[j], 16 * (NT // 4))

        @block.gpsimd
        def _(pool):
            pool.memset(ident[:, :], 0.0).then_inc(consts_ready, 1)
            pool.memset(ones[:, :], 1.0).then_inc(consts_ready, 1)
            pool.memset(ones_b[:, :], 1.0).then_inc(consts_ready, 1)
            pool.memset(mask_ij[:, :], 0.0).then_inc(consts_ready, 1)
            pool.memset(mask_ji[:, :], 0.0).then_inc(consts_ready, 1)
            pool.memset(eps_col[:, :], EPS).then_inc(consts_ready, 1)
            pool.memset(eps4_col[:, :], EPS / 4).then_inc(consts_ready, 1)
            pool.wait_ge(consts_ready, 7)
            pool.affine_select(out=ident[:, :], in_=ident[:, :], compare_op=ALU.not_equal, fill=1.0, base=0,
                               pattern=[[-1, P]], channel_multiplier=1).then_inc(consts_ready, 1)
            pool.affine_select(out=mask_ij[:, :], in_=mask_ij[:, :], compare_op=ALU.is_ge, fill=MASKED, base=0,
                               pattern=[[-1, P]], channel_multiplier=1).then_inc(consts_ready, 1)
            pool.affine_select(out=mask_ji[:, :], in_=mask_ji[:, :], compare_op=ALU.is_ge, fill=MASKED, base=0,
                               pattern=[[1, P]], channel_multiplier=-1).then_inc(consts_ready, 1)
            pool.affine_select(out=before_b[:, :], in_=ones_b[:, :], compare_op=ALU.is_gt, fill=0.0, base=0,
                               pattern=[[1, P]], channel_multiplier=-1).then_inc(consts_ready, 1)
            pool.wait_ge(consts_ready, 8)
            pool.tensor_copy(ident_b[:, :], ident[:, :]).then_inc(consts_ready, 1)
            for i in range(2):
                pool.memset(stack[i][:, :, :, :, 32:48].bitcast(F32), 0.0).then_inc(consts_ready, 1)
                pool.memset(v_aug[i][:, :, :, D:VW], 0.0).then_inc(consts_ready, 1)
            pool.wait_ge(consts_ready, 16)
            for i in range(2):
                pool.memset(stack[i][:, :, 1, :, 32:34].bitcast(F32), 1.0).then_inc(consts_ready, 1)
                pool.memset(v_aug[i][:, :, :, D:D + 1], 1.0).then_inc(consts_ready, 1)

            def project(b, half):
                u = 2 * b.at + half
                pool.wait_ge(raw_ready, TT * (u + 1))
                at_least(pool, low_ready, 2 * u)
                pool.tensor_tensor(squares[:, :, :], raw[:, :, :], raw[:, :, :], ALU.mult).then_inc(squares_ready, 1)
                pool.memset(stack[half][:, :, 0, :, 32:34].bitcast(F32), 0.0).then_inc(max_cleared, 1)

            def norm(b, half):
                u = 2 * b.at + half
                pool.wait_ge(normed_ready, u + 1)
                scale_shift(pool, 0, gained_q, shifted_q, u)

            def join(b, half):
                if half == 1:
                    pool.wait_ge(res_loaded, 16 * (b.at + 1))
                    pool.tensor_tensor(x_res, x_res, bo_row[:, :].unsqueeze(1).broadcast_to([P, TT, EMB]),
                                       ALU.add).then_inc(res_ready, 1)

            pool.wait_ge(w_ready, 3)
            pool.memset(empty_slots, 0.0).then_inc(slots_imaged, 1)
            pool.wait_ge(slots_imaged, 1)
            for i in range(2):
                if i > 0:
                    pool.wait_ge(slots_emptied, 16)
                pool.iota(empty_slots[:, :, EMB:EMB + 1].bitcast(I32), [[P, SLOT_TILES // 2], [1, 1]],
                          base=NB * T * K + i * SLOTS // 2, channel_multiplier=1).then_inc(slots_imaged, 1)
            attention(pool, Steps(project=project, norm=norm, join=join))

            pool.wait_ge(out_taken, len(out_steps))
            pool.wait_ge(x1_saved, 16 * NB)
            pool.iota(expert_iota[:, :], [[1, E]], base=0, channel_multiplier=0,
                      allow_small_or_imprecise_dtypes=True).then_inc(iotas_ready, 1)
            pool.iota(tile_iota[:, :], [[1, SLOT_TILES]], base=0, channel_multiplier=0,
                      allow_small_or_imprecise_dtypes=True).then_inc(iotas_ready, 1)
            pool.iota(result_row[:, :].bitcast(I32), [[K * P, NT]], base=0, channel_multiplier=K).then_inc(
                iotas_ready, 1)
            pool.wait_ge(slots_emptied, 32)
            pool.wait_ge(x1_loaded, 16 * NB)
            for k in range(K):
                pool.wait_ge(rows_named, k + 1)
                if k == 0:
                    pool.wait_ge(slots_ready, 1)
                for t in range(NT):
                    pool.indirect_dma_start(xs_dram, bass.IndirectOffsetOnAxis(slot_u[:, k, t % TT * NB + t // TT:t % TT * NB + t // TT + 1], 0),
                                            x1_all[:, t, :], None).then_inc(scattered[k], 16)

            with pool.Fori(0, SLOT_TILES // 2) as i:
                for par in range(2):
                    pool.wait_ge(yo_ready, 2 * (2 * i + par + 1))
                    pool.sem_inc(send_passed, 1)
                    pool.indirect_dma_start(ys_dram, bass.IndirectOffsetOnAxis(y_at[par][:, 0:1], 0),
                                            y_out[par][:, :], None).then_inc(yo_sent[par], 16)

        @block.scalar
        def _(act):
            act.preload_act_table_set("natural_log_exp_and_others")

            def take_x(b):
                for c in range(EC):
                    n, k, _ = prep("x", b, 0, c)
                    act.wait_ge(prep_full, n + 1)
                    act.copy(xT[:, c, :], prep_bank[k][:, :]).then_inc(prep_taken[k], 1)

            def project(b, half):
                u = 2 * b.at + half
                at_least(act, normed_ready, u)
                for t in range(TT):
                    n, k, _ = prep("project", b, half, t)
                    act.wait_ge(prep_full, n + 1)
                    act.copy(raw[:, t, :], prep_bank[k][:, 0:2 * P]).then_inc(raw_ready, 1)
                    act.copy(v_aug[half][:, t, :, 0:D],
                             prep_bank[k][:, 2 * P:3 * P].rearrange("p (h d) -> p h d", d=D)).then_inc(
                        prep_taken[k], 1)

            def sums(b, half):
                u = 2 * b.at + half
                act.wait_ge(ssum_ready, u + 1)
                act.activation(nt[0][:, :, :], ssum[:, :, :], ACT.Ln, bias=eps_col[:, :],
                               scale=1.0 / D).then_inc(ln_ready, 1)
                act.wait_ge(ln_ready, u + 1)
                act.activation(nt[1][:, :, :], nt[0][:, :, :], ACT.Exp, scale=-0.5).then_inc(seed_ready, 1)

            def split(b, half):
                act.wait_ge(high_ready, 2 * b.at + half + 1)
                act.copy(stack[half][:, :, 0, :, 48:64], stack[half][:, :, 0, :, 0:D].bitcast(F32)).then_inc(
                    again_ready, 1)
                act.copy(stack[half][:, :, 1, :, 16:32], stack[half][:, :, 1, :, 0:D].bitcast(F32)).then_inc(
                    again_ready, 1)

            def turn(b, half, p):
                n, k, _ = prep("k", b, half, p)
                act.wait_ge(prep_full, n + 1)
                act.copy(kT[half][:, p, :], prep_bank[k][:, :]).then_inc(prep_taken[k], 1)

            def with_maxima(b, half, p):
                act.wait_ge(out_full, outs("q", b, half, p)[0] + 1)
                act.copy(qT[half][:, p, :], out_bank[:, :]).then_inc(out_taken, 1)

            def weigh(b, half, p, pieces):
                u = 2 * b.at + half
                if 0 in pieces:
                    at_least(act, pv_done, PAIRS * u + p - 1)
                for i in pieces:
                    act.wait_ge(st_full, PIECES * (PAIRS * u + p) + i + 1)
                    act.activation(probsT[p % 2][:, i, 0:WIDTH[i]], st_bank[i % STB][:, 0:WIDTH[i]],
                                   ACT.Exp).then_inc(st_taken[i % STB], 1)

            def scores(b, half, p):
                weigh(b, half, p, range(PIECES))

            def values(b, half, p, ahead, beside):
                if ahead:
                    with_maxima(*ahead)
                    weigh(*ahead, range(PIECES // 2))

            def more_values(b, half, p, ahead):
                if ahead:
                    weigh(*ahead, range(PIECES // 2, PIECES))
                if p % 2 == 1:
                    act.wait_ge(pv_done, PAIRS * (2 * b.at + half) + p + 1)
                    act.copy(sumsT[:, :], pv_bank[p // 2][:, :]).then_inc(sumsT_ready, 1)

            def join(b, half):
                act.wait_ge(out_full, outs("join", b, half, 0)[0] + 1)
                act.copy(headsT[:, half, :], out_bank[:, :]).then_inc(out_taken, 1)

            def norm_x1(b):
                act.wait_ge(y_mv_ready, TT * (b.at + 1))
                act.activation(yn[0][:, :], y_mv[:, :, 1], ACT.Ln, bias=eps_col[:, :]).then_inc(y_ln_ready, 1)
                act.wait_ge(y_ln_ready, b.at + 1)
                act.activation(yn[1][:, :], yn[0][:, :], ACT.Exp, scale=-0.5).then_inc(y_seed_ready, 1)

            def turn_x1(b, c):
                act.wait_ge(out_full, outs("x1", b, 1, c)[0] + 1)
                act.copy(x1T[:, c, :], out_bank[:, :]).then_inc(out_taken, 1)

            act.wait_ge(consts_ready, 20)
            attention(act, Steps(take_x=take_x, project=project, sums=sums, split=split, turn=turn,
                                 with_maxima=with_maxima, scores=scores, values=values,
                                 more_values=more_values, join=join, norm_x1=norm_x1, turn_x1=turn_x1))

            for i in range(ITERS):
                act.wait_ge(route_v, routed(i, 1))
                act.activation(exps[:, :, :], logits[:, :, :, :].rearrange("p t b e -> p (t b) e"),
                               ACT.Exp).then_inc(route_a, 1)
                act.wait_ge(route_v, routed(i, 2))
                act.activation(row_b[:, :], row_a[:, :], ACT.Ln).then_inc(route_a, 1)
                act.wait_ge(route_v, routed(i, 4))
                act.activation(col_exps[:, :], other_bank[0][0:NB * E, :], ACT.Exp, bias=col_nmax[:, :],
                               accum_out=col_sum[:, :]).then_inc(route_a, 1)
                act.wait_ge(route_a, 4 * i + 3)
                act.activation(col_ln[:, :], col_sum[:, :], ACT.Ln).then_inc(route_a, 1)
            act.wait_ge(route_v, routed(ITERS, 0))
            act.activation(gates[:, :, :], logits[:, :, :, :].rearrange("p t b e -> p (t b) e"),
                           ACT.Exp).then_inc(route_a, 1)

            def turned(t, par):
                act.wait_ge(xg_turned, t + 1)
                act.copy(xgT[par][:, :, :], x_bank[:, 0:EMB].rearrange("p (c n) -> p c n", c=EC)).then_inc(
                    xgT_ready, 1)

            def gate(t, par):
                act.wait_ge(g_full, t + 1)
                act.activation(gate_act[par][:, :], g_bank[:, :], ACT.Relu).then_inc(relu_ready, 1)

            def hidden(t, par):
                act.wait_ge(hid_turned, t + 1)
                act.copy(hidT[par][:, :, :], h_bank[:, :].rearrange("p (c n) -> p c n", c=FC)).then_inc(
                    hidT_ready, 1)

            turned(0, 0)
            gate(0, 0)
            turned(1, 1)
            with act.Fori(0, SLOT_TILES // 2 - 1) as i:
                for par in range(2):
                    t = 2 * i + par
                    hidden(t, par)
                    gate(t + 1, 1 - par)
                    turned(t + 2, par)
            hidden(SLOT_TILES - 2, 0)
            gate(SLOT_TILES - 1, 1)
            hidden(SLOT_TILES - 1, 1)

            with act.Fori(0, NT // 4) as g:
                act.wait_ge(comb_mv, 4 * (g + 1))
                act.activation(zn[0][:, :], z_mv[:, :, 1], ACT.Ln, bias=eps4_col[:, :]).then_inc(comb_ln, 1)
                act.wait_ge(comb_ln, g + 1)
                act.activation(zn[1][:, :], zn[0][:, :], ACT.Exp, scale=-0.5).then_inc(comb_seed, 1)

        @block.vector
        def _(dve):
            def rsqrt_newton(seed, half_v, t2, t3, to, var, scale, chain, count, ready, at, eps=EPS):
                dve.tensor_scalar(half_v, var, -0.5 * scale, -0.5 * eps, ALU.mult, ALU.add).then_inc(chain, 1)
                dve.wait_ge(ready, at)
                dve.wait_ge(chain, count + 1)
                dve.tensor_tensor(t2, half_v, seed, ALU.mult).then_inc(chain, 1)
                dve.wait_ge(chain, count + 2)
                dve.tensor_tensor(t3, t2, seed, ALU.mult).then_inc(chain, 1)
                dve.wait_ge(chain, count + 3)
                dve.scalar_tensor_tensor(out=to, in0=t3, scalar=1.5, in1=seed, op0=ALU.add,
                                         op1=ALU.mult).then_inc(chain, 1)
                dve.wait_ge(chain, count + 4)

            dve.wait_ge(inputs_loaded, 16 * 12)
            dve.tensor_scalar(gains[:, :, :], gains[:, :, :], QK_SCALE, None, ALU.mult).then_inc(w_ready, 1)
            dve.tensor_scalar(shifts[:, :, :], shifts[:, :, :], QK_SCALE, None, ALU.mult).then_inc(w_ready, 1)
            dve.tensor_scalar(inv_temp[:, :], temp_col[:, :], 0.1, None, ALU.max).then_inc(w_ready, 1)
            dve.wait_ge(w_ready, 3)
            dve.reciprocal(inv_temp[:, :], inv_temp[:, :]).then_inc(w_ready, 1)
            for i in range(4):
                dve.wait_ge(w_turned, i + 1)
                for c in range(EC):
                    src = other_bank[i][:, c * EMB:(c + 1) * EMB]
                    if i < 3:
                        dve.tensor_copy(w_qkvT[:, c, :, i, :], src.rearrange("p (h n) -> p h n", h=2)).then_inc(
                            w_copied, 1)
                    else:
                        dve.tensor_copy(w_oT[:, c, :], src).then_inc(w_copied, 1)
            dve.wait_ge(w_turned, 5)
            dve.tensor_copy(rwT[:, :, :], out_bank[:, 0:EC * E].rearrange("p (c e) -> p c e", c=EC)).then_inc(
                w_copied, 1)
            dve.wait_ge(w_copied, 9)
            for i in range(2):
                for c in range(EC):
                    dve.tensor_reduce(w_mean[:, i, c, :], w_qkvT[:, c, :, i, :].rearrange(
                        "p h (g d) -> p h g d", d=D), AX, ALU.add).then_inc(w_mean_done, 1)
            dve.wait_ge(w_mean_done, 4)
            for i in range(2):
                for c in range(EC):
                    for h in range(2):
                        v = w_qkvT[:, c, h, i, :].rearrange("p (g d) -> p g d", d=D)
                        m = w_mean[:, i, c, h * HH:(h + 1) * HH].unsqueeze(2).broadcast_to([P, HH, D])
                        dve.scalar_tensor_tensor(out=v, in0=m, scalar=-1.0 / D, in1=v, op0=ALU.mult,
                                                 op1=ALU.add).then_inc(w_ready, 1)

            def sums(b, half):
                u = 2 * b.at + half
                dve.wait_ge(squares_ready, u + 1)
                dve.tensor_reduce(ssum[:, :, :], squares[:, :, :].rearrange("p t (h d) -> p t h d", d=D), AX,
                                  ALU.add).then_inc(ssum_ready, 1)

            def norm(b, half):
                u = 2 * b.at + half
                dve.wait_ge(ssum_ready, u + 1)
                rsqrt_newton(nt[1][:, :, :], nt[2][:, :, :], nt[3][:, :, :], nt[4][:, :, :], rstd[:, :, :],
                             ssum[:, :, :], 1.0 / D, newton, 4 * u, seed_ready, u + 1)
                dve.tensor_tensor(normed[:, :, :].rearrange("p t (h d) -> p t h d", d=D),
                                  raw[:, :, :].rearrange("p t (h d) -> p t h d", d=D),
                                  rstd[:, :, :].unsqueeze(3).broadcast_to([P, TT, 2 * HH, D]),
                                  ALU.mult).then_inc(normed_ready, 1)
                dve.wait_ge(normed_ready, u + 1)
                scale_shift(dve, 1, gained_k, shifted_k, u)

            def split(b, half):
                u = 2 * b.at + half
                st = stack[half]
                n5 = normed[:, :, :].rearrange("p t (h d) -> p (t h) d", d=D)
                s5 = st[:, :, :, :, :].rearrange("p t s h w -> p (t s h) w")
                dve.wait_ge(shifted_k, u + 1)
                dve.wait_ge(shifted_q, u + 1)
                dve.tensor_copy(s5[:, :, 0:D], n5).then_inc(high_ready, 1)
                dve.wait_ge(high_ready, u + 1)
                for s, at in ((0, 16), (1, 48)):
                    nrm = normed[:, :, s * P:(s + 1) * P].rearrange("p t (h d) -> p t h d", d=D)
                    dve.tensor_tensor(st[:, :, s, :, at:at + D], nrm, st[:, :, s, :, 0:D].bitcast(F32),
                                      ALU.subtract).then_inc(low_ready, 1)

            def turn(b, half, p):
                n, k, _ = prep("q", b, half, p)
                dve.wait_ge(prep_full, n + 1)
                dve.tensor_copy(qT[half][:, p, :], prep_bank[k][:, :]).then_inc(prep_taken[k], 1)

            def maxima(b, half, p):
                u = 2 * b.at + half
                h0 = 2 * p
                for i, regions in enumerate(MAX_REGIONS):
                    n, k, _ = prep("max", b, half, MAXB * p + i)
                    dve.wait_ge(prep_full, n + 1)
                    s = prep_bank[k]
                    for h, t, c in regions:
                        last = dve.tensor_reduce(neg_max[:, t, h0 + h:h0 + h + 1], s[:, c:c + (t + 1) * P], AX,
                                                 ALU.max, negate=True)
                    last.then_inc(prep_taken[k], 1)
                prep_done(dve, prep("max", b, half, MAXB * p + MAXB - 1))
                m = neg_max[:, :, h0:h0 + 2]
                high = stack[half][:, :, 0, h0:h0 + 2, 32]
                dve.tensor_copy(high, m).then_inc(max_high, 1)
                dve.wait_ge(max_high, PAIRS * u + p + 1)
                dve.tensor_tensor(stack[half][:, :, 0, h0:h0 + 2, 33], m, high.bitcast(F32),
                                  ALU.subtract).then_inc(max_ready, 1)

            def values(b, half, p, ahead, beside):
                if beside:
                    maxima(*beside)

            def heads_of(b, half, g):
                dve.wait_ge(out_full, outs("heads", b, half, g)[0] + 1)
                o = out_bank[:, :].rearrange("p (t h d) -> p t h d", t=TT, h=4)
                dve.reciprocal(recip[:, :, :], o[:, :, :, D]).then_inc(recip_ready, 1)
                dve.wait_ge(recip_ready, 2 * (2 * b.at + half) + g + 1)
                dve.tensor_tensor(heads[:, :, g * 4 * D:(g + 1) * 4 * D].rearrange("p t (h d) -> p t h d", h=4),
                                  o[:, :, :, 0:D], recip[:, :, :].unsqueeze(3).broadcast_to([P, TT, 4, D]),
                                  ALU.mult).then_inc(out_taken, 1)

            def project_out(b, i):
                if i == 0:
                    dve.wait_ge(res_ready, b.at + 1)
                dve.wait_ge(out_full, outs("y", b, 1, i)[0] + 1)
                dve.tensor_tensor(y[:, 2 * i:2 * i + 2, :], out_bank[:, :].rearrange("p (t e) -> p t e", t=2),
                                  x_res[:, 2 * i:2 * i + 2, :], ALU.add).then_inc(out_taken, 1)
                out_done(dve, outs("y", b, 1, i))
                for t in (2 * i, 2 * i + 1):
                    dve.bn_stats(y_stats[:, t, :], y[:, t, :]).then_inc(y_stats_ready, 1)
                if i == 0:
                    return
                dve.wait_ge(y_stats_ready, TT * (b.at + 1))
                dve.sem_inc(wait_passed, 1)
                for t in range(TT):
                    dve.bn_aggr(y_mv[:, t, :], y_stats[:, t, :]).then_inc(y_mv_ready, 1)

            def norm_x1(b):
                dve.wait_ge(y_mv_ready, TT * (b.at + 1))
                rsqrt_newton(yn[1][:, :], yn[2][:, :], yn[3][:, :], yn[4][:, :], y_rstd[:, :], y_mv[:, :, 1], 1.0,
                             y_newton, 4 * b.at, y_seed_ready, b.at + 1)
                at_least(dve, x1_saved, 16 * b.at)
                for t in range(TT):
                    dve.tensor_scalar(x1[:, t, :], y[:, t, :], y_mv[:, t, 0:1], y_rstd[:, t:t + 1], ALU.subtract,
                                      ALU.mult).then_inc(x1_ready, 1)

            def route_logits(b):
                dve.wait_ge(out_full, outs("logits", b, 1, 0)[0] + 1)
                dve.tensor_tensor(logits[:, :, bass.ds(b.at, 1), :].rearrange("p t o e -> p (t o) e"),
                                  out_bank[:, 0:TT * E].rearrange("p (t e) -> p t e", e=E),
                                  rb_row[:, :].unsqueeze(1).broadcast_to([P, TT, E]), ALU.add).then_inc(
                    out_taken, 1)

            attention(dve, Steps(sums=sums, norm=norm, split=split, turn=turn, maxima=maxima, values=values,
                                 heads=heads_of, project_out=project_out, norm_x1=norm_x1,
                                 route_logits=route_logits))

            lg = logits[:, :, :, :].rearrange("p t b e -> p (t b) e")
            dve.wait_ge(out_taken, len(out_steps))
            dve.tensor_scalar(lg, lg, inv_temp[:, 0:1], None, ALU.mult).then_inc(route_v, 1)
            for i in range(ITERS):
                dve.wait_ge(route_v, routed(i, 0))
                dve.tensor_reduce(row_a[:, :], lg, AX, ALU.max).then_inc(rows_max, 1)
                dve.wait_ge(rows_max, i + 1)
                dve.tensor_tensor(lg, lg, row_a[:, :].unsqueeze(2).broadcast_to([P, NT, E]), ALU.subtract).then_inc(
                    route_v, 1)
                dve.wait_ge(route_a, 4 * i + 1)
                dve.tensor_reduce(row_a[:, :], exps[:, :, :], AX, ALU.add).then_inc(route_v, 1)
                dve.wait_ge(route_a, 4 * i + 2)
                dve.tensor_tensor(lg, lg, row_b[:, :].unsqueeze(2).broadcast_to([P, NT, E]), ALU.subtract).then_inc(
                    route_v, 1)
                dve.wait_ge(route_p, 2 * i + 1)
                dve.tensor_reduce(col_nmax[:, :], other_bank[0][0:NB * E, :], AX, ALU.max, negate=True).then_inc(
                    route_v, 1)
                dve.wait_ge(route_a, 4 * i + 4)
                dve.tensor_tensor(col_lse[:, :], col_ln[:, :], col_nmax[:, :], ALU.subtract).then_inc(route_v, 1)
                dve.wait_ge(route_v, routed(i, 5))
                dve.tensor_scalar(col_diag[:, :], ident[0:NB * E, 0:NB * E], col_lse[:, 0:1], None,
                                  ALU.mult).then_inc(route_v, 1)
                dve.wait_ge(route_p, 2 * i + 2)
                cols = other_bank[1][:, 0:NB * E].rearrange("p (b e) -> p b e", b=NB).unsqueeze(1).broadcast_to(
                    [P, TT, NB, E])
                dve.tensor_tensor(logits[:, :, :, :], logits[:, :, :, :], cols, ALU.subtract).then_inc(route_v, 1)
            done = routed(ITERS, 0)
            dve.wait_ge(route_a, 4 * ITERS + 1)
            link = Chain(dve, route_v, done)
            link(dve.tensor_reduce(row_a[:, :], gates[:, :, :], AX, ALU.add))
            link(dve.tensor_scalar(row_a[:, :], row_a[:, :], 1e-8, None, ALU.add))
            link(dve.reciprocal(row_b[:, :], row_a[:, :]))
            link(dve.tensor_tensor(gates[:, :, :], gates[:, :, :], row_b[:, :].unsqueeze(2).broadcast_to([P, NT, E]),
                                   ALU.mult))
            for t in range(NT):
                last = dve.max(best[:, t, :], gates[:, t, :])
            link(last)
            for t in range(NT):
                last = dve.max_index(best_at[:, t, :], best[:, t, :], gates[:, t, :])
            link(last)
            link(dve.tensor_copy(best_atf[:, :, :], best_at[:, :, 0:K]))
            dve.wait_ge(iotas_ready, 3)
            for k in range(K):
                link(dve.tensor_tensor(chosen[k][:, :, :], best_atf[:, :, k:k + 1].broadcast_to([P, NT, E]),
                                       expert_iota[:, :].unsqueeze(1).broadcast_to([P, NT, E]), ALU.is_equal))
            dve.tensor_tensor(chosen_b[:, :, :], chosen[0][:, :, :], chosen[1][:, :, :], ALU.add).then_inc(choice_ready, 1)
            dve.wait_ge(route_p, 2 * ITERS + 1)
            link(dve.tensor_copy(counts[:, :, :], other_bank[3][:, 0:NT * E].rearrange("p (t e) -> p t e", e=E)))
            src, step, n = counts, 1, 0
            while step < NT:
                dst = scan[n % 2]
                link(dve.tensor_copy(dst[:, 0:step, :], src[:, 0:step, :]))
                link(dve.tensor_tensor(dst[:, step:, :], src[:, step:, :], src[:, 0:NT - step, :], ALU.add))
                src, step, n = dst, 2 * step, n + 1
            upto, other = src, scan[n % 2]
            link(dve.tensor_scalar(n_tiles_i[:, :], upto[:, NT - 1, :], float(P - 1), None, ALU.add))
            link(dve.tensor_scalar(n_tiles_j[:, :], n_tiles_i[:, :], 7, None, ALU.arith_shift_right))
            link(dve.tensor_copy(n_tiles[:, :], n_tiles_j[:, :]))
            src_e, step, n = n_tiles, 1, 0
            while step < E:
                dst = escan[n % 2]
                link(dve.tensor_copy(dst[:, 0:step], src_e[:, 0:step]))
                link(dve.tensor_tensor(dst[:, step:], src_e[:, step:], src_e[:, 0:E - step], ALU.add))
                src_e, step, n = dst, 2 * step, n + 1
            link(dve.tensor_tensor(first_slot[:, :], src_e[:, :], n_tiles[:, :], ALU.subtract))
            link(dve.tensor_scalar(first_slot[:, :], first_slot[:, :], float(P), None, ALU.mult))
            link(dve.tensor_tensor(past[:, :, :], src_e[0:1, :].unsqueeze(1).broadcast_to([1, SLOT_TILES, E]),
                                   tile_iota[:, :].unsqueeze(2).broadcast_to([1, SLOT_TILES, E]), ALU.is_le))
            link(dve.tensor_reduce(tile_ef[:, :], past[:, :, :], AX, ALU.add))
            dve.tensor_scalar(tile_e[:, :], tile_ef[:, :], float(E - 1), None, ALU.min).then_inc(tiles_ready, 1)
            link(dve.tensor_tensor(other[:, :, :], upto[:, :, :], counts[:, :, :], ALU.subtract))
            link(dve.tensor_tensor(other[:, :, :], other[:, :, :],
                                   other_bank[2][:, 0:NT * E].rearrange("p (t e) -> p t e", e=E), ALU.add))
            link(dve.tensor_tensor(slot_all[:, :, :], other[:, :, :],
                                   first_slot[:, :].unsqueeze(1).broadcast_to([P, NT, E]), ALU.add))
            for k in range(K):
                link(dve.tensor_tensor(slot_of[k][:, :, :], slot_all[:, :, :], chosen[k][:, :, :], ALU.mult))
                link(dve.tensor_reduce(slot_f[:, k, :], slot_of[k][:, :, :], AX, ALU.add))
            dve.tensor_copy(slot_u[:, :, :], slot_f[:, :, :]).then_inc(slots_ready, 1)
            dve.wait_ge(x1_loaded, 16 * NB)
            dve.tensor_copy(x1_all[:, :, EMB].bitcast(U32), result_row[:, :]).then_inc(rows_named, 1)
            link(dve.tensor_tensor(top_sum[:, :], best[:, :, 0], best[:, :, 1], ALU.add))
            link(dve.tensor_scalar(top_sum[:, :], top_sum[:, :], 1e-8, None, ALU.add))
            link(dve.reciprocal(top_sum[:, :], top_sum[:, :]))
            link(dve.tensor_scalar(top_sum[:, :], top_sum[:, :], 0.5, None, ALU.mult))
            link(dve.tensor_tensor(top_gate[:, :, :].rearrange("p (b t) k -> p t b k", b=NB),
                                   best[:, :, 0:K].rearrange("p (t b) k -> p t b k", b=NB),
                                   top_sum[:, :].rearrange("p (t b) -> p t b", b=NB).unsqueeze(3).broadcast_to(
                                       [P, TT, NB, K]), ALU.mult))
            dve.wait_ge(scattered[0], 16 * NT)
            dve.tensor_scalar(x1_all[:, :, EMB].bitcast(U32), result_row[:, :], 1.0, None, ALU.add).then_inc(
                rows_named, 1)

            def hidden(t, par):
                dve.wait_ge(relu_ready, t + 1)
                dve.wait_ge(p_full, t + 1)
                dve.tensor_tensor(hid[par][:, :], gate_act[par][:, :], p_bank[:, :], ALU.mult).then_inc(hid_ready, 1)

            def result(i, k):
                t, par = 4 * i + k, k % 2
                dve.wait_ge(yo_full, t + 1)
                at_least(dve, yo_sent[par], 16 * (2 * i + k // 2))
                dve.tensor_copy(y_out[par][:, :], y_bank[:, 0:EMB]).then_inc(yo_ready, 1)
                dve.tensor_copy(y_at[par][:, :], xg[k][:, EMB:EMB + 1].bitcast(U32)).then_inc(yo_ready, 1)

            def four_tiles(i, last=False):
                for k in range(4):
                    if not (last and k == 3):
                        hidden(4 * i + k + 1, (k + 1) % 2)
                    result(i, k)

            hidden(0, 0)
            four_tiles(0)
            with dve.Fori(1, SLOT_TILES // 4 - 1) as i:
                four_tiles(i)
            four_tiles(SLOT_TILES // 4 - 1, True)

            def four(g, first):
                for j in range(4):
                    dve.wait_ge(yt_loaded[j], 16 * (g + 1))
                    if not first:
                        dve.wait_ge(stored[j], 16 * g)
                    dve.scalar_tensor_tensor(out=acc[j][:, :], in0=y_two[j][:, 0, :],
                                             scalar=top_gate[:, bass.ds(4 * g + j, 1), 0],
                                             in1=x1_all[:, bass.ds(4 * g + j, 1), 0:EMB].rearrange(
                                                 "p o e -> p (o e)"), op0=ALU.mult, op1=ALU.add).then_inc(comb_a, 1)
                for j in range(4):
                    dve.wait_ge(comb_a, 4 * g + j + 1)
                    dve.scalar_tensor_tensor(out=acc[j][:, :], in0=y_two[j][:, 1, :],
                                             scalar=top_gate[:, bass.ds(4 * g + j, 1), 1], in1=acc[j][:, :],
                                             op0=ALU.mult, op1=ALU.add).then_inc(comb_b, 1)
                for j in range(4):
                    dve.wait_ge(comb_b, 4 * g + j + 1)
                    dve.bn_stats(z_stats[:, j, :], acc[j][:, :]).then_inc(comb_stats, 1)
                dve.wait_ge(comb_stats, 4 * (g + 1))
                dve.sem_inc(wait_passed, 1)
                for j in range(4):
                    dve.bn_aggr(z_mv[:, j, :], z_stats[:, j, :]).then_inc(comb_mv, 1)
                dve.wait_ge(comb_mv, 4 * (g + 1))
                rsqrt_newton(zn[1][:, :], zn[2][:, :], zn[3][:, :], zn[4][:, :], z_rstd[:, :], z_mv[:, :, 1], 1.0,
                             comb_newton, 4 * g, comb_seed, g + 1, EPS / 4)
                for j in range(4):
                    dve.tensor_scalar(acc[j][:, :], acc[j][:, :], z_mv[:, j, 0:1], z_rstd[:, j:j + 1], ALU.subtract,
                                      ALU.mult).then_inc(comb_ready, 1)

            four(0, True)
            with dve.Fori(1, NT // 4) as g:
                four(g, False)

        @block.tensor
        def _(pe):
            pe.wait_ge(consts_ready, 20)
            pe.wait_ge(inputs_loaded, 16 * 12)
            for i in range(4):
                for c in range(EC):
                    for r in range(2):
                        last = pe.transpose(other_bank[i][:, c * EMB + r * P:c * EMB + (r + 1) * P],
                                            w_rows[:, i, r, c * P:(c + 1) * P], ident[:, :])
                last.then_inc(w_turned, 1)
            for c in range(EC):
                last = pe.transpose(out_bank[:, c * E:(c + 1) * E], rw_rows[:, c * P:(c + 1) * P], ident[0:E, 0:E])
            last.then_inc(w_turned, 1)
            pe.wait_ge(w_ready, 12)

            def free_prep(kind, b, half, i):
                _, k, uses = prep(kind, b, half, i)
                at_least(pe, prep_taken[k], uses)
                return prep_bank[k]

            def free_out(kind, b, half, i):
                at_least(pe, out_taken, outs(kind, b, half, i)[0])
                return out_bank

            def turn_stack(to, b, half, s, p):
                for t in range(TT):
                    last = pe.transpose(to[:, t * P:(t + 1) * P],
                                        stack[half][:, t, s, 2 * p:2 * p + 2, :].rearrange(
                                            "p h w -> p (h w)").bitcast(F32), ident[:, :])
                return last

            def take_x(b):
                pe.wait_ge(x_loaded, 16 * (b.at + 1))
                for c in range(EC):
                    to = free_prep("x", b, 0, c)
                    for t in range(TT):
                        last = pe.transpose(to[:, t * P:(t + 1) * P], x_in[:, t, c * P:(c + 1) * P], ident[:, :])
                    last.then_inc(prep_full, 1)

            def project(b, half):
                if half == 0:
                    for c in range(EC):
                        prep_done(pe, prep("x", b, 0, c))
                for t in range(TT):
                    to = free_prep("project", b, half, t)
                    for c in range(EC):
                        last = pe.matmul(to[:, 0:3 * P], xT[:, c, t * P:(t + 1) * P],
                                         w_qkvT[:, c, half, :, :].rearrange("p s n -> p (s n)"),
                                         start=c == 0, stop=c == EC - 1)
                    last.then_inc(prep_full, 1)

            def turn(b, half, p):
                u = 2 * b.at + half
                pe.wait_ge(low_ready, 2 * (u + 1))
                pe.wait_ge(again_ready, 2 * (u + 1))
                pe.wait_ge(max_cleared, u + 1)
                for s, kind in ((1, "k"), (0, "q")):
                    turn_stack(free_prep(kind, b, half, p), b, half, s, p).then_inc(prep_full, 1)

            def row_maxima(b, half, p, i):
                if i == 0:
                    prep_done(pe, prep("k", b, half, p))
                    prep_done(pe, prep("q", b, half, p))
                to = free_prep("max", b, half, MAXB * p + i)
                for n, (h, t, c) in enumerate(MAX_REGIONS[i]):
                    rows = slice(h * SW, (h + 1) * SW)
                    pe.matmul(to[:, c:c + (t + 1) * P], qT[half][rows, p, t * P:(t + 1) * P],
                              kT[half][rows, p, 0:(t + 1) * P], start=n == 0, stop=False, skip_group_check=True)
                    last = pe.matmul(to[:, c + t * P:c + (t + 1) * P], ident_b[:, :], mask_ij[:, :], start=False,
                                     stop=n == len(MAX_REGIONS[i]) - 1, skip_group_check=True)
                last.then_inc(prep_full, 1)

            def maxima(b, half, p):
                for i in range(MAXB):
                    row_maxima(b, half, p, i)

            def with_maxima(b, half, p):
                pe.wait_ge(max_ready, PAIRS * (2 * b.at + half) + p + 1)
                turn_stack(free_out("q", b, half, p), b, half, 0, p).then_inc(out_full, 1)

            def score(b, half, p, i):
                u = 2 * b.at + half
                if i == 0:
                    out_done(pe, outs("q", b, half, p))
                to = st_bank[i % STB]
                at_least(pe, st_taken[i % STB], 2 * (PAIRS * u + p) + i // STB)
                for n, (h, j, c) in enumerate(ST_REGIONS[i]):
                    rows = slice(h * SW, (h + 1) * SW)
                    w = (TT - j) * P
                    pe.matmul(to[:, c:c + w], kT[half][rows, p, j * P:(j + 1) * P],
                              qT[half][rows, p, j * P:T], start=n == 0, stop=False, skip_group_check=True)
                    last = pe.matmul(to[:, c:c + P], ident_b[:, :], mask_ji[:, :], start=False,
                                     stop=n == len(ST_REGIONS[i]) - 1, skip_group_check=True)
                last.then_inc(st_full, 1)

            def scores(b, half, p):
                for i in range(PIECES):
                    score(b, half, p, i)

            def value(b, half, p, j, h):
                u = 2 * b.at + half
                i, c = PLACE[h, j]
                pe.wait_ge(st_taken[i % STB], 2 * (PAIRS * u + p) + i // STB + 1)
                rows = slice((2 * p + h) % 4 * VW, ((2 * p + h) % 4 + 1) * VW)
                return pe.matmul(pv_bank[p // 2][rows, j * P:T], v_aug[half][:, j, 2 * p + h, :],
                                 probsT[p % 2][:, i, c:c + (TT - j) * P], start=j == 0, stop=j == TT - 1,
                                 skip_group_check=True)

            def values(b, half, p, ahead, beside):
                u = 2 * b.at + half
                prep_done(pe, prep("project", b, half, TT - 1))
                if p % 2 == 0:
                    at_least(pe, sumsT_ready, 2 * u + p // 2 - 1)
                value(b, half, p, 0, 0)
                if beside:
                    row_maxima(*beside, 0)
                    row_maxima(*beside, 1)
                if ahead:
                    with_maxima(*ahead)
                value(b, half, p, 0, 1)
                if beside:
                    row_maxima(*beside, 2)
                value(b, half, p, 1, 0)
                if beside:
                    row_maxima(*beside, 3)
                if ahead:
                    score(*ahead, 0)
                value(b, half, p, 1, 1)
                if beside:
                    row_maxima(*beside, 4)
                if ahead:
                    score(*ahead, 1)
                if beside:
                    row_maxima(*beside, 5)
                if ahead:
                    score(*ahead, 2)

            def more_values(b, half, p, ahead):
                value(b, half, p, 2, 0)
                if ahead:
                    score(*ahead, 3)
                value(b, half, p, 2, 1)
                if ahead:
                    score(*ahead, 4)
                value(b, half, p, 3, 0)
                if ahead:
                    score(*ahead, 5)
                value(b, half, p, 3, 1).then_inc(pv_done, 1)

            def heads_of(b, half, g):
                pe.wait_ge(sumsT_ready, 2 * (2 * b.at + half) + g + 1)
                to = free_out("heads", b, half, g)
                for t in range(TT):
                    last = pe.transpose(to[:, t * P:(t + 1) * P], sumsT[:, t * P:(t + 1) * P], ident[:, :])
                last.then_inc(out_full, 1)

            def join(b, half):
                out_done(pe, outs("heads", b, half, 1))
                to = free_out("join", b, half, 0)
                for t in range(TT):
                    last = pe.transpose(to[:, t * P:(t + 1) * P], heads[:, t, :], ident[:, :])
                last.then_inc(out_full, 1)

            def project_out(b, i):
                out_done(pe, outs("join", b, 1, 0))
                to = free_out("y", b, 1, i)
                for t in range(2):
                    for c in range(EC):
                        last = pe.matmul(to[:, t * EMB:(t + 1) * EMB],
                                         headsT[:, c, (2 * i + t) * P:(2 * i + t + 1) * P], w_oT[:, c, :],
                                         start=c == 0, stop=c == EC - 1)
                last.then_inc(out_full, 1)

            def turn_x1(b, c):
                pe.wait_ge(x1_ready, TT * (b.at + 1))
                to = free_out("x1", b, 1, c)
                for t in range(TT):
                    last = pe.transpose(to[:, t * P:(t + 1) * P], x1[:, t, c * P:(c + 1) * P], ident[:, :])
                last.then_inc(out_full, 1)

            def route_logits(b):
                out_done(pe, outs("x1", b, 1, EC - 1))
                to = free_out("logits", b, 1, 0)
                for t in range(TT):
                    for c in range(EC):
                        last = pe.matmul(to[:, t * E:(t + 1) * E], x1T[:, c, t * P:(t + 1) * P], rwT[:, c, :],
                                         start=c == 0, stop=c == EC - 1)
                last.then_inc(out_full, 1)

            attention(pe, Steps(take_x=take_x, project=project, turn=turn, maxima=maxima, with_maxima=with_maxima,
                                scores=scores, values=values, more_values=more_values, heads=heads_of, join=join,
                                project_out=project_out,
                                turn_x1=turn_x1, route_logits=route_logits))

            for i in range(ITERS):
                pe.wait_ge(route_v, routed(i, 3))
                for t in range(TT):
                    last = pe.transpose(other_bank[0][0:NB * E, t * P:(t + 1) * P], logits[:, t, :, :].rearrange("p b e -> p (b e)"), ident[:, :])
                last.then_inc(route_p, 1)
                pe.wait_ge(route_v, routed(i, 6))
                pe.matmul(other_bank[1][:, 0:NB * E], ones[0:NB * E, :], col_diag[:, :], start=True,
                          stop=True).then_inc(route_p, 1)
            pe.wait_ge(choice_ready, 1)
            pe.matmul(other_bank[2][:, 0:NT * E], before_b[:, :], chosen_b[:, :, :].rearrange("p t e -> p (t e)"),
                      start=True, stop=True)
            pe.matmul(other_bank[3][:, 0:NT * E], ones_b[:, :], chosen_b[:, :, :].rearrange("p t e -> p (t e)"),
                      start=True, stop=True).then_inc(route_p, 1)

            def turn_x(i, k):
                t = 4 * i + k
                pe.wait_ge(xg_loaded[k % 4], 16 * (i + k // 4 + 1))
                at_least(pe, xgT_ready, t)
                for c in range(EC):
                    last = pe.transpose(x_bank[:, c * P:(c + 1) * P], xg[k % 4][:, c * P:(c + 1) * P], ident[:, :])
                last.then_inc(xg_turned, 1)

            def up(i, k):
                t = 4 * i + k
                e = pe.value_load(tile_e[0:1, bass.ds(t, 1)], min_val=0, max_val=E - 1)
                pe.wait_ge(xgT_ready, t + 1)
                at_least(pe, hid_ready, t)
                for w, to, full in ((wg_sb, g_bank, g_full), (wp_sb, p_bank, p_full)):
                    for c in range(EC):
                        last = pe.matmul(to[:, :], xgT[k % 2][:, c, :],
                                         w[:, bass.ds(e, 1), c * FF:(c + 1) * FF].rearrange("p o n -> p (o n)"),
                                         start=c == 0, stop=c == EC - 1)
                    last.then_inc(full, 1)

            def turn_h(i, k):
                t = 4 * i + k
                pe.wait_ge(hid_ready, t + 1)
                at_least(pe, hidT_ready, t)
                for c in range(FC):
                    last = pe.transpose(h_bank[:, c * P:(c + 1) * P], hid[k % 2][:, c * P:(c + 1) * P], ident[:, :])
                last.then_inc(hid_turned, 1)

            def down(i, k):
                t = 4 * i + k
                e = pe.value_load(tile_e[0:1, bass.ds(t, 1)], min_val=0, max_val=E - 1)
                pe.wait_ge(hidT_ready, t + 1)
                at_least(pe, yo_ready, 2 * t)
                for c in range(FC):
                    last = pe.matmul(y_bank[:, 0:EMB], hidT[k % 2][:, c, :],
                                     wo_sb[:, bass.ds(e, 1), c * EMB:(c + 1) * EMB].rearrange("p o n -> p (o n)"),
                                     start=c == 0, stop=c == FC - 1)
                last.then_inc(yo_full, 1)

            def four_tiles(i, last=False):
                for k in range(4):
                    turn_h(i, k)
                    if not (last and k == 3):
                        up(i, k + 1)
                    if not (last and k >= 2):
                        turn_x(i, k + 2)
                    down(i, k)

            pe.wait_ge(tiles_ready, 1)
            pe.wait_ge(slots_ready, 1)
            pe.wait_ge(experts_loaded, 16 * 3 * E)
            turn_x(0, 0)
            up(0, 0)
            turn_x(0, 1)
            four_tiles(0)
            with pe.Fori(1, SLOT_TILES // 4 - 1) as i:
                four_tiles(i)
            four_tiles(SLOT_TILES // 4 - 1, True)


_INS = ["L0_attn_x", "L0_attn_Wk", "L0_attn_Wq", "L0_attn_Wv", "L0_attn_Wo", "L0_attn_bo", "L0_attn_kln_g",
        "L0_attn_kln_b", "L0_attn_qln_g", "L0_attn_qln_b", "L0_ffn_router_w", "L0_ffn_router_b",
        "L0_ffn_temperature", "L0_ffn_wg", "L0_ffn_wp", "L0_ffn_wo"]


def kernel(**inputs):
    import numpy as np
    import concourse.bacc as bacc
    from concourse.bass_utils import run_bass_kernel_spmd

    nc = bacc.Bacc("TRN2", target_bir_lowering=False, num_devices=1)
    arrays, args = {}, []
    for name in _INS:
        v = np.ascontiguousarray(inputs[name])
        arrays[f"in_{name}"] = v
        args.append(nc.dram_tensor(f"in_{name}", v.shape, mybir.dt.from_np(v.dtype), kind="ExternalInput").ap())
    args.append(nc.dram_tensor("out_dram", (NB, T, EMB), F32, kind="ExternalOutput").ap())
    layer(nc, *args)
    r = run_bass_kernel_spmd(nc, [arrays], core_ids=[0])
    return r.results[0]["out_dram"]
```

```python
from contextlib import ExitStack

import concourse.bass as bass
from concourse import mybir

P = 128
NB, T, EMB = 8, 512, 256
H, D = 16, 16
E, FF, K = 8, 512, 2
TT = T // P
NT = NB * TT
EC = EMB // P
FC = FF // P
HH = H // 2
PAIRS = HH // 2
SW = 64
EPS = 1e-5
QK_SCALE = EMB ** -0.25
MASKED = -1e30
SLOT_TILES = NB * T * K // P + E
SLOTS = SLOT_TILES * P
HOTS = 8
ITERS = 3
GROUPS = NT // 4

ALU = mybir.AluOpType
ACT = mybir.ActivationFunctionType
AX = mybir.AxisListType.X
F32 = mybir.dt.float32
F32R = mybir.dt.float32r
BF16 = mybir.dt.bfloat16
I32 = mybir.dt.int32
U32 = mybir.dt.uint32

MAXB = 6
EARLY, LATE = range(4), range(4, 6)
VW = 32
PIECES = 6
PREPB = 3
STB = 3


def at_least(engine, semaphore, value):
    if not isinstance(value, int) or value > 0:
        engine.wait_ge(semaphore, value)


class Batch:

    def __init__(self, at, like=None):
        self.at, self.like = at, at if like is None else like

    def after(self, n):
        return Batch(self.at + n, self.like + n)


class Order:

    def __init__(self, steps, banks):
        self.number = {step: n for n, step in enumerate(steps)}
        self.banks = banks
        per = [self.number[s] - self.number[(s[0], s[1] - 1) + s[2:]] for s in steps if s[1] == 3]
        assert len(set(per)) == 1 and per[0] % banks == 0
        self.per_batch = per[0]

    def __call__(self, kind, b, half, i):
        n = self.number[kind, b.like, half, i]
        ahead = b.at - b.like
        return (self.per_batch * ahead + n, n % self.banks, self.per_batch // self.banks * ahead + n // self.banks)


class Chain:

    def __init__(self, engine, semaphore, count):
        self.engine, self.semaphore, self.count = engine, semaphore, count

    def __call__(self, instruction):
        self.count += 1
        instruction.then_inc(self.semaphore, 1)
        self.engine.wait_ge(self.semaphore, self.count)


def layer(nc, x, Wk, Wq, Wv, Wo, bo, kln_g, kln_b, qln_g, qln_b, router_w, router_b,
          temperature, wg, wp, wo, out):
    x_tiles = x.rearrange("b (t p) e -> b p t e", p=P)
    out_tiles = out.rearrange("b (t p) e -> (b t) p e", p=P)
    x1_dram = nc.dram_tensor("x1_dram", [NB * T, EMB], F32, kind="Internal").ap()
    x1_tiles = x1_dram.rearrange("(b t p) e -> b p t e", b=NB, p=P)
    ys_dram = nc.dram_tensor("ys_dram", [NB * T * K + SLOTS, EMB], F32, kind="Internal").ap()

    with ExitStack() as ctx:
        def sb(name, shape, dt=F32, where=ctx):
            return where.enter_context(nc.sbuf_tensor(name, shape, dt))

        def bank(name, shape=(P, 512), dt=F32, where=ctx):
            return where.enter_context(nc.psum_tensor(name, list(shape), dt))

        def sem(name):
            return ctx.enter_context(nc.semaphore(name))

        experts = sb("experts", [P, 2, E * EC * FF])
        w_high = experts[:, :, :].rearrange("p s (e n) -> p s e n", e=E).bitcast(F32R)
        flat = experts[:, :, :].rearrange("p a n -> p (a n)")
        w_rows = flat[:, 2 * E * EC * FF - 8 * EMB:].rearrange("p (i c e) -> p i c e", i=4, c=2)
        ident = sb("ident", [P, P])
        ident_b = sb("ident_b", [P, P], BF16)
        ones = sb("ones", [P, P])
        ones_b = sb("ones_b", [P, P], BF16)
        before_b = sb("before_b", [P, P], BF16)
        mask = sb("mask", [P, P], BF16)
        eps_col = sb("eps_col", [P, 1])
        eps4_col = sb("eps4_col", [P, 1])
        logits = sb("logits", [P, TT, NB, E])
        rb_row = sb("rb_row", [P, E])
        temp_col = sb("temp_col", [P, 1])
        inv_temp = sb("inv_temp", [P, 1])

        spare = flat[:, 0:4 * TT * EMB]
        x_in, x_res, y, x1 = (spare[:, i * TT * EMB:(i + 1) * TT * EMB].rearrange("p (t e) -> p t e", e=EMB)
                              for i in range(4))

        probs_at = 4 * TT * EMB
        probs_mem = [flat[:, probs_at + i * PIECES * 512:probs_at + (i + 1) * PIECES * 512].rearrange(
            "p (i n) -> p i n", i=PIECES) for i in range(3)]

        att_mem = ExitStack()
        a = lambda name, shape, dt=F32: sb(name, shape, dt, att_mem)
        w_qkvT = a("w_qkvT", [P, EC, 2, 3, P])
        w_oT = a("w_oT", [P, EC, EMB])
        w_mean = a("w_mean", [P, 2, EC, H])
        rw_rows = a("rw_rows", [E, EMB])
        rwT = a("rwT", [P, EC, E])
        gains = a("gains", [P, 2, D])
        shifts = a("shifts", [P, 2, D])
        bo_row = a("bo_row", [P, EMB])
        xT = a("xT", [P, EC, T])
        raw = a("raw", [P, TT, 2 * P])
        normed = a("normed", [P, TT, 2 * P])
        squares = normed
        ssum = a("ssum", [P, TT, 2 * HH])
        nt = [a(f"nt{i}", [P, TT, 2 * HH]) for i in range(5)]
        rstd = a("rstd", [P, TT, 2 * HH])
        stack = [a(f"stack{i}", [P, TT, 2, HH, SW], F32R) for i in range(2)]
        kT = [a(f"kT{i}", [P, PAIRS, T], F32R) for i in range(2)]
        qT = [a(f"qT{i}", [P, PAIRS, T], F32R) for i in range(2)]
        v_aug = [a(f"v_aug{i}", [P, TT, HH, VW]) for i in range(2)]
        neg_max = a("neg_max", [P, TT, HH])
        probsT = [probs_mem[0], probs_mem[1], probs_mem[2], probs_mem[1]]
        sumsT = a("sumsT", [P, T])
        recip = a("recip", [P, TT, 4])
        heads = a("heads", [P, TT, P])
        headsT = a("headsT", [P, 2, T])
        y_stats = a("y_stats", [P, TT, 6])
        y_mv = a("y_mv", [P, TT, 2])
        yn = [a(f"yn{i}", [P, TT]) for i in range(5)]
        y_rstd = a("y_rstd", [P, TT])
        x1T = headsT
        att_mem.close()

        ffn_mem = ExitStack()
        f = lambda name, shape, dt=F32: sb(name, shape, dt, ffn_mem)
        w_low = f("w_low", [P, 2, E, EC * FF], BF16)
        wo_sb = f("wo_sb", [P, E, FC * EMB])
        row_a = f("row_a", [P, NT])
        row_b = f("row_b", [P, NT])
        col_nmax = f("col_nmax", [NB * E, 1])
        col_sum = f("col_sum", [NB * E, 1])
        col_ln = f("col_ln", [NB * E, 1])
        col_lse = f("col_lse", [NB * E, 1])
        col_diag = f("col_diag", [NB * E, NB * E])
        gates = f("gates", [P, NT, E])
        best = f("best", [P, NT, 8])
        best_at = f("best_at", [P, NT, 8], U32)
        best_atf = f("best_atf", [P, NT, K])
        expert_iota = f("expert_iota", [P, E])
        chosen = [f(f"chosen{k}", [P, NT, E]) for k in range(K)]
        chosen_b = f("chosen_b", [P, NT, E], BF16)
        counts = f("counts", [P, NT, E])
        scan = [f(f"scan{i}", [P, NT, E]) for i in range(2)]
        n_tiles_i = f("n_tiles_i", [P, E], I32)
        n_tiles_j = f("n_tiles_j", [P, E], I32)
        n_tiles = f("n_tiles", [P, E])
        escan = [f(f"escan{i}", [P, E]) for i in range(2)]
        first_slot = f("first_slot", [P, E])
        with ExitStack() as sinkhorn_mem:
            exps = sb("exps", [P, NT, E], where=sinkhorn_mem)
            col_exps = sb("col_exps", [NB * E, T], where=sinkhorn_mem)
        slot_all = f("slot_all", [P, NT, E])
        slot_of = [f(f"slot_of{k}", [P, NT, E]) for k in range(K)]
        slot_f = f("slot_f", [P, K, NT])
        slot_i = f("slot_i", [P, K, NT], I32)
        slot_tile_i = f("slot_tile_i", [P, K, NT], I32)
        slot_tile = f("slot_tile", [P, K, NT])
        slot_row = f("slot_row", [P, K, NT])
        code_parts = f("code_parts", [P, 2, K, NT])
        code_sum = f("code_sum", [P, SLOT_TILES])
        row_iota = f("row_iota", [P, P])
        code_row = f("code_row", [P, SLOT_TILES])
        code_row_i = f("code_row_i", [P, SLOT_TILES], I32)
        unfilled_row = f("unfilled_row", [P, SLOT_TILES])
        unfilled = f("unfilled", [P, SLOT_TILES])
        send_to = f("send_to", [P, SLOT_TILES], U32)
        token_of = f("token_of", [P, SLOT_TILES], U32)
        top_sum = f("top_sum", [P, NT])
        top_gate = f("top_gate", [P, NT, K])
        tile_iota = f("tile_iota", [P, SLOT_TILES])
        past = f("past", [1, SLOT_TILES, E])
        tile_ef = f("tile_ef", [1, SLOT_TILES])
        tile_e = f("tile_e", [1, SLOT_TILES], I32)
        with ExitStack() as list_mem:
            row_hot = sb("row_hot", [P, K * NT, P], BF16, where=list_mem)
            tile_code = sb("tile_code", [P, K * NT, 2, SLOT_TILES], BF16, where=list_mem)
            tile_hot = [sb(f"tile_hot{i}", [P, HOTS, SLOT_TILES], where=list_mem) for i in range(2)]
            w_raw = [sb(f"w_raw{i}", [P, 2, EC * FF], where=list_mem) for i in range(2)]
        x1_all = f("x1_all", [P, NT, EMB])
        y_two = [flat[:, i * K * EMB:(i + 1) * K * EMB].rearrange("p (k e) -> p k e", k=K) for i in range(8)]
        acc = [flat[:, (8 * K + i) * EMB:(8 * K + i + 1) * EMB] for i in range(8)]
        scaled_z = [flat[:, (8 * K + 8 + i) * EMB:(8 * K + 9 + i) * EMB] for i in range(8)]
        z_stats = f("z_stats", [P, 4, 6])
        z_mv = [f(f"z_mv{i}", [P, 4, 2]) for i in range(2)]
        zn = [[f(f"zn{i}_{n}", [P, 4]) for n in range(5)] for i in range(2)]
        z_rstd = [f(f"z_rstd{i}", [P, 4]) for i in range(2)]
        z_shift = [f(f"z_shift{i}", [P, 4]) for i in range(2)]
        xg = [f(f"xg{i}", [P, EMB]) for i in range(4)]
        xgT = [f(f"xgT{i}", [P, EC, P], F32R) for i in range(2)]
        xgT_low = [f(f"xgT_low{i}", [P, EC, P], F32R) for i in range(2)]
        xgT_b = [f(f"xgT_b{i}", [P, EC, P], BF16) for i in range(2)]
        gate_act = [f(f"gate_act{i}", [P, FF]) for i in range(2)]
        hid = [f(f"hid{i}", [P, FF]) for i in range(2)]
        hidT = [f(f"hidT{i}", [P, FC, P]) for i in range(2)]
        y_out = [f(f"y_out{i}", [P, EMB]) for i in range(2)]
        y_at = [f(f"y_at{i}", [P, 1], U32) for i in range(2)]
        x_at = [f(f"x_at{i}", [P, 1], U32) for i in range(4)]
        ffn_mem.close()

        psum_a = ExitStack()
        st_bank = [bank(f"st_bank{i}", where=psum_a) for i in range(STB)]
        pv_bank = bank("pv_bank", where=psum_a)
        prep_bank = [bank(f"prep_bank{i}", where=psum_a) for i in range(PREPB)]
        out_bank = bank("out_bank", where=psum_a)
        other_bank = st_bank + [pv_bank]
        g_bank, p_bank, h_bank, y_bank = other_bank
        x_bank = prep_bank[0]

        consts_ready = sem("consts_ready")
        inputs_loaded = sem("inputs_loaded")
        w_turned = sem("w_turned")
        w_copied = sem("w_copied")
        w_mean_done = sem("w_mean_done")
        w_ready = sem("w_ready")
        experts_loaded = sem("experts_loaded")
        x_loaded = sem("x_loaded")
        res_loaded = sem("res_loaded")
        res_ready = sem("res_ready")
        prep_full = sem("prep_full")
        prep_taken = [sem(f"prep_taken{i}") for i in range(PREPB)]
        squares_ready = sem("squares_ready")
        ssum_ready = sem("ssum_ready")
        ln_ready = sem("ln_ready")
        seed_ready = sem("seed_ready")
        newton = sem("newton")
        normed_ready = sem("normed_ready")
        gained_q = sem("gained_q")
        gained_k = sem("gained_k")
        shifted_q = sem("shifted_q")
        shifted_k = sem("shifted_k")
        high_ready = sem("high_ready")
        low_ready = sem("low_ready")
        again_ready = sem("again_ready")
        max_cleared = sem("max_cleared")
        max_high = sem("max_high")
        max_ready = sem("max_ready")
        out_full = sem("out_full")
        out_taken = sem("out_taken")
        st_full = sem("st_full")
        st_taken = [sem(f"st_taken{i}") for i in range(STB)]
        masked = sem("masked")
        pv_done = sem("pv_done")
        sumsT_ready = sem("sumsT_ready")
        recip_ready = sem("recip_ready")
        y_stats_ready = sem("y_stats_ready")
        y_mv_ready = sem("y_mv_ready")
        y_ln_ready = sem("y_ln_ready")
        y_seed_ready = sem("y_seed_ready")
        y_newton = sem("y_newton")
        x1_ready = sem("x1_ready")
        x1_saved = sem("x1_saved")
        route_v = sem("route_v")
        route_a = sem("route_a")
        route_p = sem("route_p")
        rows_max = sem("rows_max")
        wait_passed = sem("wait_passed")
        send_passed = sem("send_passed")
        choice_ready = sem("choice_ready")
        iotas_ready = sem("iotas_ready")
        x1_loaded = sem("x1_loaded")
        tile_equal = sem("tile_equal")
        tile_coded = sem("tile_coded")
        row_hot_v = sem("row_hot_v")
        row_apart = sem("row_apart")
        row_apart2 = sem("row_apart2")
        row_hot_a = sem("row_hot_a")
        slots_coded = sem("slots_coded")
        lists_ready = sem("lists_ready")
        x_at_ready = sem("x_at_ready")
        y_at_ready = sem("y_at_ready")
        slots_ready = sem("slots_ready")
        tiles_ready = sem("tiles_ready")
        xg_loaded = [sem(f"xg_loaded{i}") for i in range(4)]
        xg_turned = sem("xg_turned")
        xgT_ready = sem("xgT_ready")
        xgT_b_ready = sem("xgT_b_ready")
        xgT_low_ready = sem("xgT_low_ready")
        w_raw_loaded = [sem(f"w_raw_loaded{i}") for i in range(2)]
        w_high_ready = sem("w_high_ready")
        w_low_ready = sem("w_low_ready")
        g_full = sem("g_full")
        p_full = sem("p_full")
        relu_ready = sem("relu_ready")
        hid_ready = sem("hid_ready")
        hid_turned = sem("hid_turned")
        hidT_ready = sem("hidT_ready")
        yo_full = sem("yo_full")
        yo_ready = sem("yo_ready")
        yo_sent = [sem(f"yo_sent{i}") for i in range(2)]
        yt_loaded = [sem(f"yt_loaded{i}") for i in range(8)]
        comb_scale = sem("comb_scale")
        comb_a = sem("comb_a")
        comb_b = sem("comb_b")
        comb_stats = sem("comb_stats")
        comb_mv = sem("comb_mv")
        comb_ln = sem("comb_ln")
        comb_seed = sem("comb_seed")
        comb_newton = sem("comb_newton")
        comb_ready = sem("comb_ready")
        stored = [sem(f"stored{i}") for i in range(8)]

        PARAMS = 11

        def half_of(b, half, first, last, do):
            nb, nh = (b, 1) if half == 0 else (b.after(1), 0)
            pb, ph = (b, 0) if half == 1 else (b.after(-1), 1)
            more = not (last and half == 1)
            done = not (first and half == 0)
            ends = done and half == 0
            for p in range(PAIRS):
                following = [(b, half, q) for q in range(p + 1, PAIRS)]
                if more:
                    following += [(nb, nh, q) for q in range(2)]
                following += [None, None]
                if p == 1 and more:
                    do.norm(nb, nh)
                if p == 0 and half == 1 and not first:
                    do.turn_x1(b.after(-1), 1)
                if p == 1 and done:
                    do.join(pb, ph)
                if p == 1 and more:
                    do.project_v(nb, nh)
                if p == 2 and more:
                    do.turn(nb, nh, 0)
                if p == 2 and half == 0 and not last:
                    do.take_x(b.after(1))
                if p == 3 and more:
                    do.turn(nb, nh, 2)
                if p == 3 and ends:
                    do.norm_x1(pb)
                do.values(b, half, p, following[0], following[1])
                if p == 0 and done:
                    do.heads(pb, ph, 1)
                if p == 0 and half == 1 and not first:
                    do.route_logits(b.after(-1))
                if p == 1 and more:
                    do.split(nb, nh)
                if p == 1 and ends:
                    do.project_out(pb, 0)
                if p == 2 and more:
                    do.turn(nb, nh, 1)
                if p == 2 and ends:
                    do.project_out(pb, 1)
                if p == 3 and more:
                    do.turn(nb, nh, 3)
                if p == 3 and ends:
                    do.turn_x1(pb, 0)
                if p == 2 and not last:
                    do.project(b.after(1), half)
                if p == 2:
                    do.heads(b, half, 0)
                if p == 3 and not last:
                    do.sums(b.after(1), half)
                do.more_values(b, half, p, following[0], following[1])

        def attention(engine, do):
            first = Batch(0)
            do.take_x(first)
            do.project(first, 0)
            do.project_v(first, 0)
            do.sums(first, 0)
            do.norm(first, 0)
            do.split(first, 0)
            do.project(first, 1)
            for p in range(PAIRS):
                do.turn(first, 0, p)
            do.sums(first, 1)
            for p in range(2):
                do.maxima(first, 0, p)
            do.with_maxima(first, 0, 0)
            do.scores(first, 0, 0)
            half_of(first, 0, True, False, do)
            half_of(first, 1, True, False, do)
            if engine is None:
                for b in range(1, NB - 1):
                    half_of(Batch(b), 0, False, False, do)
                    half_of(Batch(b), 1, False, False, do)
            else:
                with engine.Fori(1, NB - 1) as at:
                    half_of(Batch(at, 2), 0, False, False, do)
                    half_of(Batch(at, 2), 1, False, False, do)
            last = Batch(NB - 1)
            half_of(last, 0, False, True, do)
            half_of(last, 1, False, True, do)
            do.heads(last, 1, 1)
            do.join(last, 1)
            for i in range(2):
                do.project_out(last, i)
            do.norm_x1(last)
            for c in range(EC):
                do.turn_x1(last, c)
            do.route_logits(last)

        def nothing(*_):
            pass

        class Steps:

            def __init__(self, take_x=nothing, project=nothing, project_v=nothing, sums=nothing, norm=nothing, split=nothing,
                         turn=nothing, maxima=nothing, with_maxima=nothing, scores=nothing, values=nothing,
                         more_values=nothing, heads=nothing, join=nothing, project_out=nothing, norm_x1=nothing,
                         turn_x1=nothing, route_logits=nothing):
                self.take_x = take_x
                self.project = project
                self.project_v = project_v
                self.sums = sums
                self.norm = norm
                self.split = split
                self.turn = turn
                self.maxima = maxima
                self.with_maxima = with_maxima
                self.scores = scores
                self.values = values
                self.more_values = more_values
                self.heads = heads
                self.join = join
                self.project_out = project_out
                self.norm_x1 = norm_x1
                self.turn_x1 = turn_x1
                self.route_logits = route_logits

        prep_steps, out_steps = [], []

        def note_maxima(b, half, p, some=range(MAXB)):
            prep_steps.extend(("max", b.at, half, MAXB * p + i) for i in some)

        def note_with_maxima(b, half, p):
            out_steps.append(("q", b.at, half, p))

        def note_values(b, half, p, ahead, beside):
            if beside:
                note_maxima(*beside, EARLY)
            if ahead:
                note_with_maxima(*ahead)

        def note_more_values(b, half, p, ahead, beside):
            if beside:
                note_maxima(*beside, LATE)

        attention(None, Steps(
            take_x=lambda b: prep_steps.extend(("x", b.at, 0, c) for c in range(EC)),
            project=lambda b, half: prep_steps.extend(("project", b.at, half, i) for i in range(TT // 2)),
            project_v=lambda b, half: prep_steps.append(("v", b.at, half, 0)),
            turn=lambda b, half, p: prep_steps.extend((kind, b.at, half, p) for kind in ("k", "q")),
            maxima=note_maxima, with_maxima=note_with_maxima, values=note_values,
            more_values=note_more_values,
            heads=lambda b, half, g: out_steps.append(("heads", b.at, half, g)),
            join=lambda b, half: out_steps.append(("join", b.at, half, 0)),
            project_out=lambda b, i: out_steps.append(("y", b.at, 1, i)),
            turn_x1=lambda b, c: out_steps.append(("x1", b.at, 1, c)),
            route_logits=lambda b: out_steps.append(("logits", b.at, 1, 0))))
        prep = Order(prep_steps, PREPB)
        outs = Order(out_steps, 1)

        def routed(i, k):
            return 1 + 7 * i + k

        MAX_REGIONS = [[(0, 3, 0)], [(1, 3, 0)], [(0, 2, 0), (0, 0, 384)], [(1, 2, 0), (1, 0, 384)],
                       [(0, 1, 0)], [(1, 1, 0)]]
        ST_REGIONS = [[(0, 0, 0)], [(1, 0, 0)], [(0, 1, 0), (0, 3, 384)], [(1, 1, 0), (1, 3, 384)],
                      [(0, 2, 0)], [(1, 2, 0)]]
        WIDTH = [512, 512, 512, 512, 256, 256]
        PLACE = {(h, j): (i, c) for i, regions in enumerate(ST_REGIONS) for h, j, c in regions}

        def out_done(engine, step, after=1):
            engine.wait_ge(out_taken, step[0] + after)

        def prep_done(engine, step):
            _, k, uses = step
            engine.wait_ge(prep_taken[k], uses + 1)

        def row_hots(engine, i, op):
            some = slice(i * HOTS, (i + 1) * HOTS)
            rows = slot_row[:, :, :].rearrange("p k t -> p (k t)")[:, some]
            return engine.tensor_tensor(row_hot[:, some, :], rows.unsqueeze(2).broadcast_to([P, HOTS, P]),
                                        row_iota[:, :].unsqueeze(1).broadcast_to([P, HOTS, P]), op)

        def scale_shift(engine, s, gained, shifted, u):
            v = normed[:, :, s * P:(s + 1) * P].rearrange("p t (h d) -> p t h d", d=D)
            engine.tensor_tensor(v, v, gains[:, s:s + 1, :].unsqueeze(2).broadcast_to([P, TT, HH, D]),
                                 ALU.mult).then_inc(gained, 1)
            engine.wait_ge(gained, u + 1)
            engine.tensor_tensor(v, v, shifts[:, s:s + 1, :].unsqueeze(2).broadcast_to([P, TT, HH, D]),
                                 ALU.add).then_inc(shifted, 1)

        block = ctx.enter_context(nc.Block())

        @block.sync
        def _(sp):
            for i, w in enumerate((Wq, Wk, Wv, Wo)):
                sp.dma_start(w_rows[:, i, :, :], w.rearrange("(c p) e -> p c e", p=P)).then_inc(inputs_loaded, 16)
            sp.dma_start(x_in[:, :, :], x_tiles[0]).then_inc(x_loaded, 16)
            sp.dma_start(rw_rows[:, :], router_w).then_inc(inputs_loaded, 16)
            rows = ((gains[:, 0, :], qln_g), (gains[:, 1, :], kln_g), (shifts[:, 0, :], qln_b),
                    (shifts[:, 1, :], kln_b), (bo_row[:, :], bo), (rb_row[:, :], router_b))
            for to, row in rows:
                sp.dma_start(to, row.partition_broadcast(P)).then_inc(inputs_loaded, 16)
            sp.dma_start(temp_col[:, :], temperature.partition_broadcast(P)).then_inc(inputs_loaded, 16)
            sp.dma_start(x_res[:, :, :], x_tiles[0]).then_inc(res_loaded, 16)

            def load_x(b):
                sp.wait_ge(prep_full, prep("x", b.after(-1), 0, EC - 1)[0] + 1)
                sp.dma_start(x_in[:, :, :], x_tiles[bass.ds(b.at, 1)].rearrange(
                    "o p t e -> (o p) t e")).then_inc(x_loaded, 16)

            def load_residual(b):
                out_done(sp, outs("y", b.after(-1), 1, 1))
                sp.dma_start(x_res[:, :, :], x_tiles[bass.ds(b.at, 1)].rearrange(
                    "o p t e -> (o p) t e")).then_inc(res_loaded, 16)

            def save_x1(b):
                sp.wait_ge(x1_ready, TT * (b.at + 1))
                sp.dma_start(x1_tiles[bass.ds(b.at, 1)].rearrange("o p t e -> (o p) t e"), x1).then_inc(
                    x1_saved, 16)

            load_x(Batch(1))
            with sp.Fori(1, NB - 1) as at:
                load_x(Batch(at, 2).after(1))
                load_residual(Batch(at, 2))
                save_x1(Batch(at, 2).after(-1))
            load_residual(Batch(NB - 1))
            save_x1(Batch(NB - 2))
            save_x1(Batch(NB - 1))

            sp.wait_ge(x1_saved, 16 * NB)
            sp.wait_ge(out_taken, len(out_steps))
            for e in range(E):
                if e >= 2:
                    sp.wait_ge(w_low_ready, e - 1)
                for i, w in enumerate((wg, wp)):
                    sp.dma_start(w_raw[e % 2][:, i, :].rearrange("p (c n) -> p c n", c=EC),
                                 w[e].rearrange("(c p) n -> p c n", p=P)).then_inc(w_raw_loaded[e % 2], 16)
            for e in range(E):
                sp.dma_start(wo_sb[:, e, :].rearrange("p (c n) -> p c n", c=FC),
                             wo[e].rearrange("(c p) n -> p c n", p=P)).then_inc(experts_loaded, 16)
            sp.wait_ge(lists_ready, 1)
            for b in range(NB):
                sp.dma_start(x1_all[:, b * TT:(b + 1) * TT, :], x1_tiles[b]).then_inc(x1_loaded, 16)

            for par in range(2):
                sp.wait_ge(yo_sent[par], 16 * (SLOT_TILES // 2))
            y_rows = ys_dram[0:NB * T * K, :].rearrange("(t p k) e -> t p k e", p=P, k=K)

            def load_two(g, half):
                for j in range(4):
                    n = half * 4 + j
                    if g is not None:
                        sp.wait_ge(comb_b, 4 * (g - 2) + j + 1)
                    t = half * 4 + j if g is None else 4 * g + j
                    sp.dma_start(y_two[n][:, :, :], y_rows[bass.ds(t, 1)].rearrange(
                        "o p k e -> (o p) k e")).then_inc(yt_loaded[n], 16)

            def store(g, half):
                for j in range(4):
                    n = half * 4 + j
                    sp.wait_ge(comb_ready, 4 * g + j + 1)
                    sp.dma_start(out_tiles[bass.ds(4 * g + j, 1)].rearrange("o p e -> (o p) e"),
                                 scaled_z[n][:, :]).then_inc(stored[n], 16)

            load_two(None, 0)
            load_two(None, 1)
            with sp.Fori(1, GROUPS // 2) as i:
                for half in range(2):
                    load_two(2 * i + half, half)
                    store(2 * i - 2 + half, half)
            for half in range(2):
                store(GROUPS - 2 + half, half)
            for n in range(8):
                sp.wait_ge(stored[n], 16 * (GROUPS // 2))

        @block.gpsimd
        def _(pool):
            pool.memset(ident[:, :], 0.0).then_inc(consts_ready, 1)
            pool.memset(ones[:, :], 1.0).then_inc(consts_ready, 1)
            pool.memset(ones_b[:, :], 1.0).then_inc(consts_ready, 1)
            pool.memset(mask[:, :], 0.0).then_inc(consts_ready, 1)
            pool.memset(eps_col[:, :], EPS).then_inc(consts_ready, 1)
            pool.memset(eps4_col[:, :], EPS / 4).then_inc(consts_ready, 1)
            pool.wait_ge(consts_ready, 6)
            pool.affine_select(out=ident[:, :], in_=ident[:, :], compare_op=ALU.not_equal, fill=1.0, base=0,
                               pattern=[[-1, P]], channel_multiplier=1).then_inc(consts_ready, 1)
            pool.affine_select(out=mask[:, :], in_=mask[:, :], compare_op=ALU.is_ge, fill=MASKED, base=0,
                               pattern=[[-1, P]], channel_multiplier=1).then_inc(consts_ready, 1)
            pool.affine_select(out=before_b[:, :], in_=ones_b[:, :], compare_op=ALU.is_gt, fill=0.0, base=0,
                               pattern=[[1, P]], channel_multiplier=-1).then_inc(consts_ready, 1)
            pool.wait_ge(consts_ready, 7)
            pool.tensor_copy(ident_b[:, :], ident[:, :]).then_inc(consts_ready, 1)
            for i in range(2):
                pool.memset(stack[i][:, :, :, :, 32:48].bitcast(F32), 0.0).then_inc(consts_ready, 1)
                pool.memset(v_aug[i][:, :, :, D:VW], 0.0).then_inc(consts_ready, 1)
            pool.wait_ge(consts_ready, 14)
            for i in range(2):
                pool.memset(stack[i][:, :, 1, :, 32:34].bitcast(F32), 1.0).then_inc(consts_ready, 1)
                pool.memset(v_aug[i][:, :, :, D:D + 1], 1.0).then_inc(consts_ready, 1)

            def project(b, half):
                u = 2 * b.at + half
                for i in range(TT // 2):
                    prep_done(pool, prep("project", b, half, i))
                at_least(pool, low_ready, 2 * u)
                pool.tensor_tensor(squares[:, :, :], raw[:, :, :], raw[:, :, :], ALU.mult).then_inc(squares_ready, 1)
                pool.memset(stack[half][:, :, 0, :, 32:34].bitcast(F32), 0.0).then_inc(max_cleared, 1)

            def norm(b, half):
                u = 2 * b.at + half
                pool.wait_ge(normed_ready, u + 1)
                scale_shift(pool, 0, gained_q, shifted_q, u)

            def heads_of(b, half, g):
                if half == 1 and g == 0:
                    pool.wait_ge(res_loaded, 16 * (b.at + 1))
                    pool.tensor_tensor(x_res, x_res, bo_row[:, :].unsqueeze(1).broadcast_to([P, TT, EMB]),
                                       ALU.add).then_inc(res_ready, 1)

            pool.wait_ge(w_ready, 3)
            def hide_later(b, half, p, groups):
                n = PAIRS * (2 * b.at + half) + p
                for g in groups:
                    for i in (2 * g, 2 * g + 1):
                        pool.wait_ge(st_taken[i % STB], 2 * n + i // STB + 1)
                    pool.sem_inc(send_passed, 1)
                    for _, _, c in ST_REGIONS[2 * g]:
                        v = probsT[p][:, 2 * g:2 * g + 2, c:c + P]
                        pool.affine_select(out=v, in_=v, compare_op=ALU.is_ge, fill=0.0, base=0,
                                           pattern=[[0, 2], [1, P]], channel_multiplier=-1).then_inc(masked, 1)

            def values(b, half, p, ahead, beside):
                if ahead:
                    hide_later(*ahead, (0, 1))

            def more_values(b, half, p, ahead, beside):
                if ahead:
                    hide_later(*ahead, (2,))

            attention(pool, Steps(scores=lambda b, half, p: hide_later(b, half, p, range(3)), values=values,
                                  more_values=more_values, project=project, norm=norm, heads=heads_of))

            pool.wait_ge(out_taken, len(out_steps))
            pool.wait_ge(x1_saved, 16 * NB)

            def row_differences():
                pool.wait_ge(iotas_ready, 8)
                pool.wait_ge(slots_ready, 1)
                for i in range(1, K * NT // HOTS, 2):
                    row_hots(pool, i, ALU.subtract).then_inc(row_apart, 1)

            pool.iota(expert_iota[:, :], [[1, E]], base=0, channel_multiplier=0,
                      allow_small_or_imprecise_dtypes=True).then_inc(iotas_ready, 1)
            pool.iota(tile_iota[:, :], [[1, SLOT_TILES]], base=0, channel_multiplier=0,
                      allow_small_or_imprecise_dtypes=True).then_inc(iotas_ready, 1)
            pool.iota(row_iota[:, :], [[1, P]], base=0, channel_multiplier=0,
                      allow_small_or_imprecise_dtypes=True).then_inc(iotas_ready, 1)
            pool.iota(unfilled_row[:, :], [[P, SLOT_TILES]], base=NB * T * K, channel_multiplier=1,
                      allow_small_or_imprecise_dtypes=True).then_inc(iotas_ready, 1)
            for k in range(K):
                pool.iota(code_parts[:, 0, k, :], [[K * P, TT], [K * T, NB]], base=0, channel_multiplier=0,
                          allow_small_or_imprecise_dtypes=True).then_inc(iotas_ready, 1)
                pool.iota(code_parts[:, 1, k, :], [[0, NT]], base=k + 1, channel_multiplier=K,
                          allow_small_or_imprecise_dtypes=True).then_inc(iotas_ready, 1)
            for e in range(E):
                pool.wait_ge(w_high_ready, e + 1)
                pool.tensor_tensor(w_low[:, :, e, :], w_raw[e % 2][:, :, :], w_high[:, :, e, :].bitcast(F32),
                                   ALU.subtract).then_inc(w_low_ready, 1)
            row_differences()

            def gather(t, k, n):
                at_least(pool, xg_loaded[k], 16 * n)
                pool.tensor_copy(x_at[k][:, :], token_of[:, bass.ds(t, 1)]).then_inc(x_at_ready, 1)
                pool.wait_ge(x_at_ready, t + 1)
                pool.sem_inc(send_passed, 1)
                at_least(pool, xg_turned, t - 3)
                pool.sem_inc(send_passed, 1)
                pool.indirect_dma_start(xg[k][:, :], None, x1_dram,
                                        bass.IndirectOffsetOnAxis(x_at[k][:, 0:1], 0)).then_inc(xg_loaded[k], 16)

            def send(t, par, n):
                at_least(pool, yo_sent[par], 16 * n)
                pool.tensor_copy(y_at[par][:, :], send_to[:, bass.ds(t, 1)]).then_inc(y_at_ready, 1)
                pool.wait_ge(y_at_ready, t + 1)
                pool.sem_inc(send_passed, 1)
                pool.wait_ge(yo_ready, t + 1)
                pool.sem_inc(send_passed, 1)
                pool.indirect_dma_start(ys_dram, bass.IndirectOffsetOnAxis(y_at[par][:, 0:1], 0),
                                        y_out[par][:, :], None).then_inc(yo_sent[par], 16)

            pool.wait_ge(lists_ready, 1)
            for k in range(4):
                gather(k, k, 0)

            def four_tiles(i, last=False):
                for k in range(4):
                    send(4 * i + k, k % 2, 2 * i + k // 2)
                    if not last:
                        gather(4 * (i + 1) + k, k, i + 1)

            four_tiles(0)
            with pool.Fori(1, SLOT_TILES // 4 - 1) as i:
                four_tiles(i)
            four_tiles(SLOT_TILES // 4 - 1, True)

            def scale_four(g, half):
                _, seed, half_v, t2, t3 = (m[:, :] for m in zn[half])
                rstd_4, shift_4 = z_rstd[half][:, :], z_shift[half][:, :]
                pool.wait_ge(comb_mv, 4 * (g + 1))
                link = Chain(pool, comb_newton, 6 * g)
                pool.sem_inc(send_passed, 1)
                link(pool.tensor_scalar(half_v, z_mv[half][:, :, 1], -0.5, -0.5 * EPS / 4, ALU.mult, ALU.add))
                pool.wait_ge(comb_seed, g + 1)
                link(pool.tensor_tensor(t2, half_v, seed, ALU.mult))
                link(pool.tensor_tensor(t3, t2, seed, ALU.mult))
                pool.sem_inc(send_passed, 1)
                link(pool.tensor_scalar(t3, t3, 1.5, None, ALU.add))
                at_least(pool, comb_ready, 4 * (g - 1))
                link(pool.tensor_tensor(rstd_4, t3, seed, ALU.mult))
                link(pool.tensor_tensor(t2, z_mv[half][:, :, 0], rstd_4, ALU.mult))
                pool.sem_inc(send_passed, 1)
                pool.tensor_scalar(shift_4, t2, -1.0, None, ALU.mult).then_inc(comb_scale, 1)

            scale_four(0, 0)
            scale_four(1, 1)
            with pool.Fori(1, GROUPS // 2) as i:
                scale_four(2 * i, 0)
                scale_four(2 * i + 1, 1)

        @block.scalar
        def _(act):
            act.preload_act_table_set("natural_log_exp_and_others")

            def take_x(b):
                for c in range(EC):
                    n, k, _ = prep("x", b, 0, c)
                    act.wait_ge(prep_full, n + 1)
                    act.copy(xT[:, c, :], prep_bank[k][:, :]).then_inc(prep_taken[k], 1)

            def project(b, half):
                u = 2 * b.at + half
                at_least(act, normed_ready, u)
                for i in range(TT // 2):
                    n, k, _ = prep("project", b, half, i)
                    act.wait_ge(prep_full, n + 1)
                    act.copy(raw[:, 2 * i:2 * i + 2, :], prep_bank[k][:, :].rearrange("p (t n) -> p t n", t=2)).then_inc(
                        prep_taken[k], 1)

            def project_v(b, half):
                n, k, _ = prep("v", b, half, 0)
                act.wait_ge(prep_full, n + 1)
                act.copy(v_aug[half][:, :, :, 0:D],
                         prep_bank[k][:, :].rearrange("p (t h d) -> p t h d", t=TT, d=D)).then_inc(prep_taken[k], 1)

            def sums(b, half):
                u = 2 * b.at + half
                act.wait_ge(ssum_ready, u + 1)
                act.activation(nt[0][:, :, :], ssum[:, :, :], ACT.Ln, bias=eps_col[:, :],
                               scale=1.0 / D).then_inc(ln_ready, 1)
                act.wait_ge(ln_ready, u + 1)
                act.activation(nt[1][:, :, :], nt[0][:, :, :], ACT.Exp, scale=-0.5).then_inc(seed_ready, 1)

            def split(b, half):
                act.wait_ge(high_ready, 2 * b.at + half + 1)
                act.copy(stack[half][:, :, 0, :, 48:64], stack[half][:, :, 0, :, 0:D].bitcast(F32)).then_inc(
                    again_ready, 1)
                act.copy(stack[half][:, :, 1, :, 16:32], stack[half][:, :, 1, :, 0:D].bitcast(F32)).then_inc(
                    again_ready, 1)

            def turn(b, half, p):
                for kind, to in (("k", kT), ("q", qT)):
                    n, k, _ = prep(kind, b, half, p)
                    act.wait_ge(prep_full, n + 1)
                    act.copy(to[half][:, p, :], prep_bank[k][:, :]).then_inc(prep_taken[k], 1)

            def with_maxima(b, half, p):
                act.wait_ge(out_full, outs("q", b, half, p)[0] + 1)
                act.copy(qT[half][:, p, :], out_bank[:, :]).then_inc(out_taken, 1)

            def weigh(b, half, p, pieces):
                u = 2 * b.at + half
                if 0 in pieces:
                    at_least(act, pv_done, 2 * u + (-1, 0, 0, 1)[p])
                for i in pieces:
                    act.wait_ge(st_full, PIECES * (PAIRS * u + p) + i + 1)
                    act.activation(probsT[p][:, i, 0:WIDTH[i]], st_bank[i % STB][:, 0:WIDTH[i]],
                                   ACT.Exp).then_inc(st_taken[i % STB], 1)

            def scores(b, half, p):
                weigh(b, half, p, range(PIECES))

            def values(b, half, p, ahead, beside):
                if ahead:
                    with_maxima(*ahead)
                    weigh(*ahead, EARLY)

            def more_values(b, half, p, ahead, beside):
                if ahead:
                    weigh(*ahead, LATE)
                if p % 2 == 1:
                    act.wait_ge(pv_done, 2 * (2 * b.at + half) + p // 2 + 1)
                    act.copy(sumsT[:, :], pv_bank[:, :]).then_inc(sumsT_ready, 1)

            def join(b, half):
                act.wait_ge(out_full, outs("join", b, half, 0)[0] + 1)
                act.copy(headsT[:, half, :], out_bank[:, :]).then_inc(out_taken, 1)

            def norm_x1(b):
                act.wait_ge(y_mv_ready, TT * (b.at + 1))
                act.activation(yn[0][:, :], y_mv[:, :, 1], ACT.Ln, bias=eps_col[:, :]).then_inc(y_ln_ready, 1)
                act.wait_ge(y_ln_ready, b.at + 1)
                act.activation(yn[1][:, :], yn[0][:, :], ACT.Exp, scale=-0.5).then_inc(y_seed_ready, 1)

            def turn_x1(b, c):
                act.wait_ge(out_full, outs("x1", b, 1, c)[0] + 1)
                act.copy(x1T[:, c, :], out_bank[:, :]).then_inc(out_taken, 1)

            act.wait_ge(consts_ready, 18)
            attention(act, Steps(take_x=take_x, project=project, project_v=project_v, sums=sums, split=split, turn=turn,
                                 with_maxima=with_maxima, scores=scores, values=values,
                                 more_values=more_values, join=join, norm_x1=norm_x1, turn_x1=turn_x1))

            def take_high(e):
                act.wait_ge(w_raw_loaded[e % 2], 32 * (e // 2 + 1))
                act.copy(w_high[:, :, e, :], w_raw[e % 2][:, :, :]).then_inc(w_high_ready, 1)

            for i in range(ITERS):
                act.wait_ge(route_v, routed(i, 1))
                act.activation(exps[:, :, :], logits[:, :, :, :].rearrange("p t b e -> p (t b) e"),
                               ACT.Exp).then_inc(route_a, 1)
                act.wait_ge(route_v, routed(i, 2))
                act.activation(row_b[:, :], row_a[:, :], ACT.Ln).then_inc(route_a, 1)
                act.wait_ge(route_v, routed(i, 4))
                act.activation(col_exps[:, :], other_bank[0][0:NB * E, :], ACT.Exp, bias=col_nmax[:, :],
                               accum_out=col_sum[:, :]).then_inc(route_a, 1)
                act.wait_ge(route_a, 4 * i + 3)
                act.activation(col_ln[:, :], col_sum[:, :], ACT.Ln).then_inc(route_a, 1)
                take_high(i)
            act.wait_ge(route_v, routed(ITERS, 0))
            act.activation(gates[:, :, :], logits[:, :, :, :].rearrange("p t b e -> p (t b) e"),
                           ACT.Exp).then_inc(route_a, 1)

            def near_rows():
                for i in range(K * NT // HOTS // 2):
                    some = slice((2 * i + 1) * HOTS, (2 * i + 2) * HOTS)
                    act.wait_ge(row_apart, i + 1)
                    act.activation(row_hot[:, some, :], row_hot[:, some, :], ACT.Square).then_inc(row_apart2, 1)
                    act.wait_ge(row_apart2, i + 1)
                    act.activation(row_hot[:, some, :], row_hot[:, some, :], ACT.Relu, bias=ones[:, 0:1],
                                   scale=-1.0).then_inc(row_hot_a, 1)

            for e in range(ITERS, E):
                take_high(e)
            near_rows()

            def turned(t, par):
                act.wait_ge(xg_turned, t + 1)
                act.copy(xgT[par][:, :, :], x_bank[:, 0:EMB].rearrange("p (c n) -> p c n", c=EC)).then_inc(
                    xgT_ready, 1)
                act.wait_ge(xgT_ready, t + 1)
                act.copy(xgT_b[par][:, :, :], xgT[par][:, :, :].bitcast(F32)).then_inc(xgT_b_ready, 1)

            def gate(t, par):
                act.wait_ge(g_full, t + 1)
                act.activation(gate_act[par][:, :], g_bank[:, :], ACT.Relu).then_inc(relu_ready, 1)

            def hidden(t, par):
                act.wait_ge(hid_turned, t + 1)
                act.copy(hidT[par][:, :, :], h_bank[:, :].rearrange("p (c n) -> p c n", c=FC)).then_inc(
                    hidT_ready, 1)

            turned(0, 0)
            gate(0, 0)
            turned(1, 1)
            with act.Fori(0, SLOT_TILES // 2 - 1) as i:
                for par in range(2):
                    t = 2 * i + par
                    hidden(t, par)
                    gate(t + 1, 1 - par)
                    turned(t + 2, par)
            hidden(SLOT_TILES - 2, 0)
            gate(SLOT_TILES - 1, 1)
            hidden(SLOT_TILES - 1, 1)

            def seed(g, half):
                act.wait_ge(comb_mv, 4 * (g + 1))
                act.activation(zn[half][0][:, :], z_mv[half][:, :, 1], ACT.Ln, bias=eps4_col[:, :]).then_inc(comb_ln, 1)
                act.wait_ge(comb_ln, g + 1)
                act.activation(zn[half][1][:, :], zn[half][0][:, :], ACT.Exp, scale=-0.5).then_inc(comb_seed, 1)

            def scaled(g, half, i):
                act.wait_ge(comb_scale, g + 1)
                for j in range(4):
                    at_least(act, stored[half * 4 + j], 16 * i)
                    act.activation(scaled_z[half * 4 + j][:, :], acc[half * 4 + j][:, :], ACT.Identity,
                                   bias=z_shift[half][:, j:j + 1], scale=z_rstd[half][:, j:j + 1]).then_inc(comb_ready, 1)

            for half in range(2):
                seed(half, half)
                scaled(half, half, 0)
            with act.Fori(1, GROUPS // 2) as i:
                for half in range(2):
                    seed(2 * i + half, half)
                    scaled(2 * i + half, half, i)

        @block.vector
        def _(dve):
            def rsqrt_newton(seed, half_v, t2, t3, to, var, scale, chain, count, ready, at, eps=EPS):
                dve.tensor_scalar(half_v, var, -0.5 * scale, -0.5 * eps, ALU.mult, ALU.add).then_inc(chain, 1)
                dve.wait_ge(ready, at)
                dve.wait_ge(chain, count + 1)
                dve.tensor_tensor(t2, half_v, seed, ALU.mult).then_inc(chain, 1)
                dve.wait_ge(chain, count + 2)
                dve.tensor_tensor(t3, t2, seed, ALU.mult).then_inc(chain, 1)
                dve.wait_ge(chain, count + 3)
                dve.scalar_tensor_tensor(out=to, in0=t3, scalar=1.5, in1=seed, op0=ALU.add,
                                         op1=ALU.mult).then_inc(chain, 1)
                dve.wait_ge(chain, count + 4)

            dve.wait_ge(inputs_loaded, 16 * 12)
            dve.tensor_scalar(gains[:, :, :], gains[:, :, :], QK_SCALE, None, ALU.mult).then_inc(w_ready, 1)
            dve.tensor_scalar(shifts[:, :, :], shifts[:, :, :], QK_SCALE, None, ALU.mult).then_inc(w_ready, 1)
            dve.tensor_scalar(inv_temp[:, :], temp_col[:, :], 0.1, None, ALU.max).then_inc(w_ready, 1)
            dve.wait_ge(w_ready, 3)
            dve.reciprocal(inv_temp[:, :], inv_temp[:, :]).then_inc(w_ready, 1)
            for i in range(4):
                dve.wait_ge(w_turned, i + 1)
                for c in range(EC):
                    src = other_bank[i][:, c * EMB:(c + 1) * EMB]
                    if i < 3:
                        dve.tensor_copy(w_qkvT[:, c, :, i, :], src.rearrange("p (h n) -> p h n", h=2)).then_inc(
                            w_copied, 1)
                    else:
                        dve.tensor_copy(w_oT[:, c, :], src).then_inc(w_copied, 1)
            dve.wait_ge(w_turned, 5)
            dve.tensor_copy(rwT[:, :, :], out_bank[:, 0:EC * E].rearrange("p (c e) -> p c e", c=EC)).then_inc(
                w_copied, 1)
            dve.wait_ge(w_copied, 9)
            for i in range(2):
                for c in range(EC):
                    dve.tensor_reduce(w_mean[:, i, c, :], w_qkvT[:, c, :, i, :].rearrange(
                        "p h (g d) -> p h g d", d=D), AX, ALU.add).then_inc(w_mean_done, 1)
            dve.wait_ge(w_mean_done, 4)
            for i in range(2):
                for c in range(EC):
                    for h in range(2):
                        v = w_qkvT[:, c, h, i, :].rearrange("p (g d) -> p g d", d=D)
                        m = w_mean[:, i, c, h * HH:(h + 1) * HH].unsqueeze(2).broadcast_to([P, HH, D])
                        dve.scalar_tensor_tensor(out=v, in0=m, scalar=-1.0 / D, in1=v, op0=ALU.mult,
                                                 op1=ALU.add).then_inc(w_ready, 1)

            def sums(b, half):
                u = 2 * b.at + half
                dve.wait_ge(squares_ready, u + 1)
                dve.tensor_reduce(ssum[:, :, :], squares[:, :, :].rearrange("p t (h d) -> p t h d", d=D), AX,
                                  ALU.add).then_inc(ssum_ready, 1)

            def norm(b, half):
                u = 2 * b.at + half
                dve.wait_ge(ssum_ready, u + 1)
                rsqrt_newton(nt[1][:, :, :], nt[2][:, :, :], nt[3][:, :, :], nt[4][:, :, :], rstd[:, :, :],
                             ssum[:, :, :], 1.0 / D, newton, 4 * u, seed_ready, u + 1)
                dve.tensor_tensor(normed[:, :, :].rearrange("p t (h d) -> p t h d", d=D),
                                  raw[:, :, :].rearrange("p t (h d) -> p t h d", d=D),
                                  rstd[:, :, :].unsqueeze(3).broadcast_to([P, TT, 2 * HH, D]),
                                  ALU.mult).then_inc(normed_ready, 1)
                dve.wait_ge(normed_ready, u + 1)
                scale_shift(dve, 1, gained_k, shifted_k, u)

            def split(b, half):
                u = 2 * b.at + half
                st = stack[half]
                n5 = normed[:, :, :].rearrange("p t (h d) -> p (t h) d", d=D)
                s5 = st[:, :, :, :, :].rearrange("p t s h w -> p (t s h) w")
                dve.wait_ge(shifted_k, u + 1)
                dve.wait_ge(shifted_q, u + 1)
                dve.tensor_copy(s5[:, :, 0:D], n5).then_inc(high_ready, 1)
                dve.wait_ge(high_ready, u + 1)
                for s, at in ((0, 16), (1, 48)):
                    nrm = normed[:, :, s * P:(s + 1) * P].rearrange("p t (h d) -> p t h d", d=D)
                    dve.tensor_tensor(st[:, :, s, :, at:at + D], nrm, st[:, :, s, :, 0:D].bitcast(F32),
                                      ALU.subtract).then_inc(low_ready, 1)

            def maxima(b, half, p, some=range(MAXB)):
                u = 2 * b.at + half
                h0 = 2 * p
                for i in some:
                    n, k, _ = prep("max", b, half, MAXB * p + i)
                    dve.wait_ge(prep_full, n + 1)
                    s = prep_bank[k]
                    for h, t, c in MAX_REGIONS[i]:
                        last = dve.tensor_reduce(neg_max[:, t, h0 + h:h0 + h + 1], s[:, c:c + (t + 1) * P], AX,
                                                 ALU.max, negate=True)
                    last.then_inc(prep_taken[k], 1)
                if MAXB - 1 not in some:
                    return
                prep_done(dve, prep("max", b, half, MAXB * p + MAXB - 1))
                m = neg_max[:, :, h0:h0 + 2]
                high = stack[half][:, :, 0, h0:h0 + 2, 32]
                dve.tensor_copy(high, m).then_inc(max_high, 1)
                dve.wait_ge(max_high, PAIRS * u + p + 1)
                dve.tensor_tensor(stack[half][:, :, 0, h0:h0 + 2, 33], m, high.bitcast(F32),
                                  ALU.subtract).then_inc(max_ready, 1)

            def values(b, half, p, ahead, beside):
                if beside:
                    maxima(*beside, EARLY)

            def more_values(b, half, p, ahead, beside):
                if beside:
                    maxima(*beside, LATE)

            def heads_of(b, half, g):
                dve.wait_ge(out_full, outs("heads", b, half, g)[0] + 1)
                o = out_bank[:, :].rearrange("p (t h d) -> p t h d", t=TT, h=4)
                dve.reciprocal(recip[:, :, :], o[:, :, :, D]).then_inc(recip_ready, 1)
                dve.wait_ge(recip_ready, 2 * (2 * b.at + half) + g + 1)
                dve.tensor_tensor(heads[:, :, g * 4 * D:(g + 1) * 4 * D].rearrange("p t (h d) -> p t h d", h=4),
                                  o[:, :, :, 0:D], recip[:, :, :].unsqueeze(3).broadcast_to([P, TT, 4, D]),
                                  ALU.mult).then_inc(out_taken, 1)

            def project_out(b, i):
                if i == 0:
                    dve.wait_ge(res_ready, b.at + 1)
                dve.wait_ge(out_full, outs("y", b, 1, i)[0] + 1)
                dve.tensor_tensor(y[:, 2 * i:2 * i + 2, :], out_bank[:, :].rearrange("p (t e) -> p t e", t=2),
                                  x_res[:, 2 * i:2 * i + 2, :], ALU.add).then_inc(out_taken, 1)
                out_done(dve, outs("y", b, 1, i))
                for t in (2 * i, 2 * i + 1):
                    dve.bn_stats(y_stats[:, t, :], y[:, t, :]).then_inc(y_stats_ready, 1)
                if i == 0:
                    return
                dve.wait_ge(y_stats_ready, TT * (b.at + 1))
                dve.sem_inc(wait_passed, 1)
                for t in range(TT):
                    dve.bn_aggr(y_mv[:, t, :], y_stats[:, t, :]).then_inc(y_mv_ready, 1)

            def norm_x1(b):
                dve.wait_ge(y_mv_ready, TT * (b.at + 1))
                rsqrt_newton(yn[1][:, :], yn[2][:, :], yn[3][:, :], yn[4][:, :], y_rstd[:, :], y_mv[:, :, 1], 1.0,
                             y_newton, 4 * b.at, y_seed_ready, b.at + 1)
                at_least(dve, x1_saved, 16 * b.at)
                for t in range(TT):
                    dve.tensor_scalar(x1[:, t, :], y[:, t, :], y_mv[:, t, 0:1], y_rstd[:, t:t + 1], ALU.subtract,
                                      ALU.mult).then_inc(x1_ready, 1)

            def route_logits(b):
                dve.wait_ge(out_full, outs("logits", b, 1, 0)[0] + 1)
                dve.tensor_tensor(logits[:, :, bass.ds(b.at, 1), :].rearrange("p t o e -> p (t o) e"),
                                  out_bank[:, 0:TT * E].rearrange("p (t e) -> p t e", e=E),
                                  rb_row[:, :].unsqueeze(1).broadcast_to([P, TT, E]), ALU.add).then_inc(
                    out_taken, 1)

            attention(dve, Steps(sums=sums, norm=norm, split=split, maxima=maxima, values=values,
                                 more_values=more_values, heads=heads_of, project_out=project_out, norm_x1=norm_x1,
                                 route_logits=route_logits))

            lg = logits[:, :, :, :].rearrange("p t b e -> p (t b) e")
            dve.wait_ge(out_taken, len(out_steps))
            dve.tensor_scalar(lg, lg, inv_temp[:, 0:1], None, ALU.mult).then_inc(route_v, 1)
            for i in range(ITERS):
                dve.wait_ge(route_v, routed(i, 0))
                dve.tensor_reduce(row_a[:, :], lg, AX, ALU.max).then_inc(rows_max, 1)
                dve.wait_ge(rows_max, i + 1)
                dve.tensor_tensor(lg, lg, row_a[:, :].unsqueeze(2).broadcast_to([P, NT, E]), ALU.subtract).then_inc(
                    route_v, 1)
                dve.wait_ge(route_a, 4 * i + 1)
                dve.tensor_reduce(row_a[:, :], exps[:, :, :], AX, ALU.add).then_inc(route_v, 1)
                dve.wait_ge(route_a, 4 * i + 2)
                dve.tensor_tensor(lg, lg, row_b[:, :].unsqueeze(2).broadcast_to([P, NT, E]), ALU.subtract).then_inc(
                    route_v, 1)
                dve.wait_ge(route_p, 2 * i + 1)
                dve.tensor_reduce(col_nmax[:, :], other_bank[0][0:NB * E, :], AX, ALU.max, negate=True).then_inc(
                    route_v, 1)
                dve.wait_ge(route_a, 4 * i + 4)
                dve.tensor_tensor(col_lse[:, :], col_ln[:, :], col_nmax[:, :], ALU.subtract).then_inc(route_v, 1)
                dve.wait_ge(route_v, routed(i, 5))
                dve.tensor_scalar(col_diag[:, :], ident[0:NB * E, 0:NB * E], col_lse[:, 0:1], None,
                                  ALU.mult).then_inc(route_v, 1)
                dve.wait_ge(route_p, 2 * i + 2)
                cols = other_bank[1][:, 0:NB * E].rearrange("p (b e) -> p b e", b=NB).unsqueeze(1).broadcast_to(
                    [P, TT, NB, E])
                dve.tensor_tensor(logits[:, :, :, :], logits[:, :, :, :], cols, ALU.subtract).then_inc(route_v, 1)
            done = routed(ITERS, 0)
            dve.wait_ge(route_a, 4 * ITERS + 1)
            link = Chain(dve, route_v, done)
            link(dve.tensor_reduce(row_a[:, :], gates[:, :, :], AX, ALU.add))
            link(dve.tensor_scalar(row_a[:, :], row_a[:, :], 1e-8, None, ALU.add))
            link(dve.reciprocal(row_b[:, :], row_a[:, :]))
            link(dve.tensor_tensor(gates[:, :, :], gates[:, :, :], row_b[:, :].unsqueeze(2).broadcast_to([P, NT, E]),
                                   ALU.mult))
            for t in range(NT):
                last = dve.max(best[:, t, :], gates[:, t, :])
            link(last)
            for t in range(NT):
                last = dve.max_index(best_at[:, t, :], best[:, t, :], gates[:, t, :])
            link(last)
            link(dve.tensor_copy(best_atf[:, :, :], best_at[:, :, 0:K]))
            dve.wait_ge(iotas_ready, 8)
            for k in range(K):
                link(dve.tensor_tensor(chosen[k][:, :, :], best_atf[:, :, k:k + 1].broadcast_to([P, NT, E]),
                                       expert_iota[:, :].unsqueeze(1).broadcast_to([P, NT, E]), ALU.is_equal))
            dve.tensor_tensor(chosen_b[:, :, :], chosen[0][:, :, :], chosen[1][:, :, :], ALU.add).then_inc(choice_ready, 1)
            dve.wait_ge(route_p, 2 * ITERS + 1)
            link(dve.tensor_copy(counts[:, :, :], other_bank[3][:, 0:NT * E].rearrange("p (t e) -> p t e", e=E)))
            src, step, n = counts, 1, 0
            while step < NT:
                dst = scan[n % 2]
                link(dve.tensor_copy(dst[:, 0:step, :], src[:, 0:step, :]))
                link(dve.tensor_tensor(dst[:, step:, :], src[:, step:, :], src[:, 0:NT - step, :], ALU.add))
                src, step, n = dst, 2 * step, n + 1
            upto, other = src, scan[n % 2]
            link(dve.tensor_scalar(n_tiles_i[:, :], upto[:, NT - 1, :], float(P - 1), None, ALU.add))
            link(dve.tensor_scalar(n_tiles_j[:, :], n_tiles_i[:, :], 7, None, ALU.arith_shift_right))
            link(dve.tensor_copy(n_tiles[:, :], n_tiles_j[:, :]))
            src_e, step, n = n_tiles, 1, 0
            while step < E:
                dst = escan[n % 2]
                link(dve.tensor_copy(dst[:, 0:step], src_e[:, 0:step]))
                link(dve.tensor_tensor(dst[:, step:], src_e[:, step:], src_e[:, 0:E - step], ALU.add))
                src_e, step, n = dst, 2 * step, n + 1
            link(dve.tensor_tensor(first_slot[:, :], src_e[:, :], n_tiles[:, :], ALU.subtract))
            link(dve.tensor_scalar(first_slot[:, :], first_slot[:, :], float(P), None, ALU.mult))
            link(dve.tensor_tensor(past[:, :, :], src_e[0:1, :].unsqueeze(1).broadcast_to([1, SLOT_TILES, E]),
                                   tile_iota[0:1, :].unsqueeze(2).broadcast_to([1, SLOT_TILES, E]), ALU.is_le))
            link(dve.tensor_reduce(tile_ef[:, :], past[:, :, :], AX, ALU.add))
            dve.tensor_scalar(tile_e[:, :], tile_ef[:, :], float(E - 1), None, ALU.min).then_inc(tiles_ready, 1)
            link(dve.tensor_tensor(other[:, :, :], upto[:, :, :], counts[:, :, :], ALU.subtract))
            link(dve.tensor_tensor(other[:, :, :], other[:, :, :],
                                   other_bank[2][:, 0:NT * E].rearrange("p (t e) -> p t e", e=E), ALU.add))
            link(dve.tensor_tensor(slot_all[:, :, :], other[:, :, :],
                                   first_slot[:, :].unsqueeze(1).broadcast_to([P, NT, E]), ALU.add))
            for k in range(K):
                link(dve.tensor_tensor(slot_of[k][:, :, :], slot_all[:, :, :], chosen[k][:, :, :], ALU.mult))
                link(dve.tensor_reduce(slot_f[:, k, :], slot_of[k][:, :, :], AX, ALU.add))
            link(dve.tensor_copy(slot_i[:, :, :], slot_f[:, :, :]))
            link(dve.tensor_scalar(slot_tile_i[:, :, :], slot_i[:, :, :], 7, None, ALU.arith_shift_right))
            link(dve.tensor_copy(slot_tile[:, :, :], slot_tile_i[:, :, :]))
            dve.scalar_tensor_tensor(out=slot_row[:, :, :], in0=slot_tile[:, :, :], scalar=-float(P),
                                     in1=slot_f[:, :, :], op0=ALU.mult, op1=ALU.add).then_inc(slots_ready, 1)
            dve.wait_ge(slots_ready, 1)
            for i in range(K * NT // HOTS):
                some = slice(i * HOTS, (i + 1) * HOTS)

                def spread(m):
                    return m.rearrange("p k t -> p (k t)")[:, some].unsqueeze(2).broadcast_to([P, HOTS, SLOT_TILES])

                hot = tile_hot[i % 2][:, :, :]
                dve.tensor_tensor(hot, spread(slot_tile[:, :, :]),
                                  tile_iota[:, :].unsqueeze(1).broadcast_to([P, HOTS, SLOT_TILES]),
                                  ALU.is_equal).then_inc(tile_equal, 1)
                if i % 2 == 0:
                    row_hots(dve, i, ALU.is_equal).then_inc(row_hot_v, 1)
                dve.wait_ge(tile_equal, i + 1)
                for part in range(2):
                    dve.tensor_tensor(tile_code[:, some, part, :], hot, spread(code_parts[:, part, :, :]),
                                      ALU.mult).then_inc(tile_coded, 1)
            dve.wait_ge(slots_coded, 1)
            link(dve.tensor_reduce(code_sum[:, :], other_bank[1][:, 0:2 * SLOT_TILES].rearrange(
                "p (s t) -> p t s", s=2), AX, ALU.add))
            dve.tensor_scalar(unfilled[:, :], code_sum[:, :], 0.0, None, ALU.is_le)
            link(dve.tensor_scalar(code_row[:, :], code_sum[:, :], -1.0, 0.0, ALU.add, ALU.max))
            dve.tensor_copy(code_row_i[:, :], code_row[:, :])
            link(dve.tensor_tensor(unfilled[:, :], unfilled[:, :], unfilled_row[:, :], ALU.mult))
            link(dve.tensor_scalar(token_of[:, :].bitcast(I32), code_row_i[:, :], 1, None, ALU.arith_shift_right))
            dve.tensor_tensor(send_to[:, :], unfilled[:, :], code_row[:, :], ALU.add).then_inc(lists_ready, 1)
            link(dve.tensor_tensor(top_sum[:, :], best[:, :, 0], best[:, :, 1], ALU.add))
            link(dve.tensor_scalar(top_sum[:, :], top_sum[:, :], 1e-8, None, ALU.add))
            link(dve.reciprocal(top_sum[:, :], top_sum[:, :]))
            link(dve.tensor_scalar(top_sum[:, :], top_sum[:, :], 0.5, None, ALU.mult))
            link(dve.tensor_tensor(top_gate[:, :, :].rearrange("p (b t) k -> p t b k", b=NB),
                                   best[:, :, 0:K].rearrange("p (t b) k -> p t b k", b=NB),
                                   top_sum[:, :].rearrange("p (t b) -> p t b", b=NB).unsqueeze(3).broadcast_to(
                                       [P, TT, NB, K]), ALU.mult))

            def hidden(t, par):
                dve.wait_ge(relu_ready, t + 1)
                dve.wait_ge(p_full, t + 1)
                dve.tensor_tensor(hid[par][:, :], gate_act[par][:, :], p_bank[:, :], ALU.mult).then_inc(hid_ready, 1)

            def result(i, k):
                t, par = 4 * i + k, k % 2
                dve.wait_ge(yo_full, t + 1)
                at_least(dve, yo_sent[par], 16 * (2 * i + k // 2))
                dve.tensor_copy(y_out[par][:, :], y_bank[:, 0:EMB]).then_inc(yo_ready, 1)

            def low_tokens(t, par):
                dve.wait_ge(xgT_ready, t + 1)
                dve.tensor_tensor(xgT_low[par][:, :, :], x_bank[:, 0:EMB].rearrange("p (c n) -> p c n", c=EC),
                                  xgT[par][:, :, :].bitcast(F32), ALU.subtract).then_inc(xgT_low_ready, 1)

            def four_tiles(i, last=False):
                for k in range(4):
                    if not (last and k == 3):
                        hidden(4 * i + k + 1, (k + 1) % 2)
                    if not (last and k >= 2):
                        low_tokens(4 * i + k + 2, k % 2)
                    result(i, k)

            low_tokens(0, 0)
            hidden(0, 0)
            low_tokens(1, 1)
            four_tiles(0)
            with dve.Fori(1, SLOT_TILES // 4 - 1) as i:
                four_tiles(i)
            four_tiles(SLOT_TILES // 4 - 1, True)

            def add_four(i, half):
                g = 2 * i + half
                for j in range(4):
                    n = half * 4 + j
                    dve.wait_ge(yt_loaded[n], 16 * (i + 1))
                    at_least(dve, comb_ready, 4 * (g - 2) + j + 1)
                    dve.scalar_tensor_tensor(out=acc[n][:, :], in0=y_two[n][:, 0, :],
                                             scalar=top_gate[:, bass.ds(4 * g + j, 1), 0],
                                             in1=x1_all[:, bass.ds(4 * g + j, 1), :].rearrange("p o e -> p (o e)"),
                                             op0=ALU.mult, op1=ALU.add).then_inc(comb_a, 1)
                for j in range(4):
                    n = half * 4 + j
                    dve.wait_ge(comb_a, 4 * g + j + 1)
                    dve.scalar_tensor_tensor(out=acc[n][:, :], in0=y_two[n][:, 1, :],
                                             scalar=top_gate[:, bass.ds(4 * g + j, 1), 1], in1=acc[n][:, :],
                                             op0=ALU.mult, op1=ALU.add).then_inc(comb_b, 1)
                for j in range(4):
                    dve.wait_ge(comb_b, 4 * g + j + 1)
                    dve.bn_stats(z_stats[:, j, :], acc[half * 4 + j][:, :]).then_inc(comb_stats, 1)
                dve.wait_ge(comb_stats, 4 * (g + 1))
                dve.sem_inc(wait_passed, 1)
                for j in range(4):
                    dve.bn_aggr(z_mv[half][:, j, :], z_stats[:, j, :]).then_inc(comb_mv, 1)

            dve.wait_ge(x1_loaded, 16 * NB)
            add_four(0, 0)
            add_four(0, 1)
            with dve.Fori(1, GROUPS // 2) as i:
                add_four(i, 0)
                add_four(i, 1)

        @block.tensor
        def _(pe):
            pe.wait_ge(consts_ready, 18)
            pe.wait_ge(inputs_loaded, 16 * 12)
            for i in range(4):
                for c in range(EC):
                    for r in range(2):
                        last = pe.transpose(other_bank[i][:, c * EMB + r * P:c * EMB + (r + 1) * P],
                                            w_rows[:, i, r, c * P:(c + 1) * P], ident[:, :])
                last.then_inc(w_turned, 1)
            for c in range(EC):
                last = pe.transpose(out_bank[:, c * E:(c + 1) * E], rw_rows[:, c * P:(c + 1) * P], ident[0:E, 0:E])
            last.then_inc(w_turned, 1)
            pe.wait_ge(w_ready, 12)

            def free_prep(kind, b, half, i):
                _, k, uses = prep(kind, b, half, i)
                at_least(pe, prep_taken[k], uses)
                return prep_bank[k]

            def free_out(kind, b, half, i):
                at_least(pe, out_taken, outs(kind, b, half, i)[0])
                return out_bank

            def turn_stack(to, b, half, s, p):
                for t in range(TT):
                    last = pe.transpose(to[:, t * P:(t + 1) * P],
                                        stack[half][:, t, s, 2 * p:2 * p + 2, :].rearrange(
                                            "p h w -> p (h w)").bitcast(F32), ident[:, :])
                return last

            def take_x(b):
                pe.wait_ge(x_loaded, 16 * (b.at + 1))
                for c in range(EC):
                    to = free_prep("x", b, 0, c)
                    for t in range(TT):
                        last = pe.transpose(to[:, t * P:(t + 1) * P], x_in[:, t, c * P:(c + 1) * P], ident[:, :])
                    last.then_inc(prep_full, 1)

            def project(b, half):
                if half == 0:
                    for c in range(EC):
                        prep_done(pe, prep("x", b, 0, c))
                for i in range(TT // 2):
                    to = free_prep("project", b, half, i)
                    for t in range(2):
                        for c in range(EC):
                            last = pe.matmul(to[:, t * 2 * P:(t + 1) * 2 * P],
                                             xT[:, c, (2 * i + t) * P:(2 * i + t + 1) * P],
                                             w_qkvT[:, c, half, 0:2, :].rearrange("p s n -> p (s n)"),
                                             start=c == 0, stop=c == EC - 1)
                    last.then_inc(prep_full, 1)

            def project_v(b, half):
                to = free_prep("v", b, half, 0)
                for t in range(TT):
                    for c in range(EC):
                        last = pe.matmul(to[:, t * P:(t + 1) * P], xT[:, c, t * P:(t + 1) * P],
                                         w_qkvT[:, c, half, 2, :], start=c == 0, stop=c == EC - 1)
                last.then_inc(prep_full, 1)

            def turn(b, half, p):
                u = 2 * b.at + half
                pe.wait_ge(low_ready, 2 * (u + 1))
                pe.wait_ge(again_ready, 2 * (u + 1))
                pe.wait_ge(max_cleared, u + 1)
                for s, kind in ((1, "k"), (0, "q")):
                    turn_stack(free_prep(kind, b, half, p), b, half, s, p).then_inc(prep_full, 1)

            def row_maxima(b, half, p, i):
                to = free_prep("max", b, half, MAXB * p + i)
                for n, (h, t, c) in enumerate(MAX_REGIONS[i]):
                    rows = slice(h * SW, (h + 1) * SW)
                    pe.matmul(to[:, c:c + (t + 1) * P], qT[half][rows, p, t * P:(t + 1) * P],
                              kT[half][rows, p, 0:(t + 1) * P], start=n == 0, stop=False, skip_group_check=True)
                    last = pe.matmul(to[:, c + t * P:c + (t + 1) * P], ident_b[:, :], mask[:, :], start=False,
                                     stop=n == len(MAX_REGIONS[i]) - 1, skip_group_check=True)
                last.then_inc(prep_full, 1)

            def turned(b, half, p):
                first_bank = prep("max", b, half, MAXB * p)[1]
                for step in (prep("k", b, half, p), prep("q", b, half, p)):
                    if step[1] != first_bank:
                        prep_done(pe, step)

            def maxima(b, half, p):
                turned(b, half, p)
                for i in range(MAXB):
                    row_maxima(b, half, p, i)

            def with_maxima(b, half, p):
                pe.wait_ge(max_ready, PAIRS * (2 * b.at + half) + p + 1)
                turn_stack(free_out("q", b, half, p), b, half, 0, p).then_inc(out_full, 1)

            def score(b, half, p, i):
                u = 2 * b.at + half
                if i == 0:
                    out_done(pe, outs("q", b, half, p))
                to = st_bank[i % STB]
                at_least(pe, st_taken[i % STB], 2 * (PAIRS * u + p) + i // STB)
                for n, (h, j, c) in enumerate(ST_REGIONS[i]):
                    rows = slice(h * SW, (h + 1) * SW)
                    last = pe.matmul(to[:, c:c + (TT - j) * P], kT[half][rows, p, j * P:(j + 1) * P],
                                     qT[half][rows, p, j * P:T], start=n == 0, stop=n == len(ST_REGIONS[i]) - 1,
                                     skip_group_check=True)
                last.then_inc(st_full, 1)

            def scores(b, half, p):
                for i in range(PIECES):
                    score(b, half, p, i)

            def value(b, half, p, j):
                u = 2 * b.at + half
                pe.wait_ge(masked, TT * (PAIRS * u + p) + (1, 3, 4)[PLACE[0, j][0] // 2])
                for n in range(4):
                    i, c = PLACE[n % 2, j]
                    pair = p - 1 + n // 2
                    last = pe.matmul(pv_bank[n * VW:(n + 1) * VW, j * P:T], v_aug[half][:, j, 2 * pair + n % 2, :],
                                     probsT[pair][:, i, c:c + (TT - j) * P], start=j == 0, stop=j == TT - 1,
                                     skip_group_check=True)
                return last

            def values(b, half, p, ahead, beside):
                u = 2 * b.at + half
                if beside:
                    turned(*beside)
                    row_maxima(*beside, 0)
                if ahead:
                    with_maxima(*ahead)
                if beside:
                    row_maxima(*beside, 1)
                if p % 2 == 1:
                    prep_done(pe, prep("v", b, half, 0))
                    at_least(pe, sumsT_ready, 2 * u + p // 2)
                    value(b, half, p, 0)
                if beside:
                    row_maxima(*beside, 2)
                if ahead:
                    score(*ahead, 0)
                    score(*ahead, 1)
                if p % 2 == 1:
                    value(b, half, p, 1)
                if beside:
                    row_maxima(*beside, 3)
                if ahead:
                    score(*ahead, 2)
                    score(*ahead, 3)

            def more_values(b, half, p, ahead, beside):
                if beside:
                    row_maxima(*beside, 4)
                if p % 2 == 1:
                    value(b, half, p, 2)
                if beside:
                    row_maxima(*beside, 5)
                if ahead:
                    score(*ahead, 4)
                if ahead:
                    score(*ahead, 5)
                if p % 2 == 1:
                    value(b, half, p, 3).then_inc(pv_done, 1)

            def heads_of(b, half, g):
                pe.wait_ge(sumsT_ready, 2 * (2 * b.at + half) + g + 1)
                to = free_out("heads", b, half, g)
                for t in range(TT):
                    last = pe.transpose(to[:, t * P:(t + 1) * P], sumsT[:, t * P:(t + 1) * P], ident[:, :])
                last.then_inc(out_full, 1)

            def join(b, half):
                to = free_out("join", b, half, 0)
                for t in range(TT):
                    last = pe.transpose(to[:, t * P:(t + 1) * P], heads[:, t, :], ident[:, :])
                last.then_inc(out_full, 1)

            def project_out(b, i):
                to = free_out("y", b, 1, i)
                for t in range(2):
                    for c in range(EC):
                        last = pe.matmul(to[:, t * EMB:(t + 1) * EMB],
                                         headsT[:, c, (2 * i + t) * P:(2 * i + t + 1) * P], w_oT[:, c, :],
                                         start=c == 0, stop=c == EC - 1)
                last.then_inc(out_full, 1)

            def turn_x1(b, c):
                pe.wait_ge(x1_ready, TT * (b.at + 1))
                to = free_out("x1", b, 1, c)
                for t in range(TT):
                    last = pe.transpose(to[:, t * P:(t + 1) * P], x1[:, t, c * P:(c + 1) * P], ident[:, :])
                last.then_inc(out_full, 1)

            def route_logits(b):
                to = free_out("logits", b, 1, 0)
                for t in range(TT):
                    for c in range(EC):
                        last = pe.matmul(to[:, t * E:(t + 1) * E], x1T[:, c, t * P:(t + 1) * P], rwT[:, c, :],
                                         start=c == 0, stop=c == EC - 1)
                last.then_inc(out_full, 1)

            attention(pe, Steps(take_x=take_x, project=project, project_v=project_v, turn=turn, maxima=maxima,
                                with_maxima=with_maxima,
                                scores=scores, values=values, more_values=more_values, heads=heads_of, join=join,
                                project_out=project_out,
                                turn_x1=turn_x1, route_logits=route_logits))

            for i in range(ITERS):
                pe.wait_ge(route_v, routed(i, 3))
                for t in range(TT):
                    last = pe.transpose(other_bank[0][0:NB * E, t * P:(t + 1) * P],
                                        logits[:, t, :, :].rearrange("p b e -> p (b e)"), ident[:, :])
                last.then_inc(route_p, 1)
                pe.wait_ge(route_v, routed(i, 6))
                pe.matmul(other_bank[1][:, 0:NB * E], ones[0:NB * E, :], col_diag[:, :], start=True,
                          stop=True).then_inc(route_p, 1)
            pe.wait_ge(choice_ready, 1)
            pe.matmul(other_bank[2][:, 0:NT * E], before_b[:, :], chosen_b[:, :, :].rearrange("p t e -> p (t e)"),
                      start=True, stop=True)
            pe.matmul(other_bank[3][:, 0:NT * E], ones_b[:, :], chosen_b[:, :, :].rearrange("p t e -> p (t e)"),
                      start=True, stop=True).then_inc(route_p, 1)

            for n in range(K * NT):
                i = n // HOTS
                if n % HOTS == 0:
                    pe.wait_ge(tile_coded, 2 * (i + 1))
                    if i % 2 == 0:
                        pe.wait_ge(row_hot_v, i // 2 + 1)
                    else:
                        pe.wait_ge(row_hot_a, i // 2 + 1)
                last = pe.matmul(other_bank[1][:, 0:2 * SLOT_TILES], row_hot[:, n, :],
                                 tile_code[:, n, :, :].rearrange("p s t -> p (s t)"), start=n == 0,
                                 stop=n == K * NT - 1)
            last.then_inc(slots_coded, 1)

            def turn_x(i, k):
                t = 4 * i + k
                pe.wait_ge(xg_loaded[k % 4], 16 * (i + k // 4 + 1))
                at_least(pe, xgT_b_ready, t)
                at_least(pe, xgT_low_ready, t)
                for c in range(EC):
                    last = pe.transpose(x_bank[:, c * P:(c + 1) * P], xg[k % 4][:, c * P:(c + 1) * P], ident[:, :])
                last.then_inc(xg_turned, 1)

            def up(i, k):
                t = 4 * i + k
                e = pe.value_load(tile_e[0:1, bass.ds(t, 1)], min_val=0, max_val=E - 1)
                pe.wait_ge(xgT_b_ready, t + 1)
                pe.wait_ge(xgT_low_ready, t + 1)
                at_least(pe, hid_ready, t)
                for n, (to, full) in enumerate(((g_bank, g_full), (p_bank, p_full))):
                    for c in range(EC):
                        of_c = slice(c * FF, (c + 1) * FF)
                        high = w_high[:, n, bass.ds(e, 1), of_c].rearrange("p o n -> p (o n)")
                        low = w_low[:, n, bass.ds(e, 1), of_c].rearrange("p o n -> p (o n)")
                        pe.matmul(to[:, :], xgT[k % 2][:, c, :], high, start=c == 0, stop=False,
                                  skip_group_check=True)
                        pe.matmul(to[:, :], xgT_low[k % 2][:, c, :], high, start=False, stop=False,
                                  skip_group_check=True)
                        last = pe.matmul(to[:, :], xgT_b[k % 2][:, c, :], low, start=False, stop=c == EC - 1,
                                         skip_group_check=True)
                    last.then_inc(full, 1)

            def turn_h(i, k):
                t = 4 * i + k
                pe.wait_ge(hid_ready, t + 1)
                at_least(pe, hidT_ready, t)
                for c in range(FC):
                    last = pe.transpose(h_bank[:, c * P:(c + 1) * P], hid[k % 2][:, c * P:(c + 1) * P], ident[:, :])
                last.then_inc(hid_turned, 1)

            def down(i, k):
                t = 4 * i + k
                e = pe.value_load(tile_e[0:1, bass.ds(t, 1)], min_val=0, max_val=E - 1)
                pe.wait_ge(hidT_ready, t + 1)
                at_least(pe, yo_ready, t)
                for c in range(FC):
                    last = pe.matmul(y_bank[:, 0:EMB], hidT[k % 2][:, c, :],
                                     wo_sb[:, bass.ds(e, 1), c * EMB:(c + 1) * EMB].rearrange("p o n -> p (o n)"),
                                     start=c == 0, stop=c == FC - 1)
                last.then_inc(yo_full, 1)

            def four_tiles(i, last=False):
                for k in range(4):
                    turn_h(i, k)
                    if not (last and k == 3):
                        up(i, k + 1)
                    if not (last and k >= 2):
                        turn_x(i, k + 2)
                    down(i, k)

            pe.wait_ge(tiles_ready, 1)
            pe.wait_ge(lists_ready, 1)
            pe.wait_ge(experts_loaded, 16 * E)
            pe.wait_ge(w_low_ready, E)
            turn_x(0, 0)
            up(0, 0)
            turn_x(0, 1)
            four_tiles(0)
            with pe.Fori(1, SLOT_TILES // 4 - 1) as i:
                four_tiles(i)
            four_tiles(SLOT_TILES // 4 - 1, True)


_INS = ["L0_attn_x", "L0_attn_Wk", "L0_attn_Wq", "L0_attn_Wv", "L0_attn_Wo", "L0_attn_bo", "L0_attn_kln_g",
        "L0_attn_kln_b", "L0_attn_qln_g", "L0_attn_qln_b", "L0_ffn_router_w", "L0_ffn_router_b",
        "L0_ffn_temperature", "L0_ffn_wg", "L0_ffn_wp", "L0_ffn_wo"]


def kernel(**inputs):
    import numpy as np
    import concourse.bacc as bacc
    from concourse.bass_utils import run_bass_kernel_spmd

    nc = bacc.Bacc("TRN2", target_bir_lowering=False, num_devices=1)
    arrays, args = {}, []
    for name in _INS:
        v = np.ascontiguousarray(inputs[name])
        arrays[f"in_{name}"] = v
        args.append(nc.dram_tensor(f"in_{name}", v.shape, mybir.dt.from_np(v.dtype), kind="ExternalInput").ap())
    args.append(nc.dram_tensor("out_dram", (NB, T, EMB), F32, kind="ExternalOutput").ap())
    layer(nc, *args)
    r = run_bass_kernel_spmd(nc, [arrays], core_ids=[0])
    return r.results[0]["out_dram"]
```
